# Optimizing a Trainium2 kernel written in Bass

```python
import numpy as np
import jax
import jax.numpy as jnp

def _softmax(x, axis=-1):
    return jax.nn.softmax(x, axis=axis)

def _gelu(x):
    return jax.nn.gelu(x, approximate=True)

def _silu(x):
    return jax.nn.silu(x)

def _sigmoid(x):
    return jax.nn.sigmoid(x)

def _layernorm(x, axis=-1, eps=1e-05):
    m = jnp.mean(x, axis=axis, keepdims=True)
    v = jnp.var(x, axis=axis, keepdims=True)
    return (x - m) / jnp.sqrt(v + eps)

def _scatter_add(tgt, idx, src, axis=0):
    return tgt.at[idx].add(src)

def _segment_sum(src, seg, n):
    return jax.ops.segment_sum(src, seg, n)
kernel_name = 'mk_gnn_ffn_d4_gnn_r16_e521eb'

def setup_inputs(seed: int=0):
    np.random.seed(seed)
    _w = jnp.asarray

    def _rec_inputs():
        import jax
        import jax.numpy as jnp
        _gk = jax.random.key(seed)
        x = -0.0003713 + 1 * jax.random.normal(jax.random.fold_in(_gk, 1), (3125, 256), jnp.float32)
        src = jax.random.randint(jax.random.fold_in(_gk, 2), (50000,), 0, 3125, jnp.int32)
        dst = jax.random.randint(jax.random.fold_in(_gk, 3), (50000,), 0, 3125, jnp.int32)
        _o = jnp.argsort(dst, stable=True)
        src = src[_o]
        dst = dst[_o]
        edge_type_8 = jax.random.randint(jax.random.fold_in(_gk, 12), (50000,), 0, 8, jnp.int32)
        edge_weight = jax.random.uniform(jax.random.fold_in(_gk, 13), (50000,), jnp.float32, 0.0, 0.999999)
        return (x, src, dst, edge_type_8, edge_weight)
    x, src, dst, edge_type_8, edge_weight = _rec_inputs()

    def _L0_gnn_setup():
        import jax, jax.numpy as jnp
        import numpy as np
        N, IN_CH, HEADS, OUT_CH, E = (3125, 256, 4, 64, 50000)
        key = jax.random.key(seed)
        k1, k2, k3, k4, k5 = jax.random.split(key, 5)
        x = jax.random.normal(k1, (N, IN_CH), dtype=jnp.float32)
        edge_index = jax.random.randint(k2, (2, E), 0, N, dtype=jnp.int64)
        bw = float(np.sqrt(6.0 / (IN_CH + HEADS * OUT_CH)))
        ba = float(np.sqrt(6.0 / (HEADS + OUT_CH)))
        weight = jax.random.uniform(k3, (IN_CH, HEADS * OUT_CH), jnp.float32, -bw, bw)
        attn_l = jax.random.uniform(k4, (HEADS, OUT_CH), jnp.float32, -ba, ba)
        attn_r = jax.random.uniform(k5, (HEADS, OUT_CH), jnp.float32, -ba, ba)
        return {'x': x, 'edge_index': edge_index, 'weight': weight, 'attn_l': attn_l, 'attn_r': attn_r}
    _L0_gnn_all = _L0_gnn_setup()
    _L0_gnn_in = {k: v for k, v in _L0_gnn_all.items() if k in ('weight', 'attn_l', 'attn_r')}
    del _L0_gnn_all

    def _L0_ffn_setup():
        import jax, jax.numpy as jnp
        import numpy as np
        DIM = 256
        H = 8
        D = 64
        G = 64
        INNER = H * D
        SCALE = D ** (-0.5)
        key = jax.random.key(seed)
        ks = jax.random.split(key, 12)
        B, N = (4, 1024)
        x = jax.random.normal(ks[0], (B, N, DIM), dtype=jnp.float32)
        s = lambda fan_in: 1.0 / np.sqrt(fan_in)
        W_fx = jax.random.normal(ks[1], (DIM, INNER), dtype=jnp.float32) * s(DIM)
        b_fx = jnp.zeros((INNER,), dtype=jnp.float32)
        W_x = jax.random.normal(ks[2], (DIM, INNER), dtype=jnp.float32) * s(DIM)
        b_x = jnp.zeros((INNER,), dtype=jnp.float32)
        A = jax.random.normal(ks[3], (G, D), dtype=jnp.float32)
        Q, _ = jnp.linalg.qr(A.T)
        W_slice = Q[:, :G].astype(jnp.float32)
        b_slice = jnp.zeros((G,), dtype=jnp.float32)
        W_q = jax.random.normal(ks[4], (D, D), dtype=jnp.float32) * s(D)
        W_k = jax.random.normal(ks[5], (D, D), dtype=jnp.float32) * s(D)
        W_v = jax.random.normal(ks[6], (D, D), dtype=jnp.float32) * s(D)
        W_out = jax.random.normal(ks[7], (INNER, DIM), dtype=jnp.float32) * s(INNER)
        b_out = jnp.zeros((DIM,), dtype=jnp.float32)
        temperature = jnp.ones((1, H, 1, 1), dtype=jnp.float32) * 0.5
        return {'x': x, 'W_fx': W_fx, 'b_fx': b_fx, 'W_x': W_x, 'b_x': b_x, 'W_slice': W_slice, 'b_slice': b_slice, 'W_q': W_q, 'W_k': W_k, 'W_v': W_v, 'W_out': W_out, 'b_out': b_out, 'temperature': temperature}
    _L0_ffn_all = _L0_ffn_setup()
    _L0_ffn_in = {k: v for k, v in _L0_ffn_all.items() if k in ('W_fx', 'b_fx', 'W_x', 'b_x', 'W_slice', 'b_slice', 'W_q', 'W_k', 'W_v', 'W_out', 'b_out', 'temperature')}
    del _L0_ffn_all

    def _L1_gnn_setup():
        import jax, jax.numpy as jnp
        import numpy as np
        N_NODES = 3125

        def _add_self_loops(src, dst, n):
            loop = jnp.arange(n, dtype=src.dtype)
            return (jnp.concatenate([src, loop]), jnp.concatenate([dst, loop]))

        def gcn_conv(x, src, dst, W, b, n):
            h = x @ W
            deg = jnp.zeros((n,), h.dtype).at[dst].add(1.0)
            dinv = jax.lax.rsqrt(jnp.maximum(deg, 1e-12))
            norm = dinv[src] * dinv[dst]
            msg = h[src] * norm[:, None]
            return jax.ops.segment_sum(msg, dst, num_segments=n) + b
        key = jax.random.key(seed)
        ks = jax.random.split(key, 10)
        num_features, hidden = (256, 64)
        x = jax.random.normal(ks[0], (N_NODES, num_features), jnp.float32)
        edge_index = jax.random.randint(ks[1], (2, 100000), 0, N_NODES, jnp.int64)

        def glorot(k, fi, fo):
            s = jnp.sqrt(6.0 / (fi + fo)).astype(jnp.float32)
            return jax.random.uniform(k, (fi, fo), jnp.float32, -s, s)
        dims = [(num_features, 2 * hidden), (2 * hidden, hidden), (hidden, 2 * hidden), (2 * hidden, num_features)]
        params = {}
        for i, (fi, fo) in enumerate(dims):
            params[f'W{i + 1}'] = glorot(ks[2 + i], fi, fo)
            params[f'b{i + 1}'] = jnp.zeros((fo,), jnp.float32)
        return {'x': x, 'edge_index': edge_index, **params}
    _L1_gnn_all = _L1_gnn_setup()
    _L1_gnn_in = {k: v for k, v in _L1_gnn_all.items() if k in ('W1', 'b1', 'W2', 'b2', 'W3', 'b3', 'W4', 'b4')}
    del _L1_gnn_all

    def _L1_ffn_setup():
        import jax, jax.numpy as jnp
        import numpy as np
        B, S, H, F, E, K = (8, 256, 256, 512, 16, 2)
        EPS = 1e-05
        key = jax.random.key(seed)
        ks = jax.random.split(key, 9)
        sc = 0.02
        return {'x': jax.random.normal(ks[0], (B, S, H), dtype=jnp.float32), 'gate_w': jax.random.normal(ks[1], (H, E), dtype=jnp.float32) * sc, 'gate_b': jnp.zeros((E,), dtype=jnp.float32), 'w1': jax.random.normal(ks[2], (E, H, F), dtype=jnp.float32) * sc, 'b1': jnp.zeros((E, F), dtype=jnp.float32), 'w2': jax.random.normal(ks[3], (E, F, H), dtype=jnp.float32) * sc, 'b2': jnp.zeros((E, H), dtype=jnp.float32), 'gamma': jnp.ones((H,), dtype=jnp.float32), 'beta': jnp.zeros((H,), dtype=jnp.float32)}
    _L1_ffn_all = _L1_ffn_setup()
    _L1_ffn_in = {k: v for k, v in _L1_ffn_all.items() if k in ('gate_w', 'gate_b', 'w1', 'b1', 'w2', 'b2', 'gamma', 'beta')}
    del _L1_ffn_all

    def _L2_gnn_setup():
        import jax, jax.numpy as jnp
        import numpy as np
        N_NODES = 18870
        N_EDGES = 75000
        DIM = 256
        EPS = 1e-05

        def _layer_norm(x, g, b):
            mu = jnp.mean(x, axis=-1, keepdims=True)
            var = jnp.mean(jnp.square(x - mu), axis=-1, keepdims=True)
            return (x - mu) * jax.lax.rsqrt(var + EPS) * g + b

        def _gcn_conv(x, edge_index, edge_weight, W, b):
            n = x.shape[0]
            row, col = (edge_index[0], edge_index[1])
            loop = jnp.arange(n, dtype=row.dtype)
            row = jnp.concatenate([row, loop])
            col = jnp.concatenate([col, loop])
            ew = jnp.concatenate([edge_weight, jnp.ones((n,), dtype=x.dtype)])
            deg = jax.ops.segment_sum(ew, col, num_segments=n)
            dis = jnp.where(deg > 0, jax.lax.rsqrt(jnp.where(deg > 0, deg, 1.0)), 0.0)
            norm = dis[row] * ew * dis[col]
            h = x @ W.T
            msg = h[row] * norm[:, None]
            out = jax.ops.segment_sum(msg, col, num_segments=n)
            return out + b

        def _block(x, edge_index, edge_weight, g, bln, W, b):
            h = _layer_norm(x, g, bln)
            h = _gcn_conv(h, edge_index, edge_weight, W, b)
            h = jax.nn.relu(h)
            return x + h
        key = jax.random.key(seed)
        ks = jax.random.split(key, 8)
        s = 0.05
        return {'x': jax.random.normal(ks[0], (N_NODES, DIM), dtype=jnp.float32), 'edge_index': jax.random.randint(ks[1], (2, N_EDGES), 0, N_NODES, dtype=jnp.int64) if jax.config.jax_enable_x64 else jax.random.randint(ks[1], (2, N_EDGES), 0, N_NODES).astype(jnp.int32), 'edge_weight': jax.random.uniform(ks[2], (N_EDGES,), dtype=jnp.float32), 'ln6_g': jnp.ones((DIM,), jnp.float32), 'ln6_b': jnp.zeros((DIM,), jnp.float32), 'W6': jax.random.normal(ks[3], (DIM, DIM), jnp.float32) * s, 'b6': jnp.zeros((DIM,), jnp.float32), 'ln7_g': jnp.ones((DIM,), jnp.float32), 'ln7_b': jnp.zeros((DIM,), jnp.float32), 'W7': jax.random.normal(ks[4], (DIM, DIM), jnp.float32) * s, 'b7': jnp.zeros((DIM,), jnp.float32), 'Wp': jax.random.normal(ks[5], (DIM, DIM), jnp.float32) * s, 'bp': jnp.zeros((DIM,), jnp.float32)}
    _L2_gnn_all = _L2_gnn_setup()
    _L2_gnn_in = {k: v for k, v in _L2_gnn_all.items() if k in ('ln6_g', 'ln6_b', 'W6', 'b6', 'ln7_g', 'ln7_b', 'W7', 'b7', 'Wp', 'bp')}
    del _L2_gnn_all

    def _L2_ffn_setup():
        import jax, jax.numpy as jnp
        import numpy as np
        B, A = (256, 8)
        IN, OUT = (256, 256)
        SH1, SH2 = (256, 128)
        EH1, EH2 = (128, 64)
        E, TOPK = (4, 2)

        def _shared_mlp(x, W1, b1, W2, b2, W3, b3):
            h = jax.nn.relu(x @ W1 + b1)
            h = jax.nn.relu(h @ W2 + b2)
            return h @ W3 + b3

        def _experts_mlp(x, eW1, eb1, eW2, eb2, eW3, eb3):
            h = jax.nn.relu(jnp.einsum('baf,efh->ebah', x, eW1) + eb1[:, None, None, :])
            h = jax.nn.relu(jnp.einsum('ebah,ehg->ebag', h, eW2) + eb2[:, None, None, :])
            o = jnp.einsum('ebag,ego->ebao', h, eW3) + eb3[:, None, None, :]
            return jnp.moveaxis(o, 0, -1)
        key = jax.random.key(seed)
        ks = jax.random.split(key, 16)
        s = 0.05
        return {'x': jax.random.normal(ks[0], (B, A, IN), jnp.float32), 'sW1': jax.random.normal(ks[1], (IN, SH1), jnp.float32) * s, 'sb1': jnp.zeros((SH1,), jnp.float32), 'sW2': jax.random.normal(ks[2], (SH1, SH2), jnp.float32) * s, 'sb2': jnp.zeros((SH2,), jnp.float32), 'sW3': jax.random.normal(ks[3], (SH2, OUT), jnp.float32) * s, 'sb3': jnp.zeros((OUT,), jnp.float32), 'eW1': jax.random.normal(ks[4], (E, IN, EH1), jnp.float32) * s, 'eb1': jnp.zeros((E, EH1), jnp.float32), 'eW2': jax.random.normal(ks[5], (E, EH1, EH2), jnp.float32) * s, 'eb2': jnp.zeros((E, EH2), jnp.float32), 'eW3': jax.random.normal(ks[6], (E, EH2, OUT), jnp.float32) * s, 'eb3': jnp.zeros((E, OUT), jnp.float32), 'gW': jax.random.normal(ks[7], (IN, E), jnp.float32) * s, 'gb': jnp.zeros((E,), jnp.float32)}
    _L2_ffn_all = _L2_ffn_setup()
    _L2_ffn_in = {k: v for k, v in _L2_ffn_all.items() if k in ('sW1', 'sb1', 'sW2', 'sb2', 'sW3', 'sb3', 'eW1', 'eb1', 'eW2', 'eb2', 'eW3', 'eb3', 'gW', 'gb')}
    del _L2_ffn_all

    def _L3_gnn_setup():
        import jax, jax.numpy as jnp
        import numpy as np
        NUM_NODES = 3125
        NUM_EDGES = 50000
        IN_DIM = 256
        OUT_DIM = 256
        NUM_RELATIONS = 8
        key = jax.random.key(seed)
        k1, k2, k3, k4 = jax.random.split(key, 4)
        node_repr = jax.random.normal(k1, (NUM_NODES, IN_DIM), dtype=jnp.float32)
        edge_index = jax.random.randint(k2, (2, NUM_EDGES), 0, NUM_NODES, dtype=jnp.int64)
        edge_types = jax.random.randint(k3, (NUM_EDGES,), 0, NUM_RELATIONS, dtype=jnp.int64)
        limit = float(np.sqrt(6.0 / (IN_DIM + OUT_DIM)))
        weight = jax.random.uniform(k4, (NUM_RELATIONS, OUT_DIM, IN_DIM), dtype=jnp.float32, minval=-limit, maxval=limit)
        bias = jnp.zeros((OUT_DIM,), dtype=jnp.float32)
        return {'node_repr': node_repr, 'weight': weight, 'bias': bias, 'edge_index': edge_index, 'edge_types': edge_types}
    _L3_gnn_all = _L3_gnn_setup()
    _L3_gnn_in = {k: v for k, v in _L3_gnn_all.items() if k in ('weight', 'bias')}
    del _L3_gnn_all

    def _L3_ffn_setup():
        import math
        import jax, jax.numpy as jnp
        import numpy as np
        CAPACITY_FACTOR = 1.25
        key = jax.random.key(seed)
        ks = jax.random.split(key, 5)
        B, L, D, F, E = (8, 512, 256, 1024, 8)
        h = jax.random.normal(ks[0], (B, L, D), dtype=jnp.float32)
        gate_w = jax.random.normal(ks[1], (D, E), dtype=jnp.float32) * 0.02
        gate_b = jnp.zeros((E,), dtype=jnp.float32)
        w1 = jax.random.normal(ks[2], (E, D, F), dtype=jnp.float32) * (1.0 / math.sqrt(D))
        b1 = jnp.zeros((E, F), dtype=jnp.float32)
        w2 = jax.random.normal(ks[3], (E, F, D), dtype=jnp.float32) * (1.0 / math.sqrt(F))
        b2 = jnp.zeros((E, D), dtype=jnp.float32)
        return {'h': h, 'gate_w': gate_w, 'gate_b': gate_b, 'w1': w1, 'b1': b1, 'w2': w2, 'b2': b2}
    _L3_ffn_all = _L3_ffn_setup()
    _L3_ffn_in = {k: v for k, v in _L3_ffn_all.items() if k in ('gate_w', 'gate_b', 'w1', 'b1', 'w2', 'b2')}
    del _L3_ffn_all
    return {'x': x, 'src': src, 'dst': dst, 'edge_type_8': edge_type_8, 'edge_weight': edge_weight, 'L0_gnn_weight': _L0_gnn_in['weight'], 'L0_gnn_attn_l': _L0_gnn_in['attn_l'], 'L0_gnn_attn_r': _L0_gnn_in['attn_r'], 'L0_ffn_W_fx': _L0_ffn_in['W_fx'], 'L0_ffn_b_fx': _L0_ffn_in['b_fx'], 'L0_ffn_W_x': _L0_ffn_in['W_x'], 'L0_ffn_b_x': _L0_ffn_in['b_x'], 'L0_ffn_W_slice': _L0_ffn_in['W_slice'], 'L0_ffn_b_slice': _L0_ffn_in['b_slice'], 'L0_ffn_W_q': _L0_ffn_in['W_q'], 'L0_ffn_W_k': _L0_ffn_in['W_k'], 'L0_ffn_W_v': _L0_ffn_in['W_v'], 'L0_ffn_W_out': _L0_ffn_in['W_out'], 'L0_ffn_b_out': _L0_ffn_in['b_out'], 'L0_ffn_temperature': _L0_ffn_in['temperature'], 'L1_gnn_W1': _L1_gnn_in['W1'], 'L1_gnn_b1': _L1_gnn_in['b1'], 'L1_gnn_W2': _L1_gnn_in['W2'], 'L1_gnn_b2': _L1_gnn_in['b2'], 'L1_gnn_W3': _L1_gnn_in['W3'], 'L1_gnn_b3': _L1_gnn_in['b3'], 'L1_gnn_W4': _L1_gnn_in['W4'], 'L1_gnn_b4': _L1_gnn_in['b4'], 'L1_ffn_gate_w': _L1_ffn_in['gate_w'], 'L1_ffn_gate_b': _L1_ffn_in['gate_b'], 'L1_ffn_w1': _L1_ffn_in['w1'], 'L1_ffn_b1': _L1_ffn_in['b1'], 'L1_ffn_w2': _L1_ffn_in['w2'], 'L1_ffn_b2': _L1_ffn_in['b2'], 'L1_ffn_gamma': _L1_ffn_in['gamma'], 'L1_ffn_beta': _L1_ffn_in['beta'], 'L2_gnn_ln6_g': _L2_gnn_in['ln6_g'], 'L2_gnn_ln6_b': _L2_gnn_in['ln6_b'], 'L2_gnn_W6': _L2_gnn_in['W6'], 'L2_gnn_b6': _L2_gnn_in['b6'], 'L2_gnn_ln7_g': _L2_gnn_in['ln7_g'], 'L2_gnn_ln7_b': _L2_gnn_in['ln7_b'], 'L2_gnn_W7': _L2_gnn_in['W7'], 'L2_gnn_b7': _L2_gnn_in['b7'], 'L2_gnn_Wp': _L2_gnn_in['Wp'], 'L2_gnn_bp': _L2_gnn_in['bp'], 'L2_ffn_sW1': _L2_ffn_in['sW1'], 'L2_ffn_sb1': _L2_ffn_in['sb1'], 'L2_ffn_sW2': _L2_ffn_in['sW2'], 'L2_ffn_sb2': _L2_ffn_in['sb2'], 'L2_ffn_sW3': _L2_ffn_in['sW3'], 'L2_ffn_sb3': _L2_ffn_in['sb3'], 'L2_ffn_eW1': _L2_ffn_in['eW1'], 'L2_ffn_eb1': _L2_ffn_in['eb1'], 'L2_ffn_eW2': _L2_ffn_in['eW2'], 'L2_ffn_eb2': _L2_ffn_in['eb2'], 'L2_ffn_eW3': _L2_ffn_in['eW3'], 'L2_ffn_eb3': _L2_ffn_in['eb3'], 'L2_ffn_gW': _L2_ffn_in['gW'], 'L2_ffn_gb': _L2_ffn_in['gb'], 'L3_gnn_weight': _L3_gnn_in['weight'], 'L3_gnn_bias': _L3_gnn_in['bias'], 'L3_ffn_gate_w': _L3_ffn_in['gate_w'], 'L3_ffn_gate_b': _L3_ffn_in['gate_b'], 'L3_ffn_w1': _L3_ffn_in['w1'], 'L3_ffn_b1': _L3_ffn_in['b1'], 'L3_ffn_w2': _L3_ffn_in['w2'], 'L3_ffn_b2': _L3_ffn_in['b2']}

def reference(x, src, dst, edge_type_8, edge_weight, L0_gnn_weight, L0_gnn_attn_l, L0_gnn_attn_r, L0_ffn_W_fx, L0_ffn_b_fx, L0_ffn_W_x, L0_ffn_b_x, L0_ffn_W_slice, L0_ffn_b_slice, L0_ffn_W_q, L0_ffn_W_k, L0_ffn_W_v, L0_ffn_W_out, L0_ffn_b_out, L0_ffn_temperature, L1_gnn_W1, L1_gnn_b1, L1_gnn_W2, L1_gnn_b2, L1_gnn_W3, L1_gnn_b3, L1_gnn_W4, L1_gnn_b4, L1_ffn_gate_w, L1_ffn_gate_b, L1_ffn_w1, L1_ffn_b1, L1_ffn_w2, L1_ffn_b2, L1_ffn_gamma, L1_ffn_beta, L2_gnn_ln6_g, L2_gnn_ln6_b, L2_gnn_W6, L2_gnn_b6, L2_gnn_ln7_g, L2_gnn_ln7_b, L2_gnn_W7, L2_gnn_b7, L2_gnn_Wp, L2_gnn_bp, L2_ffn_sW1, L2_ffn_sb1, L2_ffn_sW2, L2_ffn_sb2, L2_ffn_sW3, L2_ffn_sb3, L2_ffn_eW1, L2_ffn_eb1, L2_ffn_eW2, L2_ffn_eb2, L2_ffn_eW3, L2_ffn_eb3, L2_ffn_gW, L2_ffn_gb, L3_gnn_weight, L3_gnn_bias, L3_ffn_gate_w, L3_ffn_gate_b, L3_ffn_w1, L3_ffn_b1, L3_ffn_w2, L3_ffn_b2):
    import jax
    import jax.numpy as jnp

    def _L0_gnn_ref(x, edge_index, weight, attn_l, attn_r):
        import jax, jax.numpy as jnp
        import numpy as np
        N, IN_CH, HEADS, OUT_CH, E = (3125, 256, 4, 64, 50000)
        heads, out_ch = attn_l.shape
        n = x.shape[0]
        xt = jnp.matmul(x, weight).reshape(-1, heads, out_ch)
        row, col = (edge_index[0], edge_index[1])
        alpha_l = jnp.einsum('ehd,hd->eh', xt[row], attn_l)
        alpha_r = jnp.einsum('ehd,hd->eh', xt[col], attn_r)
        alpha = jax.nn.softmax(jax.nn.leaky_relu(alpha_l + alpha_r, 0.01), axis=1)
        tmp = jnp.einsum('nh,nhd->nd', alpha[:n], xt[col[:n]])
        out = jnp.broadcast_to(tmp[:, None, :], (n, heads, out_ch))
        return out.reshape(n, heads * out_ch)

    def _L0_ffn_ref(x, W_fx, b_fx, W_x, b_x, W_slice, b_slice, W_q, W_k, W_v, W_out, b_out, temperature):
        import jax, jax.numpy as jnp
        import numpy as np
        DIM = 256
        H = 8
        D = 64
        G = 64
        INNER = H * D
        SCALE = D ** (-0.5)
        B, N, _ = x.shape
        fx_mid = (x @ W_fx + b_fx).reshape(B, N, H, D).transpose(0, 2, 1, 3)
        x_mid = (x @ W_x + b_x).reshape(B, N, H, D).transpose(0, 2, 1, 3)
        temp = jnp.clip(temperature, 0.1, 5.0)
        slice_weights = jax.nn.softmax((x_mid @ W_slice + b_slice) / temp, axis=-1)
        slice_norm = slice_weights.sum(axis=2)
        slice_token = jnp.einsum('bhnc,bhng->bhgc', fx_mid, slice_weights)
        slice_token = slice_token / (slice_norm[..., None] + 1e-05)
        q = slice_token @ W_q
        k = slice_token @ W_k
        v = slice_token @ W_v
        attn = jax.nn.softmax(jnp.einsum('bhgc,bhkc->bhgk', q, k) * SCALE, axis=-1)
        out_slice = jnp.einsum('bhgk,bhkc->bhgc', attn, v)
        out_x = jnp.einsum('bhgc,bhng->bhnc', out_slice, slice_weights)
        out_x = out_x.transpose(0, 2, 1, 3).reshape(B, N, INNER)
        return out_x @ W_out + b_out

    def _L1_gnn_ref(x, edge_index, W1, b1, W2, b2, W3, b3, W4, b4):
        import jax, jax.numpy as jnp
        import numpy as np
        N_NODES = 3125

        def _add_self_loops(src, dst, n):
            loop = jnp.arange(n, dtype=src.dtype)
            return (jnp.concatenate([src, loop]), jnp.concatenate([dst, loop]))

        def gcn_conv(x, src, dst, W, b, n):
            h = x @ W
            deg = jnp.zeros((n,), h.dtype).at[dst].add(1.0)
            dinv = jax.lax.rsqrt(jnp.maximum(deg, 1e-12))
            norm = dinv[src] * dinv[dst]
            msg = h[src] * norm[:, None]
            return jax.ops.segment_sum(msg, dst, num_segments=n) + b
        n = x.shape[0]
        src, dst = _add_self_loops(edge_index[0], edge_index[1], n)
        h = jax.nn.relu(gcn_conv(x, src, dst, W1, b1, n))
        z = jax.nn.relu(gcn_conv(h, src, dst, W2, b2, n))
        h = jax.nn.relu(gcn_conv(z, src, dst, W3, b3, n))
        x_hat = gcn_conv(h, src, dst, W4, b4, n)
        return x_hat

    def _L1_ffn_ref(x, gate_w, gate_b, w1, b1, w2, b2, gamma, beta):
        import jax, jax.numpy as jnp
        import numpy as np
        B, S, H, F, E, K = (8, 256, 256, 512, 16, 2)
        EPS = 1e-05
        gate_logits = x @ gate_w + gate_b
        topk_vals, topk_idx = jax.lax.top_k(gate_logits, K)
        topk_w = jax.nn.softmax(topk_vals, axis=-1)
        h = jax.nn.relu(jnp.einsum('bsh,ehf->bsef', x, w1) + b1)
        expert_out = jnp.einsum('bsef,efh->bseh', h, w2) + b2
        sel = jnp.take_along_axis(expert_out, topk_idx[:, :, :, None], axis=2)
        moe = jnp.sum(topk_w[..., None] * sel, axis=2)
        y = x + moe
        mu = jnp.mean(y, axis=-1, keepdims=True)
        var = jnp.var(y, axis=-1, keepdims=True)
        return (y - mu) / jnp.sqrt(var + EPS) * gamma + beta

    def _L2_gnn_ref(x, edge_index, edge_weight, ln6_g, ln6_b, W6, b6, ln7_g, ln7_b, W7, b7, Wp, bp):
        import jax, jax.numpy as jnp
        import numpy as np
        N_NODES = 18870
        N_EDGES = 75000
        DIM = 256
        EPS = 1e-05

        def _layer_norm(x, g, b):
            mu = jnp.mean(x, axis=-1, keepdims=True)
            var = jnp.mean(jnp.square(x - mu), axis=-1, keepdims=True)
            return (x - mu) * jax.lax.rsqrt(var + EPS) * g + b

        def _gcn_conv(x, edge_index, edge_weight, W, b):
            n = x.shape[0]
            row, col = (edge_index[0], edge_index[1])
            loop = jnp.arange(n, dtype=row.dtype)
            row = jnp.concatenate([row, loop])
            col = jnp.concatenate([col, loop])
            ew = jnp.concatenate([edge_weight, jnp.ones((n,), dtype=x.dtype)])
            deg = jax.ops.segment_sum(ew, col, num_segments=n)
            dis = jnp.where(deg > 0, jax.lax.rsqrt(jnp.where(deg > 0, deg, 1.0)), 0.0)
            norm = dis[row] * ew * dis[col]
            h = x @ W.T
            msg = h[row] * norm[:, None]
            out = jax.ops.segment_sum(msg, col, num_segments=n)
            return out + b

        def _block(x, edge_index, edge_weight, g, bln, W, b):
            h = _layer_norm(x, g, bln)
            h = _gcn_conv(h, edge_index, edge_weight, W, b)
            h = jax.nn.relu(h)
            return x + h
        x = _block(x, edge_index, edge_weight, ln6_g, ln6_b, W6, b6)
        x = _block(x, edge_index, edge_weight, ln7_g, ln7_b, W7, b7)
        return x @ Wp.T + bp

    def _L2_ffn_ref(x, sW1, sb1, sW2, sb2, sW3, sb3, eW1, eb1, eW2, eb2, eW3, eb3, gW, gb):
        import jax, jax.numpy as jnp
        import numpy as np
        B, A = (256, 8)
        IN, OUT = (256, 256)
        SH1, SH2 = (256, 128)
        EH1, EH2 = (128, 64)
        E, TOPK = (4, 2)

        def _shared_mlp(x, W1, b1, W2, b2, W3, b3):
            h = jax.nn.relu(x @ W1 + b1)
            h = jax.nn.relu(h @ W2 + b2)
            return h @ W3 + b3

        def _experts_mlp(x, eW1, eb1, eW2, eb2, eW3, eb3):
            h = jax.nn.relu(jnp.einsum('baf,efh->ebah', x, eW1) + eb1[:, None, None, :])
            h = jax.nn.relu(jnp.einsum('ebah,ehg->ebag', h, eW2) + eb2[:, None, None, :])
            o = jnp.einsum('ebag,ego->ebao', h, eW3) + eb3[:, None, None, :]
            return jnp.moveaxis(o, 0, -1)
        all_out = _experts_mlp(x, eW1, eb1, eW2, eb2, eW3, eb3)
        shared = _shared_mlp(x, sW1, sb1, sW2, sb2, sW3, sb3)
        gates = jax.nn.softmax(x @ gW + gb, axis=-1)
        topv, topi = jax.lax.top_k(gates, TOPK)
        topw = jax.nn.softmax(topv, axis=-1)
        sel = jnp.take_along_axis(all_out, topi[:, :, None, :], axis=-1)
        gated = jnp.sum(sel * topw[:, :, None, :], axis=-1)
        return shared + gated

    def _L3_gnn_ref(node_repr, weight, bias, edge_index, edge_types):
        import jax, jax.numpy as jnp
        import numpy as np
        NUM_NODES = 3125
        NUM_EDGES = 50000
        IN_DIM = 256
        OUT_DIM = 256
        NUM_RELATIONS = 8
        h_all = jnp.einsum('ni,roi->rno', node_repr, weight)
        src, dst = (edge_index[0], edge_index[1])
        msgs = h_all[edge_types, src]
        messages = jax.ops.segment_sum(msgs, dst, num_segments=node_repr.shape[0])
        return messages + bias

    def _L3_ffn_ref(h, gate_w, gate_b, w1, b1, w2, b2):
        import math
        import jax, jax.numpy as jnp
        import numpy as np
        CAPACITY_FACTOR = 1.25
        B, L, D = h.shape
        E = gate_w.shape[1]
        T = B * L
        C = max(1, math.ceil(CAPACITY_FACTOR * T / E))
        x = h.reshape(T, D)
        logits = x @ gate_w + gate_b
        probs = jax.nn.softmax(logits, axis=-1)
        idx = jnp.argmax(probs, axis=-1)
        prb = jnp.take_along_axis(probs, idx[:, None], axis=1)[:, 0]
        one_hot = jax.nn.one_hot(idx, E, dtype=jnp.float32)
        pos = (jnp.cumsum(one_hot, axis=0) * one_hot).sum(-1).astype(jnp.int32) - 1
        kept = pos < C
        pos_safe = jnp.where(kept, pos, C)
        buf = jnp.zeros((E, C, D), dtype=h.dtype).at[idx, pos_safe].set(x, mode='drop')
        hmid = jax.nn.relu(jnp.einsum('ecd,edf->ecf', buf, w1) + b1[:, None, :])
        ybuf = jnp.einsum('ecf,efd->ecd', hmid, w2) + b2[:, None, :]
        pos_g = jnp.minimum(pos, C - 1)
        y_tok = ybuf[idx, pos_g] * (prb * kept)[:, None]
        y = y_tok.reshape(B, L, D)
        y = jnp.nan_to_num(y, nan=0.0, posinf=10000.0, neginf=-10000.0)
        return y
    edge_index = jnp.stack([src, dst])
    x = x + _L0_gnn_ref(_layernorm(x, axis=-1), edge_index, L0_gnn_weight, L0_gnn_attn_l, L0_gnn_attn_r)
    x = x + _L0_ffn_ref(_layernorm(x, axis=-1)[None], L0_ffn_W_fx, L0_ffn_b_fx, L0_ffn_W_x, L0_ffn_b_x, L0_ffn_W_slice, L0_ffn_b_slice, L0_ffn_W_q, L0_ffn_W_k, L0_ffn_W_v, L0_ffn_W_out, L0_ffn_b_out, L0_ffn_temperature)[0]
    x = x + _L1_gnn_ref(_layernorm(x, axis=-1), edge_index, L1_gnn_W1, L1_gnn_b1, L1_gnn_W2, L1_gnn_b2, L1_gnn_W3, L1_gnn_b3, L1_gnn_W4, L1_gnn_b4)
    x = x + _L1_ffn_ref(_layernorm(x, axis=-1)[None], L1_ffn_gate_w, L1_ffn_gate_b, L1_ffn_w1, L1_ffn_b1, L1_ffn_w2, L1_ffn_b2, L1_ffn_gamma, L1_ffn_beta)[0]
    x = x + _L2_gnn_ref(_layernorm(x, axis=-1), edge_index, edge_weight, L2_gnn_ln6_g, L2_gnn_ln6_b, L2_gnn_W6, L2_gnn_b6, L2_gnn_ln7_g, L2_gnn_ln7_b, L2_gnn_W7, L2_gnn_b7, L2_gnn_Wp, L2_gnn_bp)
    x = x + _L2_ffn_ref(_layernorm(x, axis=-1)[None], L2_ffn_sW1, L2_ffn_sb1, L2_ffn_sW2, L2_ffn_sb2, L2_ffn_sW3, L2_ffn_sb3, L2_ffn_eW1, L2_ffn_eb1, L2_ffn_eW2, L2_ffn_eb2, L2_ffn_eW3, L2_ffn_eb3, L2_ffn_gW, L2_ffn_gb)[0]
    x = x + _L3_gnn_ref(_layernorm(x, axis=-1), L3_gnn_weight, L3_gnn_bias, edge_index, edge_type_8)
    x = x + _L3_ffn_ref(_layernorm(x, axis=-1)[None], L3_ffn_gate_w, L3_ffn_gate_b, L3_ffn_w1, L3_ffn_b1, L3_ffn_w2, L3_ffn_b2)[0]
    return x

_drawn_inputs = setup_inputs


def setup_inputs(seed=0):
    import zlib

    import numpy as np

    out = dict(_drawn_inputs(seed))
    spreads = {'L0_ffn_b_fx': (0.0, 0.1),
     'L0_ffn_b_x': (0.0, 0.8),
     'L0_ffn_b_slice': (0.0, 0.8),
     'L0_ffn_b_out': (0.0, 0.1),
     'L0_ffn_temperature': (0.5, 0.6),
     'L1_gnn_b1': (0.0, 0.301),
     'L1_gnn_b2': (0.0, 0.1),
     'L1_gnn_b3': (0.0, 0.1),
     'L1_gnn_b4': (0.0, 0.1),
     'L1_ffn_gate_b': (0.0, 0.279),
     'L1_ffn_b1': (0.0, 0.697),
     'L1_ffn_b2': (0.0, 0.1),
     'L1_ffn_gamma': (1.0, 0.2),
     'L1_ffn_beta': (0.0, 0.1),
     'L2_gnn_ln6_g': (1.0, 0.6),
     'L2_gnn_ln6_b': (0.0, 0.1),
     'L2_gnn_b6': (0.0, 0.1),
     'L2_gnn_ln7_g': (1.0, 0.6),
     'L2_gnn_ln7_b': (0.0, 0.315),
     'L2_gnn_b7': (0.0, 0.275),
     'L2_gnn_bp': (0.0, 0.1),
     'L2_ffn_sb1': (0.0, 0.7),
     'L2_ffn_sb2': (0.0, 0.269),
     'L2_ffn_sb3': (0.0, 0.1),
     'L2_ffn_eb1': (0.0, 2.0),
     'L2_ffn_eb2': (0.0, 0.8),
     'L2_ffn_eb3': (0.0, 0.1),
     'L2_ffn_gb': (0.0, 0.69),
     'L3_gnn_bias': (0.0, 0.388),
     'L3_ffn_gate_b': (0.0, 0.466),
     'L3_ffn_b1': (0.0, 2.0),
     'L3_ffn_b2': (0.0, 2.0)}
    factors = {'L0_ffn_W_x': 7.883,
     'L0_ffn_W_slice': 8.0,
     'L0_ffn_W_q': 8.0,
     'L0_ffn_W_k': 8.0,
     'L2_ffn_eW1': 3.154,
     'L3_ffn_w1': 2.676}
    for name, (base, spread) in spreads.items():
        noise = np.random.default_rng([zlib.crc32(name.encode()), seed]).standard_normal(out[name].shape)
        drawn = base * np.exp(spread * noise) if base else spread * noise
        out[name] = jnp.asarray(drawn.astype(out[name].dtype))
    for name, factor in factors.items():
        out[name] = (out[name] * factor).astype(out[name].dtype)
    return out
```

```python
from contextlib import ExitStack, contextmanager

import concourse.bass as bass
from concourse import mybir

F32 = mybir.dt.float32
I32 = mybir.dt.int32
ALU = mybir.AluOpType
ACT = mybir.ActivationFunctionType
AX = mybir.AxisListType.X

N = 3125
T = 25
P = N // T
D = 256
K2 = D // 128
E = 50000
EC = E // 128
EREST = E - 128 * EC
U = 8
ET = -(-(EC + 1) // U) * U
R = 16
ST = -(-((E + T * 127) // 128) // R) * R
G = 5
EPS = 1e-5
ROUND = 12582912.0
BIG = 1e30


class Shared:
    pass


def row(a, i, lo=None, hi=None, p=P):
    lo, hi = lo or 0, hi if hi is not None else a.shape[2]
    return a[0:p, bass.ds(i, 1), lo:hi].rearrange("p a d -> p (a d)")


def wide(a, p, k, n):
    return a.rearrange("p (a n) -> p a n", a=1).broadcast_to([p, k, n])


def deep(a, p, k, n):
    return a.rearrange("p (k a) -> p k a", a=1).broadcast_to([p, k, n])


def hold(eng, sem, value, turn):
    eng.wait_ge(sem, value)
    eng.sem_inc(turn, 1)


def load_keys(nc, engine, kmap, at, n, keys):
    _, values = nc.values_load_multi_w_load_instructions(
        kmap[0:1, bass.ds(at, n)], engines=(engine,), min_val=0, max_val=keys - 1,
        skip_runtime_bounds_check_because="counting_sort makes keys of 0..keys-1")
    return values


@contextmanager
def stage(nc, g):
    if g.block is None:
        with nc.Block() as block:
            yield block
        return
    yield g.block
    g.phase += 1
    everyone = 4 * g.phase

    def leave(eng):
        eng.drain().then_inc(g.phase_done, 1)
        eng.wait_ge(g.phase_done, everyone)

    for engine in (g.block.sync, g.block.scalar, g.block.tensor, g.block.vector):
        engine(leave)


def bufs(nc, ctx, tag):
    def sb(name, shape, dt=F32):
        return ctx.enter_context(nc.sbuf_tensor(f"{tag}_{name}", shape, dt))

    def ps(name, shape, dt=F32):
        return ctx.enter_context(nc.psum_tensor(f"{tag}_{name}", shape, dt))

    def sem(name):
        return ctx.enter_context(nc.semaphore(f"{tag}_{name}"))

    return sb, ps, sem



def constants(nc, g, x_dram):
    with ExitStack() as ctx:
        sb, ps, sem = bufs(nc, ctx, "const")
        loaded, filled, shaped = sem("loaded"), sem("filled"), sem("shaped")
        block = ctx.enter_context(stage(nc, g))

        @block.sync
        def _(sp):
            sp.dma_start(g.X[0:P], x_dram.rearrange("(p t) d -> p t d", p=P)).then_inc(loaded, 16)
            sp.wait_ge(loaded, 16)

        @block.gpsimd
        def _(pool):
            pool.memset(g.ident[:, :], 0.0).then_inc(filled, 1)
            pool.memset(g.tri[:, :], 1.0).then_inc(filled, 1)
            pool.iota(g.iota[:, :], pattern=[[1, ST]], base=0, channel_multiplier=0,
                      allow_small_or_imprecise_dtypes=True)
            pool.iota(g.iota_p[:, :], pattern=[[1, 1]], base=0, channel_multiplier=1,
                      allow_small_or_imprecise_dtypes=True)
            pool.wait_ge(filled, 2)
            pool.affine_select(out=g.ident[:, :], in_=g.ident[:, :], compare_op=ALU.not_equal, fill=1.0,
                               base=0, pattern=[[-1, 128]], channel_multiplier=1).then_inc(shaped, 1)
            pool.affine_select(out=g.tri[:, :], in_=g.tri[:, :], compare_op=ALU.is_gt, fill=0.0,
                               base=0, pattern=[[1, 128]], channel_multiplier=-1).then_inc(shaped, 1)
            pool.wait_ge(shaped, 2)

        @block.vector
        def _(dve):
            nc.vector.memset(g.ones[:, :], 1.0)
            nc.vector.memset(g.zeros[:, :], 0.0)


def clear_semaphores(nc):
    free = sorted(nc.free_semaphores)
    with nc.Block() as block:
        @block.gpsimd
        def _(pool):
            pool.sem_clear(range(free[0], free[-1] + 1))



def layer_norm(nc, g, tag, src, dst):
    with ExitStack() as ctx:
        sb, ps, sem = bufs(nc, ctx, tag)
        st = sb("st", [128, T, 6])
        mean, spread, var, std, rstd = (sb(n, [128, T]) for n in ("mean", "spread", "var", "std", "rstd"))
        var_ready, std_ready = sem("var_ready"), sem("std_ready")
        shift, shift_ready = sb("shift", [128, T]), sem("shift_ready")
        block = ctx.enter_context(stage(nc, g))

        @block.vector
        def _(dve):
            for t in range(T):
                nc.vector.bn_stats(st[0:P, t, :], src[0:P, t, :])
            dve.drain()
            nc.vector.tensor_tensor(mean[0:P], st[0:P, :, 1], st[0:P, :, 4], ALU.add)
            nc.vector.tensor_tensor(spread[0:P], st[0:P, :, 1], st[0:P, :, 4], ALU.subtract)
            nc.vector.tensor_tensor(var[0:P], st[0:P, :, 2], st[0:P, :, 5], ALU.add)
            dve.drain()
            nc.vector.tensor_scalar(mean[0:P], mean[0:P], 0.5, None, ALU.mult)
            nc.vector.tensor_tensor(spread[0:P], spread[0:P], spread[0:P], ALU.mult)
            nc.vector.tensor_scalar(var[0:P], var[0:P], 1.0 / D, EPS, ALU.mult, ALU.add)
            dve.drain()
            nc.vector.scalar_tensor_tensor(out=var[0:P], in0=spread[0:P], scalar=0.25, in1=var[0:P],
                                           op0=ALU.mult, op1=ALU.add).then_inc(var_ready, 1)
            dve.wait_ge(std_ready, 1)
            nc.vector.reciprocal(rstd[0:P], std[0:P])
            dve.drain()
            nc.vector.scalar_tensor_tensor(out=shift[0:P], in0=mean[0:P], scalar=-1.0, in1=rstd[0:P],
                                           op0=ALU.mult, op1=ALU.mult).then_inc(shift_ready, 1)
            for t in range(T // 2 + 1):
                nc.vector.tensor_scalar(dst[0:P, t, :], src[0:P, t, :], mean[0:P, t:t + 1],
                                        rstd[0:P, t:t + 1], ALU.subtract, ALU.mult)

        @block.scalar
        def _(act):
            act.wait_ge(var_ready, 1)
            nc.scalar.activation(std[0:P], var[0:P], ACT.Sqrt).then_inc(std_ready, 1)
            act.wait_ge(shift_ready, 1)
            for t in range(T // 2 + 1, T):
                nc.scalar.activation(dst[0:P, t, :], src[0:P, t, :], ACT.Identity, bias=shift[0:P, t:t + 1],
                                     scale=rstd[0:P, t:t + 1])



def linear(nc, g, tag, src, width, w_dram, bias_dram, nout, finish, extra=None):
    kc = [min(128, width - k) for k in range(0, width, 128)]
    nk, rows = len(kc), kc[0]
    with ExitStack() as ctx:
        sb, ps, sem = bufs(nc, ctx, tag)
        in_sbuf = w_dram.shape[0] == 128 and len(w_dram.shape) == 3
        w = w_dram if in_sbuf else sb("w", [128, nk, nout])
        bias = sb("bias", [128, nout]) if bias_dram is not None else None
        xs = sb("xs", [128, G, width])
        xT = sb("xT", [128, G, nk, P])
        psT = ps("psT", [128, 3, 512])
        psO = ps("psO", [128, 3, 512])
        w_loaded, b_loaded = sem("w_loaded"), sem("b_loaded")
        staged, turned, turn_read = sem("staged"), sem("turned"), sem("turn_read")
        multiplied, put_away, turn = sem("multiplied"), sem("put_away"), sem("turn")
        block = ctx.enter_context(stage(nc, g))

        @block.sync
        def _(sp):
            if not in_sbuf:
                sp.dma_start(w[0:rows], w_dram.rearrange("(k p) n -> p k n", p=rows)).then_inc(w_loaded, 16)
                sp.wait_ge(w_loaded, 16)
            if bias is not None:
                sp.dma_start(bias[:, :], bias_dram.partition_broadcast(128)).then_inc(b_loaded, 16)
                sp.wait_ge(b_loaded, 16)

        @block.tensor
        def _(pe):
            if not in_sbuf:
                pe.wait_ge(w_loaded, 16)
            with pe.Fori(0, T // G) as i:
                for j in range(G):
                    pe.wait_ge(staged, i * G + j + 1)
                    pe.wait_ge(turn_read, i * G + j + 1)
                    if rows < 128:
                        pe.sem_inc(turn, 1)
                    for k in range(nk):
                        last = nc.tensor.transpose(psT[0:kc[k], j % 3, k * P:(k + 1) * P],
                                                   xs[0:P, j, k * 128:k * 128 + kc[k]], g.ident[0:P, 0:P])
                    last.then_inc(turned, 1)
                for j in range(G):
                    pe.wait_ge(turn_read, i * G + j + 3)
                    pe.wait_ge(put_away, i * G + j + 1)
                    for k in range(nk):
                        last = nc.tensor.matmul(psO[0:P, j % 3, 0:nout], xT[0:kc[k], j, k, :],
                                                w[0:kc[k], k, :], start=(k == 0), stop=(k == nk - 1))
                    last.then_inc(multiplied, 1)

        @block.scalar
        def _(act):
            act.sem_inc(turned, G)
            act.sem_inc(turn_read, 2)
            with act.Fori(0, T // G) as i:
                for j in range(G):
                    act.wait_ge(turned, i * G + j + 1)
                    nc.scalar.copy(xs[0:P, j, :], row(src, i * G + j, 0, width)).then_inc(staged, 1)
                for j in range(G):
                    act.wait_ge(turned, i * G + j + 1 + G)
                    nc.scalar.copy(xT[0:rows, j, :, :], psT[0:rows, j % 3, 0:nk * P].rearrange(
                        "p (k r) -> p k r", k=nk)).then_inc(turn_read, 1)

        @block.vector
        def _(dve):
            dve.sem_inc(put_away, 2)
            if bias is not None:
                dve.wait_ge(b_loaded, 16)
            if extra is not None:
                extra(dve)
            with dve.Fori(0, T // G) as i:
                for j in range(G):
                    dve.wait_ge(multiplied, i * G + j + 1)
                    finish(dve, i * G + j, psO[0:P, j % 3, 0:nout], bias).then_inc(put_away, 1)



def counting_sort(nc, g, tag, key, p, keys, n, pos, hot, base=None, kmap=None, slots=0, tiles=None):
    with ExitStack() as ctx:
        sb, ps, sem = bufs(nc, ctx, tag)
        seen = sb("seen", [128, keys, n])
        total = sb("total", [128, keys])
        nt, ends, starts, off = (sb(m, [128, keys]) for m in ("nt", "ends", "starts", "off"))
        pE, pC = ps("pE", [128, 512]), ps("pC", [128, 512])
        counted, summed = sem("counted"), sem("summed")
        block = ctx.enter_context(stage(nc, g))

        @block.vector
        def _(dve):
            nc.vector.tensor_tensor(hot[0:p], wide(key[0:p, 0:n], p, keys, n),
                                    deep(g.iota[0:p, 0:keys], p, keys, n), ALU.is_equal)
            dve.drain()
            with dve.Fori(0, keys) as k:
                nc.vector.tensor_tensor_scan(row(seen, k, p=p), g.ones[0:p, 0:n], row(hot, k, 0, n, p=p), 0.0,
                                             ALU.mult, ALU.add)
            dve.drain()
            nc.vector.tensor_copy(total[0:p], seen[0:p, :, n - 1]).then_inc(counted, 1)
            dve.wait_ge(summed, 1)
            nc.vector.tensor_scalar(off[0:p], pE[0:p, 0:keys], -1.0, None, ALU.add)
            if base is None:
                nc.vector.tensor_scalar(nt[0:p], pC[0:p, 0:keys], 1.0 / 128, 63.5 / 128, ALU.mult, ALU.add)
                dve.drain()
                nc.vector.tensor_scalar(nt[0:p], nt[0:p], ROUND, None, ALU.add)
                dve.drain()
                nc.vector.tensor_scalar(nt[0:p], nt[0:p], -ROUND, None, ALU.add)
                dve.drain()
                nc.vector.tensor_tensor_scan(ends[0:p], g.ones[0:p, 0:keys], nt[0:p], 0.0, ALU.mult, ALU.add)
                nc.vector.memset(tiles[0:1, :], -1.0)
                dve.drain()
                nc.vector.tensor_tensor(starts[0:p], ends[0:p], nt[0:p], ALU.subtract)
                dve.drain()
                nc.vector.scalar_tensor_tensor(out=off[0:p], in0=starts[0:p], scalar=128.0, in1=off[0:p],
                                               op0=ALU.mult, op1=ALU.add)
                with dve.Fori(0, keys) as k:
                    nc.vector.scalar_tensor_tensor(out=tiles[0:1, :], in0=g.iota[0:1, 0:slots],
                                                   scalar=starts[0:1, bass.ds(k, 1)], in1=tiles[0:1, :],
                                                   op0=ALU.is_ge, op1=ALU.add)
                    dve.drain()
                nc.vector.tensor_copy(kmap[0:1, 0:slots], tiles[0:1, :])
            dve.drain()
            nc.vector.tensor_tensor(seen[0:p], seen[0:p], deep(off[0:p], p, keys, n), ALU.add)
            dve.drain()
            nc.vector.tensor_tensor(seen[0:p], seen[0:p], hot[0:p], ALU.mult)
            dve.drain()
            nc.vector.tensor_reduce(pos[0:p, 0:n], seen[0:p].rearrange("p k n -> p n k"), AX, ALU.add)

        @block.tensor
        def _(pe):
            pe.wait_ge(counted, 1)
            nc.tensor.matmul(pE[0:p, 0:keys], g.tri[0:p, 0:p], total[0:p], start=True, stop=True)
            nc.tensor.matmul(pC[0:p, 0:keys], g.ones[0:p, 0:p], total[0:p], start=True,
                             stop=True).then_inc(summed, 1)



def prepare_graph(nc, g, src, dst, etype, eweight):
    with ExitStack() as ctx:
        sb, ps, sem = bufs(nc, ctx, "edges")
        raw = sb("raw", [128, 3, ET], I32)
        rec = sb("rec", [128, ET, 4])
        hot = sb("hot", [128, 2, T, ET])
        key, pos, pad, tmp = (sb(m, [128, ET]) for m in ("key", "pos", "pad", "tmp"))
        tiles = sb("tiles", [128, ST])
        padrow = sb("padrow", [128, 1])
        cleared, loaded, blank, filled = sem("cleared"), sem("loaded"), sem("blank"), sem("filled")

        with stage(nc, g) as block:
            @block.vector
            def _(dve):
                nc.vector.memset(raw[:, :, :], 0).then_inc(cleared, 1)
                nc.vector.memset(rec[:, :, :], 0.0).then_inc(cleared, 1)
                nc.vector.memset(g.slots[:, :, :], 0.0)
                dve.drain()
                nc.vector.memset(g.slots[:, :, 1], -1.0).then_inc(blank, 1)
                nc.vector.memset(pad[:, :], 0.0)
                dve.drain()
                nc.vector.memset(pad[:, EC + 1:ET], 1.0)
                nc.vector.tensor_scalar(pad[:, EC:EC + 1], g.iota_p[:, :], float(EREST), None, ALU.is_ge)

            @block.sync
            def _(sp):
                sp.wait_ge(cleared, 2)
                for k, a in enumerate((src, dst, etype)):
                    sp.dma_start(raw[:, k, 0:EC], a[0:128 * EC].rearrange("(p t) -> p t", p=128)).then_inc(loaded, 16)
                    sp.dma_start(raw[0:EREST, k, EC:EC + 1],
                                 a[128 * EC:E].rearrange("(p t) -> p t", t=1)).then_inc(loaded, 16)
                sp.dma_start(tmp[:, 0:EC], eweight[0:128 * EC].rearrange("(p t) -> p t", p=128)).then_inc(loaded, 16)
                sp.dma_start(rec[0:EREST, EC, 2:3], eweight[128 * EC:E].rearrange("(p t) -> p t", t=1)).then_inc(loaded, 16)
                sp.wait_ge(blank, 1)
                sp.dma_start(g.slots_dram[0:128 * ST, :].rearrange("(p t) f -> p t f", p=128),
                             g.slots[:, 0:ST, :]).then_inc(filled, 16)
                sp.wait_ge(loaded, 128)
                sp.wait_ge(filled, 16)

        with stage(nc, g) as block:
            @block.vector
            def _(dve):
                nc.vector.tensor_copy(rec[:, 0:EC, 2], tmp[:, 0:EC])
                nc.vector.tensor_copy(rec[:, :, 0], raw[:, 0, :])
                nc.vector.tensor_copy(key[:, :], raw[:, 1, :])
                nc.vector.tensor_copy(rec[:, :, 3], raw[:, 2, :])
                dve.drain()
                nc.vector.scalar_tensor_tensor(out=rec[:, :, 3], in0=rec[:, :, 3], scalar=float(N),
                                               in1=rec[:, :, 0], op0=ALU.mult, op1=ALU.add)
                nc.vector.tensor_scalar(tmp[:, :], key[:, :], 1.0 / T, -(T // 2) / T, ALU.mult, ALU.add)
                dve.drain()
                nc.vector.tensor_scalar(tmp[:, :], tmp[:, :], ROUND, None, ALU.add)
                dve.drain()
                nc.vector.tensor_scalar(rec[:, :, 1], tmp[:, :], -ROUND, None, ALU.add)
                dve.drain()
                nc.vector.scalar_tensor_tensor(out=key[:, :], in0=rec[:, :, 1], scalar=-float(T),
                                               in1=key[:, :], op0=ALU.mult, op1=ALU.add)
                nc.vector.tensor_scalar(padrow[:, :], g.iota_p[:, :], float(128 * ST), None, ALU.add)
                dve.drain()
                nc.vector.scalar_tensor_tensor(out=key[:, :], in0=pad[:, :], scalar=100.0, in1=key[:, :],
                                               op0=ALU.mult, op1=ALU.add)

        counting_sort(nc, g, "sort", key, 128, T, ET, pos, hot[:, 0], kmap=g.kmap, slots=ST, tiles=tiles)

        ohl = sb("ohl", [128, U, P])
        idx = sb("idx", [128, U], I32)
        one = sb("one", [128, U, 4])
        pdeg = ps("pdeg", [128, 512])
        weighted, hot_ready, hot_used = sem("weighted"), sem("hot_ready"), sem("hot_used")
        placed, staged, opened = sem("placed"), sem("staged"), sem("opened")
        turn, slots_back, slots_placed = sem("turn"), sem("slots_back"), sem("slots_placed")
        scattered = g.moved
        before = [g.count(j, 16 * (ET // U)) - 16 * (ET // U) for j in range(U)]
        with stage(nc, g) as block:
            @block.vector
            def _(dve):
                nc.vector.tensor_scalar(tmp[:, :], pos[:, :], 1.0 / 128, -63.5 / 128, ALU.mult, ALU.add)
                dve.drain()
                nc.vector.tensor_scalar(tmp[:, :], tmp[:, :], ROUND, None, ALU.add)
                dve.drain()
                nc.vector.tensor_scalar(tmp[:, :], tmp[:, :], -ROUND, None, ALU.add)
                dve.drain()
                nc.vector.scalar_tensor_tensor(out=pos[:, :], in0=tmp[:, :], scalar=-128.0, in1=pos[:, :],
                                               op0=ALU.mult, op1=ALU.add)
                dve.drain()
                nc.vector.scalar_tensor_tensor(out=pos[:, :], in0=pos[:, :], scalar=float(ST), in1=tmp[:, :],
                                               op0=ALU.mult, op1=ALU.add)
                nc.vector.tensor_scalar(pad[:, :], pad[:, :], padrow[:, :], None, ALU.mult)
                dve.drain()
                for c in range(EC + 1, ET):
                    nc.vector.tensor_scalar(pad[:, c:c + 1], pad[:, c:c + 1], float(128 * (c - EC)), None, ALU.add)
                dve.drain()
                nc.vector.tensor_tensor(pos[:, :], pos[:, :], pad[:, :], ALU.add).then_inc(placed, 1)
                nc.vector.tensor_tensor(hot[:, 1], hot[:, 0], rec[:, :, 2:3].rearrange("p t a -> p a t").broadcast_to([128, T, ET]),
                                        ALU.mult).then_inc(weighted, 1)
                dve.sem_inc(hot_used, U)
                with dve.Fori(0, ET // U) as i:
                    for j in range(U):
                        dve.wait_ge(hot_used, i * U + j + 1)
                        nc.vector.tensor_scalar(ohl[:, j, :], g.iota[:, 0:P],
                                                row(rec, i * U + j, 1, 2, p=128), None,
                                                ALU.is_equal).then_inc(hot_ready, 1)
                dve.wait_ge(opened, 1)
                nc.vector.tensor_scalar(g.dinv1[0:P], pdeg[0:P, 0:T], 1.0, 1e-12, ALU.add, ALU.max)
                nc.vector.tensor_scalar(g.dinv2[0:P], pdeg[0:P, T:2 * T], 1.0, None, ALU.add)

            @block.tensor
            def _(pe):
                pe.wait_ge(weighted, 1)
                nc.tensor.matmul(pdeg[0:P, 0:2 * T], g.zeros[:, 0:P], g.zeros[:, 0:2 * T], start=True, stop=False)
                with pe.Fori(0, ET // U) as i:
                    for j in range(U):
                        pe.wait_ge(hot_ready, i * U + j + 1)
                        nc.tensor.matmul(pdeg[0:P, 0:2 * T], ohl[:, j, :],
                                         hot[:, :, :, bass.ds(i * U + j, 1)].rearrange("p a k t -> p (a k t)"),
                                         start=False, stop=False, skip_group_check=True).then_inc(hot_used, 1)
                nc.tensor.matmul(pdeg[0:P, 0:2 * T], g.zeros[:, 0:P], g.zeros[:, 0:2 * T], start=False,
                                 stop=True).then_inc(opened, 1)

            @block.scalar
            def _(act):
                act.wait_ge(placed, 1)
                for j in range(U):
                    nc.scalar.copy(idx[:, j:j + 1], pos[:, j:j + 1])
                    nc.scalar.copy(one[:, j, :], rec[:, j, :])
                    act.drain().then_inc(staged, 1)
                with act.Fori(1, ET // U) as i:
                    for j in range(U):
                        act.wait_ge(scattered[j], before[j] + i * 16)
                        nc.scalar.copy(idx[:, j:j + 1], pos[:, bass.ds(i * U + j, 1)])
                        nc.scalar.copy(one[:, j, :], row(rec, i * U + j, p=128))
                        act.drain().then_inc(staged, 1)

            @block.gpsimd
            def _(pool):
                with pool.Fori(0, ET // U) as i:
                    for j in range(U):
                        hold(pool, staged, i * U + j + 1, turn)
                        pool.indirect_dma_start(out=g.slots_dram[:, :],
                                                out_offset=bass.IndirectOffsetOnAxis(ap=idx[:, j:j + 1], axis=0),
                                                in_=one[:, j, :], in_offset=None).then_inc(scattered[j], 16)
                for j in range(U):
                    pool.wait_ge(scattered[j], before[j] + 16 * (ET // U))
                pool.sem_inc(slots_placed, 1)

            @block.sync
            def _(sp):
                sp.wait_ge(slots_placed, 1)
                sp.dma_start(g.slots[:, 0:ST, :], g.slots_dram[0:128 * ST, :].rearrange(
                    "(p t) f -> p t f", p=128)).then_inc(slots_back, 16)
                sp.wait_ge(slots_back, 16)

        positive, d1, d2 = sb("positive", [128, T]), sem("d1"), sem("d2")
        with stage(nc, g) as block:
            @block.vector
            def _(dve):
                nc.vector.tensor_scalar(positive[0:P], g.dinv2[0:P], 0.0, None, ALU.is_gt)
                dve.drain()
                nc.vector.tensor_tensor(g.dinv2[0:P], g.dinv2[0:P], positive[0:P], ALU.mult)
                dve.drain()
                nc.vector.scalar_tensor_tensor(out=g.dinv2[0:P], in0=g.dinv2[0:P], scalar=1.0, in1=positive[0:P],
                                               op0=ALU.add, op1=ALU.subtract).then_inc(d1, 1)
                dve.wait_ge(d2, 2)
                nc.vector.reciprocal(g.dinv1[0:P], g.dinv1[0:P])
                nc.vector.reciprocal(g.dinv2[0:P], g.dinv2[0:P])
                dve.drain()
                nc.vector.tensor_tensor(g.dinv2[0:P], g.dinv2[0:P], positive[0:P], ALU.mult)

            @block.scalar
            def _(act):
                act.wait_ge(d1, 1)
                nc.scalar.activation(g.dinv1[0:P], g.dinv1[0:P], ACT.Sqrt).then_inc(d2, 1)
                nc.scalar.activation(g.dinv2[0:P], g.dinv2[0:P], ACT.Sqrt).then_inc(d2, 1)


def aggregate(nc, g, tag, acc, table, width, weighted=False, field=0):
    AHEAD, BANKS = R // 2, 8
    with ExitStack() as ctx:
        sb, ps, sem = bufs(nc, ctx, tag)
        idx = sb("idx", [128, R], I32)
        got = sb("got", [128, R, width])
        hot = sb("hot", [128, R, P])
        pp = ps("pp", [128, BANKS, 512])
        staged, hot_ready, multiplied = sem("staged"), sem("hot_ready"), sem("multiplied")
        added, turn = sem("added"), sem("turn")
        gathered = g.moved
        before = [g.count(j, 16 * (ST // R)) - 16 * (ST // R) for j in range(R)]
        block = ctx.enter_context(stage(nc, g))

        @block.scalar
        def _(act):
            act.sem_inc(multiplied, R)
            with act.Fori(0, ST // R) as i:
                for j in range(R):
                    act.wait_ge(multiplied, i * R + j + 1)
                    nc.scalar.copy(idx[:, j:j + 1], row(g.slots, i * R + j, field, field + 1, p=128)).then_inc(staged, 1)

        @block.gpsimd
        def _(pool):
            with pool.Fori(0, ST // R) as i:
                for j in range(R):
                    hold(pool, staged, i * R + j + 1, turn)
                    pool.indirect_dma_start(out=got[:, j, :], out_offset=None, in_=table[:, :],
                                            in_offset=bass.IndirectOffsetOnAxis(ap=idx[:, j:j + 1], axis=0)
                                            ).then_inc(gathered[j], 16)

        @block.tensor
        def _(pe):
            pe.sem_inc(added, BANKS)
            with pe.Fori(0, ST // R) as i:
                for j in range(R):
                    pe.wait_ge(gathered[j], (i + 1) * 16 + before[j])
                    pe.wait_ge(hot_ready, i * R + j + 1)
                    pe.wait_ge(added, i * R + j + 1)
                    nc.tensor.matmul(pp[0:P, j % BANKS, 0:width], hot[:, j, :], got[:, j, :], start=True,
                                     stop=True).then_inc(multiplied, 1)

        def one_hot(n, j):
            dst = row(g.slots, n, 1, 2, p=128)
            if weighted:
                ins = nc.vector.tensor_scalar(hot[:, j, :], g.iota[:, 0:P], dst, row(g.slots, n, 2, 3, p=128),
                                              ALU.is_equal, ALU.mult)
            else:
                ins = nc.vector.tensor_scalar(hot[:, j, :], g.iota[:, 0:P], dst, None, ALU.is_equal)
            ins.then_inc(hot_ready, 1)

        @block.vector
        def _(dve):
            for j in range(AHEAD):
                one_hot(j, j)
            with dve.Fori(0, ST // R) as i:
                for j in range(R):
                    if j % 4 == 0:
                        tile4 = load_keys(nc, mybir.EngineType.DVE, g.kmap, i * R + j, 4, T)
                    k = tile4[j % 4]
                    dve.drain()
                    dve.wait_ge(multiplied, i * R + j + 1 + R)
                    part = row(acc, k, 0, width)
                    nc.vector.tensor_tensor(part, part, pp[0:P, j % BANKS, 0:width], ALU.add).then_inc(added, 1)
                    one_hot(i * R + j + AHEAD, (j + AHEAD) % R)


def store(nc, g, tag, dram, src, width, also=None):
    with ExitStack() as ctx:
        stored = ctx.enter_context(nc.semaphore(f"{tag}_stored"))
        block = ctx.enter_context(stage(nc, g))

        @block.sync
        def _(sp):
            sp.dma_start(dram.rearrange("(p t) d -> p t d", p=P), src[0:P, :, 0:width]).then_inc(stored, 16)
            sp.wait_ge(stored, 16)



def layer0_gnn(nc, g, a):
    layer_norm(nc, g, "l0n", g.X, g.XN)
    with ExitStack() as ctx:
        sb, ps, sem = bufs(nc, ctx, "l0g")
        XT = sb("XT", [128, T, D + 4])
        AL = sb("AL", [128, T, 4])
        prod = sb("prod", [128, T, D])
        att = sb("att", [128, 2, D])
        i_dst, i_src = sb("i_dst", [128, T], I32), sb("i_src", [128, T], I32)

        def put(dve, i, product, bias):
            return nc.vector.tensor_copy(row(XT, i, 0, D), product)

        linear(nc, g, "l0w", g.XN, D, a["L0_gnn_weight"], None, D, put)

        att_loaded = sem("att_loaded")
        with stage(nc, g) as block:
            @block.sync
            def _(sp):
                sp.dma_start(att[:, 0, :], a["L0_gnn_attn_l"].rearrange("h d -> (h d)").partition_broadcast(128)).then_inc(att_loaded, 16)
                sp.dma_start(att[:, 1, :], a["L0_gnn_attn_r"].rearrange("h d -> (h d)").partition_broadcast(128)).then_inc(att_loaded, 16)
                sp.dma_start(i_src[0:P], a["src"][0:N].rearrange("(p t) -> p t", p=P)).then_inc(att_loaded, 16)
                sp.dma_start(i_dst[0:P], a["dst"][0:N].rearrange("(p t) -> p t", p=P)).then_inc(att_loaded, 16)
                sp.wait_ge(att_loaded, 64)

            @block.vector
            def _(dve):
                dve.wait_ge(att_loaded, 64)
                for k, out in ((0, AL[0:P]), (1, XT[0:P, :, D:D + 4])):
                    nc.vector.tensor_tensor(prod[0:P], XT[0:P, :, 0:D], wide(att[0:P, k, :], P, T, D), ALU.mult)
                    dve.drain()
                    nc.vector.tensor_reduce(out, prod[0:P].rearrange("p t (h d) -> p t h d", h=4), AX, ALU.add)
                    dve.drain()

        store(nc, g, "l0s", g.table260, XT, D + 4)
        store(nc, g, "l0s2", g.table4, AL, 4)
        gathered = g.moved[0]
        done = g.count(0, 32 * T)
        with stage(nc, g) as block:
            @block.gpsimd
            def _(pool):
                for t in range(T):
                    pool.indirect_dma_start(out=XT[0:P, t, :], out_offset=None, in_=g.table260[:, :],
                                            in_offset=bass.IndirectOffsetOnAxis(ap=i_dst[0:P, t:t + 1], axis=0)
                                            ).then_inc(gathered, 16)
                    pool.indirect_dma_start(out=AL[0:P, t, :], out_offset=None, in_=g.table4[:, :],
                                            in_offset=bass.IndirectOffsetOnAxis(ap=i_src[0:P, t:t + 1], axis=0)
                                            ).then_inc(gathered, 16)
                pool.wait_ge(gathered, done)

        small = sb("small", [128, 3, T])
        raw = sb("raw", [128, T, 4])
        centred, powers = sem("centred"), sem("powers")
        with stage(nc, g) as block:
            @block.vector
            def _(dve):
                nc.vector.tensor_tensor(raw[0:P], AL[0:P], XT[0:P, :, D:D + 4], ALU.add)
                dve.drain()
                nc.vector.tensor_scalar(AL[0:P], raw[0:P], 0.01, None, ALU.mult)
                dve.drain()
                nc.vector.tensor_tensor(AL[0:P], AL[0:P], raw[0:P], ALU.max)
                dve.drain()
                nc.vector.tensor_reduce(small[0:P, 0], AL[0:P], AX, ALU.max)
                dve.drain()
                nc.vector.tensor_tensor(AL[0:P], AL[0:P], deep(small[0:P, 0], P, T, 4), ALU.subtract).then_inc(centred, 1)
                dve.wait_ge(powers, 1)
                nc.vector.tensor_reduce(small[0:P, 1], AL[0:P], AX, ALU.add)
                dve.drain()
                nc.vector.reciprocal(small[0:P, 2], small[0:P, 1])
                dve.drain()
                nc.vector.tensor_tensor(AL[0:P], AL[0:P], deep(small[0:P, 2], P, T, 4), ALU.mult)
                dve.drain()
                nc.vector.tensor_tensor(prod[0:P].rearrange("p t (h d) -> p t h d", h=4),
                                        XT[0:P, :, 0:D].rearrange("p t (h d) -> p t h d", h=4),
                                        AL[0:P].rearrange("p t (h a) -> p t h a", a=1).broadcast_to([P, T, 4, 64]), ALU.mult)
                dve.drain()
                nc.vector.tensor_reduce(XT[0:P, :, 0:64], prod[0:P].rearrange("p t (h d) -> p t d h", h=4), AX, ALU.add)
                dve.drain()
                nc.vector.tensor_tensor(g.X[0:P].rearrange("p t (h d) -> p t h d", h=4),
                                        g.X[0:P].rearrange("p t (h d) -> p t h d", h=4),
                                        XT[0:P, :, 0:64].rearrange("p t (a d) -> p t a d", a=1).broadcast_to([P, T, 4, 64]), ALU.add)

            @block.scalar
            def _(act):
                act.wait_ge(centred, 1)
                nc.scalar.activation(AL[0:P], AL[0:P], ACT.Exp).then_inc(powers, 1)

HEADS, GROUPS = 8, 64
C4 = HEADS * GROUPS // 128


def layer0_ffn(nc, g, a):
    layer_norm(nc, g, "f0n", g.X, g.XN)
    with ExitStack() as ctx:
        sb, ps, sem = bufs(nc, ctx, "f0")
        SW = sb("SW", [128, T, HEADS * GROUPS])
        wxs = sb("wxs", [128, K2, HEADS * GROUPS])
        bxs = sb("bxs", [128, HEADS * GROUPS])
        M = sb("M", [128, C4, D])
        with ExitStack() as sub:
            sb1, ps1, sem1 = bufs(nc, sub, "f0a")
            wxT = sb1("wxT", [64, HEADS, D])
            wsl = sb1("wsl", [64, GROUPS])
            bx, bsl, temp = sb1("bx", [64, HEADS]), sb1("bsl", [128, GROUPS]), sb1("temp", [128, HEADS])
            bxw = sb1("bxw", [64, HEADS, 128])
            pw, pb = ps1("pw", [128, K2, 512]), ps1("pb", [128, 512])
            loaded, spread, made = sem1("loaded"), sem1("spread"), sem1("made")
            block = sub.enter_context(stage(nc, g))

            @block.sync
            def _(sp):
                sp.dma_start(wxT[:, :, :], a["L0_ffn_W_x"].rearrange("(h c) d -> c h d", c=64)).then_inc(loaded, 16)
                sp.dma_start(wsl[:, :], a["L0_ffn_W_slice"]).then_inc(loaded, 16)
                with nc.allow_non_contiguous_dma("a few hundred values"):
                    sp.dma_start(bx[:, :], a["L0_ffn_b_x"].rearrange("(h c) -> c h", c=64)).then_inc(loaded, 16)
                sp.dma_start(bsl[:, :], a["L0_ffn_b_slice"].partition_broadcast(128)).then_inc(loaded, 16)
                sp.dma_start(temp[:, :], a["L0_ffn_temperature"].rearrange("a h b c -> (a h b c)").partition_broadcast(128)).then_inc(loaded, 16)
                sp.wait_ge(loaded, 80)

            @block.vector
            def _(dve):
                dve.wait_ge(loaded, 80)
                nc.vector.tensor_copy(bxw[:, :, :], deep(bx[:, :], 64, HEADS, 128)).then_inc(spread, 1)
                nc.vector.tensor_scalar(temp[:, :], temp[:, :], 0.1, 5.0, ALU.max, ALU.min)
                dve.drain()
                nc.vector.reciprocal(temp[:, :], temp[:, :])
                dve.wait_ge(made, 1)
                dve.drain()
                scale = deep(temp[:, :], 128, HEADS, GROUPS)
                for k in range(K2):
                    nc.vector.tensor_tensor(wxs[:, k, :].rearrange("p (h s) -> p h s", h=HEADS),
                                            pw[:, k, :].rearrange("p (h s) -> p h s", h=HEADS), scale, ALU.mult)
                b3 = bxs[:, :].rearrange("p (h s) -> p h s", h=HEADS)
                nc.vector.tensor_tensor(b3, pb[:, :].rearrange("p (h s) -> p h s", h=HEADS),
                                        wide(bsl[:, :], 128, HEADS, GROUPS), ALU.add)
                dve.drain()
                nc.vector.tensor_tensor(b3, b3, scale, ALU.mult)

            @block.tensor
            def _(pe):
                pe.wait_ge(loaded, 80)
                pe.wait_ge(spread, 1)
                for h in range(HEADS):
                    cols = slice(h * GROUPS, (h + 1) * GROUPS)
                    for k in range(K2):
                        nc.tensor.matmul(pw[:, k, cols], wxT[:, h, k * 128:(k + 1) * 128], wsl[:, :],
                                         start=True, stop=True)
                    last = nc.tensor.matmul(pb[:, cols], bxw[:, h, :], wsl[:, :], start=True, stop=True)
                last.then_inc(made, 1)

        def put(dve, i, product, bias):
            return nc.vector.tensor_tensor(row(SW, i), product, bxs[0:P, :], ALU.add)

        linear(nc, g, "f0l", g.XN, D, wxs, None, HEADS * GROUPS, put)

        with ExitStack() as sub:
            sb1, ps1, sem1 = bufs(nc, sub, "f0s")
            top = sb1("top", [128, T * HEADS])
            centred, powers = sem1("centred"), sem1("powers")
            block = sub.enter_context(stage(nc, g))
            sw = SW[0:P].rearrange("p t (h s) -> p (t h) s", h=HEADS)

            @block.vector
            def _(dve):
                nc.vector.tensor_reduce(top[0:P], sw, AX, ALU.max)
                dve.drain()
                nc.vector.tensor_tensor(sw, sw, deep(top[0:P], P, T * HEADS, GROUPS), ALU.subtract).then_inc(centred, 1)
                dve.wait_ge(powers, 1)
                nc.vector.tensor_reduce(top[0:P], sw, AX, ALU.add)
                dve.drain()
                nc.vector.reciprocal(top[0:P], top[0:P])
                dve.drain()
                nc.vector.tensor_tensor(sw, sw, deep(top[0:P], P, T * HEADS, GROUPS), ALU.mult)

            @block.scalar
            def _(act):
                act.wait_ge(centred, 1)
                nc.scalar.activation(sw, sw, ACT.Exp).then_inc(powers, 1)

        with ExitStack() as sub:
            sb1, ps1, sem1 = bufs(nc, sub, "f0t")
            S = sb1("S", [128, C4, D + 1])
            with ExitStack() as inner:
                sb2, ps2, sem2 = bufs(nc, inner, "f0u")
                xs, xe = sb2("xs", [128, G, HEADS * GROUPS]), sb2("xe", [128, G, D + 1])
                pS = ps2("pS", [128, C4, 512])
                staged, staged_x, used, opened = (sem2(m) for m in ("staged", "staged_x", "used", "opened"))
                block = inner.enter_context(stage(nc, g))

                @block.scalar
                def _(act):
                    act.sem_inc(used, G)
                    with act.Fori(0, T // G) as i:
                        for j in range(G):
                            act.wait_ge(used, i * G + j + 1)
                            nc.scalar.copy(xs[0:P, j, :], row(SW, i * G + j)).then_inc(staged, 1)

                @block.tensor
                def _(pe):
                    for c in range(C4):
                        nc.tensor.matmul(pS[:, c, 0:D + 1], g.zeros[:, 0:128], g.zeros[:, 0:D + 1], start=True, stop=False)
                    with pe.Fori(0, T // G) as i:
                        for j in range(G):
                            pe.wait_ge(staged, i * G + j + 1)
                            pe.wait_ge(staged_x, i * G + j + 1)
                            for c in range(C4):
                                last = nc.tensor.matmul(pS[:, c, 0:D + 1], xs[0:P, j, c * 128:(c + 1) * 128],
                                                        xe[0:P, j, :], start=False, stop=False, skip_group_check=True)
                            last.then_inc(used, 1)
                    for c in range(C4):
                        last = nc.tensor.matmul(pS[:, c, 0:D + 1], g.zeros[:, 0:128], g.zeros[:, 0:D + 1], start=False, stop=True)
                    last.then_inc(opened, 1)

                @block.vector
                def _(dve):
                    nc.vector.memset(xe[:, :, D:D + 1], 1.0)
                    with dve.Fori(0, T // G) as i:
                        for j in range(G):
                            dve.wait_ge(used, i * G + j + 1)
                            nc.vector.tensor_copy(xe[0:P, j, 0:D], row(g.XN, i * G + j)).then_inc(staged_x, 1)
                    dve.wait_ge(opened, 1)
                    nc.vector.tensor_copy(S[:, :, :], pS[:, :, 0:D + 1])

            slice_attention(nc, g, a, S, M)

        def put2(dve, i, product, bias):
            nc.vector.tensor_tensor(row(g.XN, i), product, bias[0:P, :], ALU.add)
            dve.drain()
            return nc.vector.tensor_tensor(row(g.X, i), row(g.XN, i), row(g.X, i), ALU.add)

        linear(nc, g, "f0o", SW, HEADS * GROUPS, M, a["L0_ffn_b_out"], D, put2)


def slice_attention(nc, g, a, S, M):
    HG = HEADS * GROUPS
    with ExitStack() as ctx:
        sb, ps, sem = bufs(nc, ctx, "sa")
        wfx, bfx = sb("wfx", [128, K2, HG]), sb("bfx", [1, HG])
        wqkv, wout = sb("wqkv", [64, 3, 64]), sb("wout", [64, HEADS, D])
        rn, nrow = sb("rn", [128, C4]), sb("nrow", [1, HG])
        ST_ = sb("ST", [128, K2, HG])
        tok, q, k, v = (sb(m, [64, HG]) for m in ("tok", "q", "k", "v"))
        att, attT = sb("att", [64, HEADS, 64]), sb("attT", [64, HEADS, 64])
        vw, m64, top = sb("vw", [64, HEADS, D]), sb("m64", [64, HEADS, D]), sb("top", [64, HEADS])
        pA, pB = ps("pA", [128, 4, 512]), ps("pB", [128, 4, 512])
        loaded, pe_done, dve_done, act_done, moved = (sem(m) for m in ("loaded", "pe_done", "dve_done", "act_done", "moved"))
        block = ctx.enter_context(stage(nc, g))

        @block.sync
        def _(sp):
            sp.dma_start(wfx[:, :, :], a["L0_ffn_W_fx"].rearrange("(k p) n -> p k n", p=128)).then_inc(loaded, 16)
            sp.dma_start(bfx[:, :], a["L0_ffn_b_fx"].rearrange("(a n) -> a n", a=1)).then_inc(loaded, 16)
            for i, w in enumerate(("W_q", "W_k", "W_v")):
                sp.dma_start(wqkv[:, i, :], a["L0_ffn_" + w]).then_inc(loaded, 16)
            sp.dma_start(wout[:, :, :], a["L0_ffn_W_out"].rearrange("(h c) n -> c h n", c=64)).then_inc(loaded, 16)
            sp.wait_ge(loaded, 96)
            sp.wait_ge(dve_done, 8)
            sp.dma_start(M[0:64, :, :], m64[:, 0:HEADS:2, :]).then_inc(moved, 16)
            sp.dma_start(M[64:128, :, :], m64[:, 1:HEADS:2, :]).then_inc(moved, 16)
            sp.wait_ge(moved, 32)

        @block.vector
        def _(dve):
            nc.vector.tensor_scalar(rn[:, :], S[:, :, D], 1e-5, None, ALU.add)
            dve.drain()
            nc.vector.reciprocal(rn[:, :], rn[:, :])
            dve.drain()
            nc.vector.tensor_tensor(S[:, :, :], S[:, :, :], deep(rn[:, :], 128, C4, D + 1), ALU.mult).then_inc(dve_done, 1)
            dve.wait_ge(pe_done, 1)
            nc.vector.tensor_copy(ST_[:, :, :], pA[:, 0:K2, :])
            nc.vector.tensor_copy(nrow[:, :], pB[0:1, 0, :]).then_inc(dve_done, 1)
            dve.wait_ge(pe_done, 2)
            nc.vector.tensor_copy(tok[:, :], pB[0:64, 1, :]).then_inc(dve_done, 1)
            dve.wait_ge(pe_done, 3)
            nc.vector.tensor_copy(q[:, :], pA[0:64, 0, :])
            nc.vector.tensor_copy(k[:, :], pA[0:64, 1, :])
            nc.vector.tensor_copy(v[:, :], pA[0:64, 2, :]).then_inc(dve_done, 1)
            dve.wait_ge(pe_done, 4)
            scores = pB[0:64, 0, :].rearrange("p (h s) -> p h s", h=HEADS)
            nc.vector.tensor_reduce(top[:, :], scores, AX, ALU.max)
            dve.drain()
            nc.vector.tensor_tensor(att[:, :, :], scores, deep(top[:, :], 64, HEADS, 64), ALU.subtract).then_inc(dve_done, 1)
            dve.wait_ge(act_done, 1)
            nc.vector.tensor_reduce(top[:, :], att[:, :, :], AX, ALU.add)
            dve.drain()
            nc.vector.reciprocal(top[:, :], top[:, :])
            dve.drain()
            nc.vector.tensor_tensor(att[:, :, :], att[:, :, :], deep(top[:, :], 64, HEADS, 64), ALU.mult).then_inc(dve_done, 1)
            dve.wait_ge(pe_done, 5)
            nc.vector.tensor_copy(attT[:, :, :], pB[0:64, 2, :].rearrange("p (h s) -> p h s", h=HEADS))
            nc.vector.tensor_copy(vw[:, :, :], pA[0:64, :, :].rearrange("p b (h n) -> p (b h) n", n=D)).then_inc(dve_done, 1)
            dve.wait_ge(pe_done, 6)
            nc.vector.tensor_copy(m64[:, :, :], pB[0:64, :, :].rearrange("p b (h n) -> p (b h) n", n=D)).then_inc(dve_done, 1)

        @block.scalar
        def _(act):
            act.wait_ge(dve_done, 5)
            nc.scalar.activation(att[:, :, :], att[:, :, :], ACT.Exp, scale=64 ** -0.5).then_inc(act_done, 1)

        @block.tensor
        def _(pe):
            pe.wait_ge(dve_done, 1)
            for c in range(C4):
                for kk in range(K2):
                    nc.tensor.transpose(pA[:, kk, c * 128:(c + 1) * 128], S[:, c, kk * 128:(kk + 1) * 128], g.ident[:, :])
                last = nc.tensor.transpose(pB[0:1, 0, c * 128:(c + 1) * 128], S[:, c, D:D + 1], g.ident[:, :])
            last.then_inc(pe_done, 1)
            pe.wait_ge(dve_done, 2)
            pe.wait_ge(loaded, 96)
            for h in range(HEADS):
                cols = slice(h * 64, (h + 1) * 64)
                nc.tensor.matmul(pB[0:64, 1, cols], wfx[:, 0, cols], ST_[:, 0, cols], start=True, stop=False)
                nc.tensor.matmul(pB[0:64, 1, cols], wfx[:, 1, cols], ST_[:, 1, cols], start=False, stop=False)
                last = nc.tensor.matmul(pB[0:64, 1, cols], bfx[:, cols], nrow[:, cols], start=False, stop=True)
            last.then_inc(pe_done, 1)
            pe.wait_ge(dve_done, 3)
            for i in range(3):
                last = nc.tensor.matmul(pA[0:64, i, :], wqkv[:, i, :], tok[:, :], start=True, stop=True)
            last.then_inc(pe_done, 1)
            pe.wait_ge(dve_done, 4)
            for h in range(HEADS):
                cols = slice(h * 64, (h + 1) * 64)
                last = nc.tensor.matmul(pB[0:64, 0, cols], q[:, cols], k[:, cols], start=True, stop=True)
            last.then_inc(pe_done, 1)
            for h in range(HEADS):
                nc.tensor.matmul(pA[0:64, h // 2, (h % 2) * D:(h % 2 + 1) * D], v[:, h * 64:(h + 1) * 64], wout[:, h, :],
                                 start=True, stop=True)
            pe.wait_ge(dve_done, 6)
            for h in range(HEADS):
                last = nc.tensor.transpose(pB[0:64, 2, h * 64:(h + 1) * 64], att[:, h, :], g.ident[0:64, 0:64])
            last.then_inc(pe_done, 1)
            pe.wait_ge(dve_done, 7)
            for h in range(HEADS):
                last = nc.tensor.matmul(pB[0:64, h // 2, (h % 2) * D:(h % 2 + 1) * D], attT[:, h, :], vw[:, h, :],
                                        start=True, stop=True)
            last.then_inc(pe_done, 1)



def gcn_finish(nc, g, tag, acc, width, dinv, bias_dram, out, relu=True, residual=None):
    with ExitStack() as ctx:
        sb, ps, sem = bufs(nc, ctx, tag)
        loaded = sem("loaded")
        bias = sb("bias", [128, width])
        block = ctx.enter_context(stage(nc, g))

        @block.sync
        def _(sp):
            if bias_dram is not None:
                sp.dma_start(bias[:, :], bias_dram.partition_broadcast(128)).then_inc(loaded, 16)
                sp.wait_ge(loaded, 16)

        @block.vector
        def _(dve):
            nc.vector.tensor_tensor(acc[0:P], acc[0:P], deep(dinv[0:P], P, T, width), ALU.mult)
            if bias_dram is not None:
                dve.wait_ge(loaded, 16)
                dve.drain()
                nc.vector.tensor_tensor(acc[0:P], acc[0:P], wide(bias[0:P, :], P, T, width), ALU.add)
            if relu:
                dve.drain()
                if residual is None:
                    nc.vector.tensor_scalar(out[0:P], acc[0:P], 0.0, None, ALU.max)
                else:
                    nc.vector.scalar_tensor_tensor(out=out[0:P], in0=acc[0:P], scalar=0.0, in1=residual[0:P],
                                                   op0=ALU.max, op1=ALU.add)


def affine(nc, g, tag, a3, scale_dram, shift_dram, add_to=None):
    with ExitStack() as ctx:
        sb, ps, sem = bufs(nc, ctx, tag)
        loaded = sem("loaded")
        both = sb("both", [128, 2, D])
        block = ctx.enter_context(stage(nc, g))

        @block.sync
        def _(sp):
            sp.dma_start(both[:, 0, :], scale_dram.partition_broadcast(128)).then_inc(loaded, 16)
            sp.dma_start(both[:, 1, :], shift_dram.partition_broadcast(128)).then_inc(loaded, 16)
            sp.wait_ge(loaded, 32)

        @block.vector
        def _(dve):
            dve.wait_ge(loaded, 32)
            nc.vector.tensor_tensor(a3[0:P], a3[0:P], wide(both[0:P, 0, :], P, T, D), ALU.mult)
            dve.drain()
            nc.vector.tensor_tensor(a3[0:P], a3[0:P], wide(both[0:P, 1, :], P, T, D), ALU.add)
            if add_to is not None:
                dve.drain()
                nc.vector.tensor_tensor(add_to[0:P], add_to[0:P], a3[0:P], ALU.add)


def add_biased(nc, dst, tmp):
    def put(dve, i, product, bias):
        nc.vector.tensor_tensor(row(tmp, i, 0, D), product, bias[0:P, :], ALU.add)
        dve.drain()
        return nc.vector.tensor_tensor(row(dst, i), row(tmp, i, 0, D), row(dst, i), ALU.add)
    return put


def layer1_gnn(nc, g, a):
    layer_norm(nc, g, "g1n", g.X, g.XN)
    with ExitStack() as ctx:
        sb, ps, sem = bufs(nc, ctx, "g1")
        Z128, Z64 = sb("Z128", [128, T, 128]), sb("Z64", [128, T, 64])

        def scaled(out):
            return lambda dve, i, product, bias: nc.vector.tensor_scalar(
                row(out, i), product, g.dinv1[0:P, bass.ds(i, 1)], None, ALU.mult)

        linear(nc, g, "g1a", g.XN, D, a["L1_gnn_W1"], None, 128, scaled(Z128))
        store(nc, g, "g1as", g.table128, Z128, 128)
        aggregate(nc, g, "g1ag", Z128, g.table128, 128)
        gcn_finish(nc, g, "g1af", Z128, 128, g.dinv1, a["L1_gnn_b1"], Z128)

        linear(nc, g, "g1b", Z128, 128, a["L1_gnn_W2"], None, 64, scaled(Z64))
        store(nc, g, "g1bs", g.table64, Z64, 64)
        aggregate(nc, g, "g1bg", Z64, g.table64, 64)
        gcn_finish(nc, g, "g1bf", Z64, 64, g.dinv1, a["L1_gnn_b2"], Z64)

        gcn_finish(nc, g, "g1cd", Z64, 64, g.dinv1, None, Z64, relu=False)
        store(nc, g, "g1cs", g.table64, Z64, 64)
        aggregate(nc, g, "g1cg", Z64, g.table64, 64)
        gcn_finish(nc, g, "g1cf", Z64, 64, g.dinv1, None, Z64, relu=False)

        def hidden(dve, i, product, bias):
            nc.vector.tensor_tensor(row(Z128, i), product, bias[0:P, :], ALU.add)
            dve.drain()
            return nc.vector.tensor_scalar(row(Z128, i), row(Z128, i), 0.0, g.dinv1[0:P, bass.ds(i, 1)],
                                           ALU.max, ALU.mult)

        linear(nc, g, "g1d", Z64, 64, a["L1_gnn_W3"], a["L1_gnn_b3"], 128, hidden)
        store(nc, g, "g1ds", g.table128, Z128, 128)
        aggregate(nc, g, "g1dg", Z128, g.table128, 128)
        gcn_finish(nc, g, "g1df", Z128, 128, g.dinv1, None, Z128, relu=False)
        linear(nc, g, "g1e", Z128, 128, a["L1_gnn_W4"], a["L1_gnn_b4"], D, add_biased(nc, g.X, g.XN))


def layer2_gnn(nc, g, a):
    layer_norm(nc, g, "g2n", g.X, g.XN)
    with ExitStack() as ctx:
        sb, ps, sem = bufs(nc, ctx, "g2")
        H = sb("H", [128, T, D])
        for n in ("6", "7"):
            layer_norm(nc, g, f"g2n{n}", g.XN, H)
            affine(nc, g, f"g2a{n}", H, a[f"L2_gnn_ln{n}_g"], a[f"L2_gnn_ln{n}_b"])

            def scaled(dve, i, product, bias):
                return nc.vector.tensor_scalar(row(H, i), product, g.dinv2[0:P, bass.ds(i, 1)], None, ALU.mult)

            linear(nc, g, f"g2l{n}", H, D, a[f"L2_gnn_W{n}"], None, D, scaled)
            store(nc, g, f"g2s{n}", g.table256, H, D)
            aggregate(nc, g, f"g2g{n}", H, g.table256, D, weighted=True)
            gcn_finish(nc, g, f"g2f{n}", H, D, g.dinv2, a[f"L2_gnn_b{n}"], g.XN, residual=g.XN)
        linear(nc, g, "g2p", g.XN, D, a["L2_gnn_Wp"], a["L2_gnn_bp"], D, add_biased(nc, g.X, H))


def layer3_gnn(nc, g, a):
    layer_norm(nc, g, "g3n", g.X, g.XN)
    NR = a["L3_gnn_weight"].shape[0]
    NC = NR * D // 512
    with ExitStack() as ctx:
        sb, ps, sem = bufs(nc, ctx, "g3")
        w = sb("w", [128, K2, NR, D])
        bias = sb("bias", [128, D])
        xs, xT, ys = sb("xs", [128, G, D]), sb("xT", [128, G, K2, P]), sb("ys", [128, G, NR * D])
        psT, psO = ps("psT", [128, 3, 512]), ps("psO", [128, NC, 512])
        w_loaded, b_loaded, staged, turned, turn_read = (sem(m) for m in ("w_loaded", "b_loaded", "staged", "turned", "turn_read"))
        multiplied, put_away, turn = sem("multiplied"), sem("put_away"), sem("turn")
        stored = [sem(f"stored{j}") for j in range(G)]
        relations = g.relations.rearrange("(r p t) d -> t p r d", r=NR, p=P)
        block = ctx.enter_context(stage(nc, g))

        @block.sync
        def _(sp):
            for k in range(K2):
                sp.dma_start(w[:, k, :, :], a["L3_gnn_weight"][:, k * 128:(k + 1) * 128, :].rearrange("r p n -> p r n")).then_inc(w_loaded, 16)
            sp.dma_start(bias[:, :], a["L3_gnn_bias"].partition_broadcast(128)).then_inc(b_loaded, 16)
            with sp.Fori(0, T // G) as i:
                for j in range(G):
                    sp.wait_ge(put_away, (i * G + j + 2) * NC)
                    sp.dma_start(relations[bass.ds(i * G + j, 1)].rearrange("a p r d -> p (a r) d"),
                                 ys[0:P, j, :].rearrange("p (r d) -> p r d", d=D)).then_inc(stored[j], 16)
            for j in range(G):
                sp.wait_ge(stored[j], 16 * (T // G + 1))

        @block.tensor
        def _(pe):
            pe.wait_ge(w_loaded, 16 * K2)
            with pe.Fori(0, T // G) as i:
                for j in range(G):
                    pe.wait_ge(staged, i * G + j + 1)
                    pe.wait_ge(turn_read, i * G + j + 1)
                    for k in range(K2):
                        last = nc.tensor.transpose(psT[:, j % 3, k * P:(k + 1) * P], xs[0:P, j, k * 128:(k + 1) * 128],
                                                   g.ident[0:P, 0:P])
                    last.then_inc(turned, 1)
                for j in range(G):
                    pe.wait_ge(turn_read, i * G + j + 3)
                    for c in range(NC):
                        pe.wait_ge(put_away, (i * G + j) * NC + c + 1)
                        for k in range(K2):
                            last = nc.tensor.matmul(psO[0:P, c, :], xT[:, j, k, :],
                                                    w[:, k, 2 * c:2 * c + 2, :].rearrange("p r n -> p (r n)"),
                                                    start=(k == 0), stop=(k == K2 - 1))
                        last.then_inc(multiplied, 1)

        @block.scalar
        def _(act):
            act.sem_inc(turned, G)
            act.sem_inc(turn_read, 2)
            with act.Fori(0, T // G) as i:
                for j in range(G):
                    act.wait_ge(turned, i * G + j + 1)
                    nc.scalar.copy(xs[0:P, j, :], row(g.XN, i * G + j)).then_inc(staged, 1)
                for j in range(G):
                    act.wait_ge(turned, i * G + j + 1 + G)
                    nc.scalar.copy(xT[:, j, :, :], psT[:, j % 3, 0:K2 * P].rearrange("p (k r) -> p k r", k=K2)).then_inc(turn_read, 1)

        @block.vector
        def _(dve):
            dve.sem_inc(put_away, NC)
            for j in range(G):
                dve.sem_inc(stored[j], 16)
            dve.wait_ge(b_loaded, 16)
            nc.vector.tensor_tensor(g.X[0:P], g.X[0:P], wide(bias[0:P, :], P, T, D), ALU.add)
            with dve.Fori(0, T // G) as i:
                for j in range(G):
                    dve.wait_ge(stored[j], (i + 1) * 16)
                    for c in range(NC):
                        dve.wait_ge(multiplied, (i * G + j) * NC + c + 1)
                        nc.vector.tensor_copy(ys[0:P, j, c * 512:(c + 1) * 512], psO[0:P, c, :]).then_inc(put_away, 1)

    aggregate(nc, g, "g3g", g.X, g.relations, D, field=3)


def route(nc, g, tag, logits, n, first, softmax_first=False, hot=None, weight=None):
    with ExitStack() as ctx:
        sb, ps, sem = bufs(nc, ctx, tag)
        low = sb("low", [128, T, n])
        hots = hot if hot is not None else sb("hots", [128, T, 2, n])
        top = sb("top", [128, 2, T])
        centred, powers = sem("centred"), sem("powers")
        block = ctx.enter_context(stage(nc, g))
        iota = wide(g.iota[0:P, 0:n], P, T, n)
        L = logits[0:P]

        @block.vector
        def _(dve):
            if softmax_first:
                nc.vector.tensor_reduce(top[0:P, 0], L, AX, ALU.max)
                dve.drain()
                nc.vector.tensor_tensor(L, L, deep(top[0:P, 0], P, T, n), ALU.subtract).then_inc(centred, 1)
                dve.wait_ge(powers, 1)
                nc.vector.tensor_reduce(top[0:P, 0], L, AX, ALU.add)
                dve.drain()
                nc.vector.reciprocal(top[0:P, 0], top[0:P, 0])
                dve.drain()
                nc.vector.tensor_tensor(L, L, deep(top[0:P, 0], P, T, n), ALU.mult)
                dve.drain()
            for k in range(2):
                nc.vector.tensor_reduce(top[0:P, k], L, AX, ALU.max)
                dve.drain()
                nc.vector.tensor_tensor(low[0:P], L, deep(top[0:P, k], P, T, n), ALU.is_lt)
                dve.drain()
                nc.vector.scalar_tensor_tensor(out=low[0:P], in0=low[0:P], scalar=100.0, in1=iota, op0=ALU.mult, op1=ALU.add)
                dve.drain()
                nc.vector.tensor_reduce(first[0:P, :, k], low[0:P], AX, ALU.min)
                dve.drain()
                nc.vector.tensor_tensor(hots[0:P, :, k, :], iota, first[0:P, :, k:k + 1].broadcast_to([P, T, n]), ALU.is_equal)
                if k == 0:
                    dve.drain()
                    nc.vector.scalar_tensor_tensor(out=L, in0=hots[0:P, :, 0, :], scalar=-BIG, in1=L, op0=ALU.mult, op1=ALU.add)
                    dve.drain()
            nc.vector.tensor_tensor(weight[0:P, :, 1], top[0:P, 1], top[0:P, 0], ALU.subtract).then_inc(centred, 1)
            dve.wait_ge(powers, 2 if softmax_first else 1)
            nc.vector.tensor_scalar(weight[0:P, :, 0], weight[0:P, :, 1], 1.0, None, ALU.add)
            dve.drain()
            nc.vector.reciprocal(weight[0:P, :, 0], weight[0:P, :, 0])
            dve.drain()
            nc.vector.tensor_tensor(weight[0:P, :, 1], weight[0:P, :, 1], weight[0:P, :, 0], ALU.mult)

        @block.scalar
        def _(act):
            if softmax_first:
                act.wait_ge(centred, 1)
                nc.scalar.activation(L, L, ACT.Exp).then_inc(powers, 1)
            act.wait_ge(centred, 2 if softmax_first else 1)
            nc.scalar.activation(weight[0:P, :, 1], weight[0:P, :, 1], ACT.Exp).then_inc(powers, 1)


def gate(nc, g, tag, w, b, n, out):
    def put(dve, i, product, bias):
        return nc.vector.tensor_tensor(row(out, i), product, bias[0:P, :], ALU.add)
    linear(nc, g, tag, g.XN, D, w, b, n, put)


def layer1_ffn(nc, g, a):
    NE, _, F = a["L1_ffn_w1"].shape
    KF = F // 128
    SLOTS = (2 * N + NE * 127) // 128
    assert SLOTS % 2 == 0
    layer_norm(nc, g, "f1n", g.X, g.XN)
    with ExitStack() as ctx:
        sb, ps, sem = bufs(nc, ctx, "f1")
        logits, chosen, weight = sb("logits", [128, T, NE]), sb("chosen", [128, T, 2]), sb("weight", [128, T, 2])
        posf, posi = sb("posf", [128, 2 * T]), sb("posi", [128, 2 * T], I32)
        kmap = sb("kmap", [1, SLOTS], I32)
        gate(nc, g, "f1g", a["L1_ffn_gate_w"], a["L1_ffn_gate_b"], NE, logits)
        route(nc, g, "f1r", logits, NE, chosen, weight=weight)
        with ExitStack() as sub:
            sb1, ps1, sem1 = bufs(nc, sub, "f1s")
            hot, tiles = sb1("hot", [128, NE, 2 * T]), sb1("tiles", [1, SLOTS])
            counting_sort(nc, g, "f1c", chosen[:, :, :].rearrange("p t k -> p (t k)"), P, NE, 2 * T, posf, hot,
                          kmap=kmap, slots=SLOTS, tiles=tiles)
            cleared, placed = sem1("cleared"), sem1("placed")
            scattered, done = g.moved[0], g.count(0, 32 * T)
            block = sub.enter_context(stage(nc, g))

            @block.sync
            def _(sp):
                sp.dma_start(g.bins.rearrange("(p r) d -> p r d", p=128),
                             wide(g.zeros[:, 0:D], 128, 64, D)).then_inc(cleared, 16)

            @block.vector
            def _(dve):
                nc.vector.tensor_copy(posi[0:P], posf[0:P]).then_inc(placed, 1)

            @block.gpsimd
            def _(pool):
                pool.wait_ge(cleared, 16)
                pool.wait_ge(placed, 1)
                for t in range(T):
                    for k in range(2):
                        pool.indirect_dma_start(out=g.bins[:, :],
                                                out_offset=bass.IndirectOffsetOnAxis(ap=posi[0:P, 2 * t + k:2 * t + k + 1], axis=0),
                                                in_=g.XN[0:P, t, :], in_offset=None).then_inc(scattered, 16)
                pool.wait_ge(scattered, done)

        store(nc, g, "f1k", g.table256, g.XN, D)
        with ExitStack() as sub:
            sb1, ps1, sem1 = bufs(nc, sub, "f1e")
            w1, w2 = sb1("w1", [128, NE, K2, F]), sb1("w2", [128, NE, KF, D])
            b = sb1("b", [1, 2, F + D])
            room = g.XN[:, :, :].rearrange("p t d -> p (t d)")
            xs = room[:, 0:2 * D].rearrange("p (j d) -> p j d", j=2)
            xT = room[:, 2 * D:4 * D].rearrange("p (j k r) -> p j k r", j=2, k=K2)
            ys = room[:, 4 * D:6 * D].rearrange("p (j d) -> p j d", j=2)
            h = room[:, 6 * D:6 * D + 2 * F].rearrange("p (j n) -> p j n", j=2)
            hT = room[:, 6 * D + 2 * F:6 * D + 4 * F].rearrange("p (j k r) -> p j k r", j=2, k=KF)
            pT, pH, pU, pY = (ps1(m, [128, 2, 512]) for m in ("pT", "pH", "pU", "pY"))
            w_loaded = sem1("w_loaded")
            loaded, stored = [sem1(f"loaded{j}") for j in range(2)], [sem1(f"stored{j}") for j in range(2)]
            x_turned, x_read, h_made, h_put, h_turned, h_read, y_made, y_put = (
                sem1(m) for m in ("x_turned", "x_read", "h_made", "h_put", "h_turned", "h_read", "y_made", "y_put"))
            bins = g.bins.rearrange("(s p) d -> s p d", p=128)
            results = g.results.rearrange("(s p) d -> s p d", p=128)
            w1f, w2f = w1[:, :, :, :].rearrange("p e k n -> p (e k n)"), w2[:, :, :, :].rearrange("p e k n -> p (e k n)")
            block = sub.enter_context(stage(nc, g))

            @block.sync
            def _(sp):
                for e in range(NE):
                    sp.dma_start(w1[:, e, :, :], a["L1_ffn_w1"][e].rearrange("(k p) n -> p k n", p=128)).then_inc(w_loaded, 16)
                    sp.dma_start(w2[:, e, :, :], a["L1_ffn_w2"][e].rearrange("(k p) n -> p k n", p=128)).then_inc(w_loaded, 16)
                sp.sem_inc(y_made, 2)
                with sp.Fori(0, SLOTS // 2) as i:
                    for j in range(2):
                        e = sp.value_load(kmap[0:1, bass.ds(2 * i + j, 1)], min_val=0, max_val=NE - 1)
                        sp.wait_ge(y_made, 2 * i + j + 1)
                        sp.dma_start(xs[:, j, :], bins[bass.ds(2 * i + j, 1)].rearrange("a p d -> (a p) d")).then_inc(loaded[j], 16)
                        sp.dma_start(b[:, j, 0:F], a["L1_ffn_b1"][bass.ds(e, 1), :]).then_inc(loaded[j], 16)
                        sp.dma_start(b[:, j, F:F + D], a["L1_ffn_b2"][bass.ds(e, 1), :]).then_inc(loaded[j], 16)

            @block.tensor
            def _(pe):
                pe.wait_ge(w_loaded, 32 * NE)
                with pe.Fori(0, SLOTS // 2) as i:
                    expert = [pe.value_load(kmap[0:1, bass.ds(2 * i + j, 1)], min_val=0, max_val=NE - 1) for j in range(2)]
                    for j in range(2):
                        pe.wait_ge(loaded[j], (i + 1) * 48)
                        for k in range(K2):
                            last = nc.tensor.transpose(pT[:, j, k * 128:(k + 1) * 128], xs[:, j, k * 128:(k + 1) * 128], g.ident[:, :])
                        last.then_inc(x_turned, 1)
                    for j in range(2):
                        pe.wait_ge(x_read, 2 * i + j + 1)
                        for k in range(K2):
                            nc.tensor.matmul(pH[:, j, :], xT[:, j, k, :], w1f[:, bass.ds(expert[j] * (K2 * F) + k * F, F)],
                                             start=(k == 0), stop=False)
                        nc.tensor.matmul(pH[:, j, :], g.ones[0:1, 0:128], b[:, j, 0:F], start=False, stop=True).then_inc(h_made, 1)
                    for j in range(2):
                        pe.wait_ge(h_put, 2 * i + j + 1)
                        for k in range(KF):
                            last = nc.tensor.transpose(pU[:, j, k * 128:(k + 1) * 128], h[:, j, k * 128:(k + 1) * 128], g.ident[:, :])
                        last.then_inc(h_turned, 1)
                    for j in range(2):
                        pe.wait_ge(h_read, 2 * i + j + 1)
                        pe.wait_ge(y_put, 2 * i + j + 1)
                        for k in range(KF):
                            nc.tensor.matmul(pY[:, j, 0:D], hT[:, j, k, :], w2f[:, bass.ds(expert[j] * (KF * D) + k * D, D)],
                                             start=(k == 0), stop=False)
                        nc.tensor.matmul(pY[:, j, 0:D], g.ones[0:1, 0:128], b[:, j, F:F + D], start=False, stop=True).then_inc(y_made, 1)

            @block.scalar
            def _(act):
                for j in range(2):
                    act.sem_inc(stored[j], 16)
                with act.Fori(0, SLOTS // 2) as i:
                    for j in range(2):
                        act.wait_ge(x_turned, 2 * i + j + 1)
                        nc.scalar.copy(xT[:, j, :, :], pT[:, j, 0:K2 * 128].rearrange("p (k r) -> p k r", k=K2)).then_inc(x_read, 1)
                    for j in range(2):
                        act.wait_ge(h_turned, 2 * i + j + 1)
                        nc.scalar.copy(hT[:, j, :, :], pU[:, j, :].rearrange("p (k r) -> p k r", k=KF)).then_inc(h_read, 1)
                    for j in range(2):
                        act.wait_ge(y_put, 2 * i + j + 3)
                        act.dma_start(results[bass.ds(2 * i + j, 1)].rearrange("a p d -> (a p) d"), ys[:, j, :]).then_inc(stored[j], 16)
                for j in range(2):
                    act.wait_ge(stored[j], 16 * (SLOTS // 2 + 1))

            @block.vector
            def _(dve):
                dve.sem_inc(y_put, 2)
                with dve.Fori(0, SLOTS // 2) as i:
                    for j in range(2):
                        dve.wait_ge(h_made, 2 * i + j + 1)
                        nc.vector.tensor_scalar(h[:, j, :], pH[:, j, :], 0.0, None, ALU.max).then_inc(h_put, 1)
                    for j in range(2):
                        dve.wait_ge(y_made, 2 * i + j + 3)
                        dve.wait_ge(stored[j], (i + 1) * 16)
                        nc.vector.tensor_copy(ys[:, j, :], pY[:, j, 0:D]).then_inc(y_put, 1)

        with ExitStack() as sub:
            sb1, ps1, sem1 = bufs(nc, sub, "f1y")
            Y = [sb1(f"Y{k}", [128, T, D]) for k in range(2)]
            gathered, done = g.moved[0], g.count(0, 32 * T)
            reloaded = sem1("reloaded")
            with stage(nc, g) as block:
                @block.sync
                def _(sp):
                    sp.dma_start(g.XN[0:P], g.table256.rearrange("(p t) d -> p t d", p=P)).then_inc(reloaded, 16)

                @block.gpsimd
                def _(pool):
                    for t in range(T):
                        for k in range(2):
                            pool.indirect_dma_start(out=Y[k][0:P, t, :], out_offset=None, in_=g.results[:, :],
                                                    in_offset=bass.IndirectOffsetOnAxis(ap=posi[0:P, 2 * t + k:2 * t + k + 1], axis=0)
                                                    ).then_inc(gathered, 16)

                @block.vector
                def _(dve):
                    dve.wait_ge(gathered, done)
                    dve.wait_ge(reloaded, 16)
                    for k in range(2):
                        nc.vector.tensor_tensor(Y[k][0:P], Y[k][0:P], weight[0:P, :, k:k + 1].broadcast_to([P, T, D]), ALU.mult)
                        dve.drain()
                        nc.vector.tensor_tensor(g.XN[0:P], g.XN[0:P], Y[k][0:P], ALU.add)
            layer_norm(nc, g, "f1m", g.XN, Y[0])
            affine(nc, g, "f1a", Y[0], a["L1_ffn_gamma"], a["L1_ffn_beta"], add_to=g.X)


def layer2_ffn(nc, g, a):
    NE, _, H1 = a["L2_ffn_eW1"].shape
    H2 = a["L2_ffn_eW2"].shape[2]
    layer_norm(nc, g, "f2n", g.X, g.XN)
    with ExitStack() as ctx:
        sb, ps, sem = bufs(nc, ctx, "f2")
        logits, chosen, weight = sb("logits", [128, T, NE]), sb("chosen", [128, T, 2]), sb("weight", [128, T, 2])
        hot, coef = sb("hot", [128, T, 2, NE]), sb("coef", [128, T, NE])
        gate(nc, g, "f2g", a["L2_ffn_gW"], a["L2_ffn_gb"], NE, logits)
        route(nc, g, "f2r", logits, NE, chosen, softmax_first=True, hot=hot, weight=weight)
        with stage(nc, g) as block:
            @block.vector
            def _(dve):
                nc.vector.tensor_tensor(hot[0:P], hot[0:P], weight[0:P].rearrange("p t (k a) -> p t k a", a=1)
                                        .broadcast_to([P, T, 2, NE]), ALU.mult)
                dve.drain()
                nc.vector.tensor_tensor(coef[0:P], hot[0:P, :, 0, :], hot[0:P, :, 1, :], ALU.add)

        s1, s2, s3 = sb("s1", [128, K2, 256]), sb("s2", [128, 2, 128]), sb("s3", [128, D])
        e1, e2, e3 = sb("e1", [128, K2, NE, H1]), sb("e2", [128, NE, H2]), sb("e3", [H2 + 1, NE, D])
        sb1_, sb2_, sb3_ = sb("sb1", [128, 2]), sb("sb2", [128, 1]), sb("sb3", [128, D])
        eb1, eb2 = sb("eb1", [128, NE]), sb("eb2", [H2, NE])
        xs, xT = sb("xs", [128, G, D]), sb("xT", [128, G, K2, P])
        hs, he = sb("hs", [128, 2, P]), sb("he", [128, NE, P])
        h2s, h2e = sb("h2s", [128, P]), sb("h2e", [H2 + 1, NE, P])
        acc = sb("acc", [128, D])
        pT = ps("pT", [128, 2, 512])
        p1, p2, pE2 = ps("p1", [128, 512]), ps("p2", [128, 512]), ps("pE2", [128, 512])
        pO = ps("pO", [128, 3, 512])
        loaded, set1, staged, turned, turn_read, turn = (sem(m) for m in ("loaded", "set1", "staged", "turned", "turn_read", "turn"))
        hid1, hid1_read, hid2, hid2_read, outs, outs_read = (
            sem(m) for m in ("hid1", "hid1_read", "hid2", "hid2_read", "outs", "outs_read"))
        block = ctx.enter_context(stage(nc, g))

        @block.sync
        def _(sp):
            for out, src in ((s1[:, :, :], a["L2_ffn_sW1"].rearrange("(k p) n -> p k n", p=128)),
                             (s2[:, :, :], a["L2_ffn_sW2"].rearrange("(k p) n -> p k n", p=128)),
                             (s3[:, :], a["L2_ffn_sW3"]),
                             (e1[:, 0], a["L2_ffn_eW1"][:, 0:128, :].rearrange("e p n -> p e n")),
                             (e1[:, 1], a["L2_ffn_eW1"][:, 128:256, :].rearrange("e p n -> p e n")),
                             (e2[:, :, :], a["L2_ffn_eW2"].rearrange("e p n -> p e n")),
                             (e3[0:H2], a["L2_ffn_eW3"].rearrange("e p n -> p e n")),
                             (e3[H2:H2 + 1, :, :], a["L2_ffn_eb3"].rearrange("(a e) n -> a e n", a=1)),
                             (sb3_[:, :], a["L2_ffn_sb3"].partition_broadcast(128))):
                sp.dma_start(out, src).then_inc(loaded, 16)
            with nc.allow_non_contiguous_dma("a few hundred values"):
                sp.dma_start(sb1_[:, :], a["L2_ffn_sb1"].rearrange("(k p) -> p k", p=128)).then_inc(loaded, 16)
                sp.dma_start(sb2_[:, :], a["L2_ffn_sb2"].rearrange("(p k) -> p k", k=1)).then_inc(loaded, 16)
                sp.dma_start(eb1[:, :], a["L2_ffn_eb1"].rearrange("e p -> p e")).then_inc(loaded, 16)
                sp.dma_start(eb2[:, :], a["L2_ffn_eb2"].rearrange("e p -> p e")).then_inc(loaded, 16)
            sp.wait_ge(loaded, 208)

        @block.gpsimd
        def _(pool):
            pool.sem_inc(turned, G)
            with pool.Fori(0, T // G) as i:
                for j in range(G):
                    hold(pool, turned, i * G + j + 1, turn)
                    nc.gpsimd.tensor_copy(xs[0:P, j, :], row(g.XN, i * G + j)).then_inc(staged, 1)

        @block.tensor
        def _(pe):
            pe.wait_ge(loaded, 208)
            pe.wait_ge(set1, 1)
            with pe.Fori(0, T // G) as i:
                for j in range(G):
                    n = i * G + j
                    pe.wait_ge(staged, n + 1)
                    pe.wait_ge(turn_read, n + 1)
                    for k in range(K2):
                        last = nc.tensor.transpose(pT[:, 0, k * P:(k + 1) * P], xs[0:P, j, k * 128:(k + 1) * 128], g.ident[0:P, 0:P])
                    last.then_inc(turned, 1)
                    pe.wait_ge(turn_read, n + 2)
                    cols = lambda c: slice(c * P, (c + 1) * P)
                    for k in range(K2):
                        for c in range(2):
                            nc.tensor.matmul(p1[:, cols(c)], s1[:, k, c * 128:(c + 1) * 128], xT[:, j, k, :],
                                             start=(k == 0 and c == 0), stop=(k == 1), skip_group_check=True)
                        for e in range(NE):
                            where = p1[:, cols(2 + e)] if e < 2 else p2[:, cols(e - 2)]
                            last = nc.tensor.matmul(where, e1[:, k, e, :], xT[:, j, k, :], start=(k == 0 and e == 2),
                                                    stop=(k == 1), skip_group_check=True)
                    last.then_inc(hid1, 1)
                    pe.wait_ge(hid1_read, n + 1)
                    for k in range(2):
                        nc.tensor.matmul(pT[:, 1, 0:P], s2[:, k, :], hs[:, k, :], start=(k == 0), stop=(k == 1))
                    for e in range(NE):
                        last = nc.tensor.matmul(pE2[0:H2, cols(e)], e2[:, e, :], he[:, e, :], start=True, stop=True)
                    last.then_inc(hid2, 1)
                    pe.wait_ge(hid2_read, n + 1)
                    pe.wait_ge(outs_read, n + 1)
                    nc.tensor.matmul(pO[0:P, 0, 0:D], h2s[:, :], s3[:, :], start=True, stop=True)
                    for e in range(NE):
                        at = e + 1
                        last = nc.tensor.matmul(pO[0:P, at // 2, (at % 2) * D:(at % 2 + 1) * D], h2e[:, e, :], e3[:, e, :],
                                                start=True, stop=True)
                    last.then_inc(outs, 1)

        @block.scalar
        def _(act):
            act.wait_ge(loaded, 208)
            act.sem_inc(turn_read, 1)
            with act.Fori(0, T // G) as i:
                for j in range(G):
                    n = i * G + j
                    act.wait_ge(turned, n + 1 + G)
                    nc.scalar.copy(xT[:, j, :, :], pT[:, 0, 0:K2 * P].rearrange("p (k r) -> p k r", k=K2)).then_inc(turn_read, 1)
                    act.wait_ge(hid1, n + 1)
                    for c in range(2):
                        nc.scalar.activation(hs[:, c, :], p1[:, c * P:(c + 1) * P], ACT.Relu, bias=sb1_[:, c:c + 1])
                    for e in range(NE):
                        where = p1[:, (2 + e) * P:(3 + e) * P] if e < 2 else p2[:, (e - 2) * P:(e - 1) * P]
                        last = nc.scalar.activation(he[:, e, :], where, ACT.Relu, bias=eb1[:, e:e + 1])
                    act.drain().then_inc(hid1_read, 1)
                    act.wait_ge(hid2, n + 1)
                    nc.scalar.activation(h2s[:, :], pT[:, 1, 0:P], ACT.Relu, bias=sb2_[:, :])
                    for e in range(NE):
                        nc.scalar.activation(h2e[0:H2, e, :], pE2[0:H2, e * P:(e + 1) * P], ACT.Relu, bias=eb2[:, e:e + 1])
                    act.drain().then_inc(hid2_read, 1)

        @block.vector
        def _(dve):
            nc.vector.memset(h2e[H2:H2 + 1, :, :], 1.0).then_inc(set1, 1)
            dve.sem_inc(outs_read, 1)
            dve.wait_ge(loaded, 208)
            nc.vector.tensor_tensor(g.X[0:P], g.X[0:P], wide(sb3_[0:P, :], P, T, D), ALU.add)
            with dve.Fori(0, T // G) as i:
                for j in range(G):
                    n = i * G + j
                    dve.drain()
                    dve.wait_ge(outs, n + 1)
                    nc.vector.tensor_tensor(acc[0:P, :], pO[0:P, 0, 0:D], row(g.X, n), ALU.add)
                    for e in range(NE):
                        dve.drain()
                        at = e + 1
                        dst = acc[0:P, :] if e < NE - 1 else row(g.X, n)
                        last = nc.vector.scalar_tensor_tensor(out=dst, in0=pO[0:P, at // 2, (at % 2) * D:(at % 2 + 1) * D],
                                                              scalar=row(coef, n, e, e + 1), in1=acc[0:P, :],
                                                              op0=ALU.mult, op1=ALU.add)
                    last.then_inc(outs_read, 1)


def layer3_ffn(nc, g, a):
    NE, _, F = a["L3_ffn_w1"].shape
    KF = F // 128
    C = -(-(5 * N) // (4 * NE))
    CS = 4
    layer_norm(nc, g, "f3n", g.X, g.XN)
    with ExitStack() as ctx:
        sb, ps, sem = bufs(nc, ctx, "f3")
        logits = sb("logits", [128, T, NE])
        low = sb("low", [128, T, NE])
        best, total, pos, kept, slot, away = (sb(m, [128, T]) for m in ("best", "total", "pos", "kept", "slot", "away"))
        to, back = sb("to", [128, T], I32), sb("back", [128, T], I32)
        gate(nc, g, "f3g", a["L3_ffn_gate_w"], a["L3_ffn_gate_b"], NE, logits)
        centred, powers = sem("centred"), sem("powers")
        with stage(nc, g) as block:
            L = logits[0:P]

            @block.vector
            def _(dve):
                nc.vector.tensor_reduce(total[0:P], L, AX, ALU.max)
                dve.drain()
                nc.vector.tensor_tensor(L, L, deep(total[0:P], P, T, NE), ALU.subtract).then_inc(centred, 1)
                dve.wait_ge(powers, 1)
                nc.vector.tensor_reduce(total[0:P], L, AX, ALU.add)
                nc.vector.tensor_reduce(best[0:P], L, AX, ALU.max)
                dve.drain()
                nc.vector.reciprocal(total[0:P], total[0:P])
                nc.vector.tensor_tensor(low[0:P], L, deep(best[0:P], P, T, NE), ALU.is_lt)
                dve.drain()
                nc.vector.scalar_tensor_tensor(out=low[0:P], in0=low[0:P], scalar=100.0,
                                               in1=wide(g.iota[0:P, 0:NE], P, T, NE), op0=ALU.mult, op1=ALU.add)
                dve.drain()
                nc.vector.tensor_reduce(best[0:P], low[0:P], AX, ALU.min)

            @block.scalar
            def _(act):
                act.wait_ge(centred, 1)
                nc.scalar.activation(L, L, ACT.Exp).then_inc(powers, 1)

        with ExitStack() as sub:
            sb1, ps1, sem1 = bufs(nc, sub, "f3s")
            hot = sb1("hot", [128, NE, T])
            counting_sort(nc, g, "f3c", best, P, NE, T, pos, hot, base=0)
            placed = sem1("placed")
            scattered, done = g.moved[0], g.count(0, 16 * T)
            block = sub.enter_context(stage(nc, g))

            @block.vector
            def _(dve):
                nc.vector.tensor_scalar(kept[0:P], pos[0:P], float(C), None, ALU.is_lt)
                nc.vector.tensor_scalar(pos[0:P], pos[0:P], float(C - 1), None, ALU.min)
                nc.vector.tensor_scalar(away[0:P], g.iota[0:P, 0:T], float(NE * CS * 128), None, ALU.add)
                nc.vector.tensor_scalar(low[0:P, 0, 0:1], g.iota_p[0:P, :], float(T), None, ALU.mult)
                dve.drain()
                nc.vector.scalar_tensor_tensor(out=slot[0:P], in0=best[0:P], scalar=float(CS * 128), in1=pos[0:P],
                                               op0=ALU.mult, op1=ALU.add)
                nc.vector.tensor_scalar(away[0:P], away[0:P], low[0:P, 0, 0:1], None, ALU.add)
                nc.vector.tensor_tensor(total[0:P], total[0:P], kept[0:P], ALU.mult)
                dve.drain()
                nc.vector.tensor_copy(back[0:P], slot[0:P])
                nc.vector.tensor_tensor(pos[0:P], slot[0:P], away[0:P], ALU.subtract)
                dve.drain()
                nc.vector.tensor_tensor(pos[0:P], pos[0:P], kept[0:P], ALU.mult)
                dve.drain()
                nc.vector.tensor_tensor(to[0:P], pos[0:P], away[0:P], ALU.add).then_inc(placed, 1)

            @block.gpsimd
            def _(pool):
                pool.wait_ge(placed, 1)
                for t in range(T):
                    pool.indirect_dma_start(out=g.bins[:, :],
                                            out_offset=bass.IndirectOffsetOnAxis(ap=to[0:P, t:t + 1], axis=0),
                                            in_=g.XN[0:P, t, :], in_offset=None).then_inc(scattered, 16)
                pool.wait_ge(scattered, done)

        with ExitStack() as sub:
            sb1, ps1, sem1 = bufs(nc, sub, "f3e")
            w1, w2 = sb1("w1", [128, 2, K2, F]), sb1("w2", [128, 2, KF, D])
            b1, b2 = sb1("b1", [128, NE, KF]), sb1("b2", [128, 2, D])
            xs, xT = sb1("xs", [128, 2, CS, D]), sb1("xT", [128, K2, CS * 128])
            hT, ys = sb1("hT", [128, KF, CS * 128]), sb1("ys", [128, 2, CS, D])
            pT, pH, pY = (ps1(m, [128, 2, 512]) for m in ("pT", "pH", "pY"))
            b_loaded = sem1("b_loaded")
            loaded, stored = [sem1(f"loaded{j}") for j in range(2)], [sem1(f"stored{j}") for j in range(2)]
            x_turned, x_read, h_made, h_read, y_made, y_put, used = (
                sem1(m) for m in ("x_turned", "x_read", "h_made", "h_read", "y_made", "y_put", "used"))
            bins = g.bins[0:NE * CS * 128, :].rearrange("(e s p) d -> e p s d", p=128, s=CS)
            results = g.results[0:NE * CS * 128, :].rearrange("(e s p) d -> e p s d", p=128, s=CS)
            block = sub.enter_context(stage(nc, g))

            @block.sync
            def _(sp):
                with nc.allow_non_contiguous_dma("the biases, once"):
                    for e in range(NE):
                        sp.dma_start(b1[:, e, :], a["L3_ffn_b1"][e].rearrange("(k p) -> p k", p=128)).then_inc(b_loaded, 16)
                sp.sem_inc(used, 2)
                with sp.Fori(0, NE // 2) as i:
                    for j in range(2):
                        ex = bass.ds(2 * i + j, 1)
                        sp.wait_ge(used, 2 * i + j + 1)
                        sp.dma_start(xs[:, j, :, :], bins[ex].rearrange("a p s d -> p (a s) d")).then_inc(loaded[j], 16)
                        sp.dma_start(w1[:, j, :, :], a["L3_ffn_w1"][ex].rearrange("a (k p) n -> p (a k) n", p=128)).then_inc(loaded[j], 16)
                        sp.dma_start(w2[:, j, :, :], a["L3_ffn_w2"][ex].rearrange("a (k p) n -> p (a k) n", p=128)).then_inc(loaded[j], 16)
                        sp.dma_start(b2[:, j, :], a["L3_ffn_b2"][ex, :].rearrange("a n -> (a n)").partition_broadcast(128)).then_inc(loaded[j], 16)

            @block.tensor
            def _(pe):
                with pe.Fori(0, NE // 2) as i:
                    for j in range(2):
                        n = 2 * i + j
                        pe.wait_ge(loaded[j], (i + 1) * 64)
                        for k in range(K2):
                            for s in range(CS):
                                last = nc.tensor.transpose(pT[:, k, s * 128:(s + 1) * 128], xs[:, j, s, k * 128:(k + 1) * 128], g.ident[:, :])
                            last.then_inc(x_turned, 1)
                        pe.wait_ge(x_read, 2 * n + 2)
                        for f in range(KF):
                            pe.wait_ge(h_read, n * KF + f + 1)
                            for k in range(K2):
                                last = nc.tensor.matmul(pH[:, f % 2, :], w1[:, j, k, f * 128:(f + 1) * 128], xT[:, k, :],
                                                        start=(k == 0), stop=(k == K2 - 1))
                            last.then_inc(h_made, 1)
                        pe.wait_ge(h_read, (n + 1) * KF + 2)
                        for s in range(CS):
                            pe.wait_ge(y_put, n * CS + s + 1)
                            for f in range(KF):
                                last = nc.tensor.matmul(pY[:, s % 2, 0:D], hT[:, f, s * 128:(s + 1) * 128], w2[:, j, f, :],
                                                        start=(f == 0), stop=(f == KF - 1))
                            last.then_inc(y_made, 1)

            @block.scalar
            def _(act):
                act.wait_ge(b_loaded, 16 * NE)
                act.sem_inc(h_read, 2)
                with act.Fori(0, NE // 2) as i:
                    for j in range(2):
                        n = 2 * i + j
                        for k in range(K2):
                            act.wait_ge(x_turned, 2 * n + k + 1)
                            nc.scalar.copy(xT[:, k, :], pT[:, k, :]).then_inc(x_read, 1)
                        for f in range(KF):
                            act.wait_ge(h_made, n * KF + f + 1)
                            nc.scalar.activation(hT[:, f, :], pH[:, f % 2, :], ACT.Relu,
                                                 bias=row(b1, n, f, f + 1, p=128)).then_inc(h_read, 1)
                        act.wait_ge(y_put, (n + 1) * CS + 2)
                        act.dma_start(results[bass.ds(n, 1)].rearrange("a p s d -> p (a s) d"), ys[:, j, :, :]).then_inc(stored[j], 16)
                for j in range(2):
                    act.wait_ge(stored[j], 16 * (NE // 2 + 1))

            @block.vector
            def _(dve):
                dve.sem_inc(y_put, 2)
                for j in range(2):
                    dve.sem_inc(stored[j], 16)
                with dve.Fori(0, NE // 2) as i:
                    for j in range(2):
                        n = 2 * i + j
                        dve.wait_ge(stored[j], (i + 1) * 16)
                        for s in range(CS):
                            dve.wait_ge(y_made, n * CS + s + 1)
                            nc.vector.tensor_tensor(ys[:, j, s, :], pY[:, s % 2, 0:D], b2[:, j, :], ALU.add).then_inc(y_put, 1)
                        dve.drain().then_inc(used, 1)

        with ExitStack() as sub:
            sb1, ps1, sem1 = bufs(nc, sub, "f3y")
            Y, flag, const = sb1("Y", [128, T, D]), sb1("flag", [128, T, D], I32), sb1("const", [128, 3])
            gathered, done = g.moved[0], g.count(0, 16 * T)
            block = sub.enter_context(stage(nc, g))

            @block.gpsimd
            def _(pool):
                for t in range(T):
                    pool.indirect_dma_start(out=Y[0:P, t, :], out_offset=None, in_=g.results[:, :],
                                            in_offset=bass.IndirectOffsetOnAxis(ap=back[0:P, t:t + 1], axis=0)
                                            ).then_inc(gathered, 16)

            @block.vector
            def _(dve):
                for k, value in enumerate((0.0, 1e4, -1e4)):
                    nc.vector.memset(const[:, k:k + 1], value)
                dve.wait_ge(gathered, done)
                nc.vector.tensor_tensor(Y[0:P], Y[0:P], deep(total[0:P], P, T, D), ALU.mult)
                dve.drain()
                largest = 3.4028234663852886e38
                nc.vector.tensor_tensor(flag[0:P], Y[0:P], Y[0:P], ALU.not_equal)
                dve.drain()
                for k in range(3):
                    if k:
                        nc.vector.tensor_scalar(flag[0:P], Y[0:P], largest if k == 1 else -largest, None,
                                                ALU.is_gt if k == 1 else ALU.is_lt)
                        dve.drain()
                    nc.vector.copy_predicated(Y[0:P], flag[0:P], const[0:P, k:k + 1].rearrange("p (a b) -> p a b", a=1).broadcast_to([P, T, D]))
                    dve.drain()
                nc.vector.tensor_tensor(g.X[0:P], g.X[0:P], Y[0:P], ALU.add)



def build(nc, a, out, stop=99):
    with ExitStack() as ctx:
        def sb(name, shape, dt=F32):
            return ctx.enter_context(nc.sbuf_tensor(name, shape, dt))

        def dram(name, shape, dt=F32):
            return nc.dram_tensor(name, shape, dt, kind="Internal").ap()

        g = Shared()
        g.X = sb("X", [128, T, D])
        g.XN = sb("XN", [128, T, D])
        g.ident = sb("ident", [128, 128])
        g.tri = sb("tri", [128, 128])
        g.iota = sb("iota", [128, ST])
        g.iota_p = sb("iota_p", [128, 1])
        g.ones = sb("ones", [128, ST])
        g.zeros = sb("zeros", [128, 264])
        g.slots = sb("slots", [128, ST + R // 2, 4])
        g.kmap = sb("kmap", [1, ST], I32)
        g.dinv1 = sb("dinv1", [128, T])
        g.dinv2 = sb("dinv2", [128, T])
        g.slots_dram = dram("slots_dram", (128 * (ST + ET - EC), 4))
        g.table260 = dram("table260", (N, D + 4))
        g.table4 = dram("table4", (N, 4))
        g.table64 = dram("table64", (N, 64))
        g.table128 = dram("table128", (N, 128))
        g.table256 = dram("table256", (N, D))
        g.relations = dram("relations", (8 * N, D))
        g.bins = dram("bins", (8192, D))
        g.results = dram("results", (8192, D))
        g.moved = [ctx.enter_context(nc.semaphore(f"moved{j}")) for j in range(R)]
        sent = [0] * R

        def count(j, n):
            sent[j] += n
            return sent[j]

        g.count = count
        g.block, g.phase = None, 0
        g.phase_done = ctx.enter_context(nc.semaphore("phase_done"))
        constants(nc, g, a["x"])
        layers = [layer0_gnn]
        if stop >= 2:
            layers.append(layer0_ffn)
        if stop >= 3:
            prepare_graph(nc, g, a["src"], a["dst"], a["edge_type_8"], a["edge_weight"])
            clear_semaphores(nc)
            layers += [layer1_gnn, layer1_ffn, layer2_gnn, layer2_ffn, layer3_gnn, layer3_ffn]
        for layer in layers[:stop]:
            layer(nc, g, a)
            clear_semaphores(nc)
        store(nc, g, "out", out, g.X, D)


TURNED = ("L0_ffn_W_x", "L2_gnn_W6", "L2_gnn_W7", "L2_gnn_Wp", "L3_gnn_weight")
STOP = 99

def kernel(**inputs):
    import numpy as np
    import concourse.bacc as bacc
    from concourse.bass_utils import run_bass_kernel_spmd as run

    nc = bacc.Bacc("TRN2", target_bir_lowering=False, num_devices=1)
    arrays, args = {}, {}
    for name, value in inputs.items():
        v = np.ascontiguousarray(value)
        if name in TURNED:
            v = np.ascontiguousarray(np.swapaxes(v, -1, -2))
        arrays[f"in_{name}"] = v
        args[name] = nc.dram_tensor(f"in_{name}", v.shape, mybir.dt.from_np(v.dtype), kind="ExternalInput").ap()
    out = nc.dram_tensor("out_x", (N, D), F32, kind="ExternalOutput").ap()
    build(nc, args, out, STOP)
    return run(nc, [arrays], core_ids=[0]).results[0]["out_x"]
```

```python
from contextlib import ExitStack, contextmanager

import concourse.bass as bass
from concourse import mybir

F32 = mybir.dt.float32
I32 = mybir.dt.int32
ALU = mybir.AluOpType
ACT = mybir.ActivationFunctionType
AX = mybir.AxisListType.X

N = 3125
T = 25
P = N // T
D = 256
K2 = D // 128
E = 50000
EC = E // 128
EREST = E - 128 * EC
U = 8
ET = -(-(EC + 1) // U) * U
R = 16
ST = -(-((E + T * 127) // 128) // R) * R
G = 5
EPS = 1e-5
ROUND = 12582912.0
BIG = 1e30


class Shared:
    pass


def row(a, i, lo=None, hi=None, p=P):
    lo, hi = lo or 0, hi if hi is not None else a.shape[2]
    return a[0:p, bass.ds(i, 1), lo:hi].rearrange("p a d -> p (a d)")


def wide(a, p, k, n):
    return a.rearrange("p (a n) -> p a n", a=1).broadcast_to([p, k, n])


def deep(a, p, k, n):
    return a.rearrange("p (k a) -> p k a", a=1).broadcast_to([p, k, n])


def hold(eng, sem, value, turn):
    eng.wait_ge(sem, value)
    eng.sem_inc(turn, 1)


def load_keys(nc, engine, kmap, at, n, keys):
    _, values = nc.values_load_multi_w_load_instructions(
        kmap[0:1, bass.ds(at, n)], engines=(engine,), min_val=0, max_val=keys - 1,
        skip_runtime_bounds_check_because="counting_sort makes keys of 0..keys-1")
    return values


@contextmanager
def stage(nc, g):
    if g.block is None:
        with nc.Block() as block:
            yield block
        return
    yield g.block
    g.phase += 1
    everyone = 4 * g.phase

    def leave(eng):
        eng.drain().then_inc(g.phase_done, 1)
        eng.wait_ge(g.phase_done, everyone)

    for engine in (g.block.sync, g.block.scalar, g.block.tensor, g.block.vector):
        engine(leave)


def bufs(nc, ctx, tag):
    def sb(name, shape, dt=F32):
        return ctx.enter_context(nc.sbuf_tensor(f"{tag}_{name}", shape, dt))

    def ps(name, shape, dt=F32):
        return ctx.enter_context(nc.psum_tensor(f"{tag}_{name}", shape, dt))

    def sem(name):
        return ctx.enter_context(nc.semaphore(f"{tag}_{name}"))

    return sb, ps, sem



def constants(nc, g, x_dram):
    with ExitStack() as ctx:
        sb, ps, sem = bufs(nc, ctx, "const")
        loaded, filled, shaped = sem("loaded"), sem("filled"), sem("shaped")
        block = ctx.enter_context(stage(nc, g))

        @block.sync
        def _(sp):
            sp.dma_start(g.X[0:P], x_dram.rearrange("(p t) d -> p t d", p=P)).then_inc(loaded, 16)
            sp.wait_ge(loaded, 16)

        @block.gpsimd
        def _(pool):
            pool.memset(g.ident[:, :], 0.0).then_inc(filled, 1)
            pool.memset(g.tri[:, :], 1.0).then_inc(filled, 1)
            pool.iota(g.iota[:, :], pattern=[[1, ST]], base=0, channel_multiplier=0,
                      allow_small_or_imprecise_dtypes=True)
            pool.iota(g.iota_p[:, :], pattern=[[1, 1]], base=0, channel_multiplier=1,
                      allow_small_or_imprecise_dtypes=True)
            pool.wait_ge(filled, 2)
            pool.affine_select(out=g.ident[:, :], in_=g.ident[:, :], compare_op=ALU.not_equal, fill=1.0,
                               base=0, pattern=[[-1, 128]], channel_multiplier=1).then_inc(shaped, 1)
            pool.affine_select(out=g.tri[:, :], in_=g.tri[:, :], compare_op=ALU.is_gt, fill=0.0,
                               base=0, pattern=[[1, 128]], channel_multiplier=-1).then_inc(shaped, 1)
            pool.wait_ge(shaped, 2)

        @block.vector
        def _(dve):
            nc.vector.memset(g.ones[:, :], 1.0)
            nc.vector.memset(g.zeros[:, :], 0.0)


def clear_semaphores(nc):
    free = sorted(nc.free_semaphores)
    with nc.Block() as block:
        @block.gpsimd
        def _(pool):
            pool.sem_clear(range(free[0], free[-1] + 1))



def layer_norm(nc, g, tag, src, dst):
    with ExitStack() as ctx:
        sb, ps, sem = bufs(nc, ctx, tag)
        st = sb("st", [128, T, 6])
        mean, spread, var, std, rstd = (sb(n, [128, T]) for n in ("mean", "spread", "var", "std", "rstd"))
        var_ready, std_ready = sem("var_ready"), sem("std_ready")
        shift, shift_ready = sb("shift", [128, T]), sem("shift_ready")
        block = ctx.enter_context(stage(nc, g))

        @block.vector
        def _(dve):
            for t in range(T):
                nc.vector.bn_stats(st[0:P, t, :], src[0:P, t, :])
            dve.drain()
            nc.vector.tensor_tensor(mean[0:P], st[0:P, :, 1], st[0:P, :, 4], ALU.add)
            nc.vector.tensor_tensor(spread[0:P], st[0:P, :, 1], st[0:P, :, 4], ALU.subtract)
            nc.vector.tensor_tensor(var[0:P], st[0:P, :, 2], st[0:P, :, 5], ALU.add)
            dve.drain()
            nc.vector.tensor_scalar(mean[0:P], mean[0:P], 0.5, None, ALU.mult)
            nc.vector.tensor_tensor(spread[0:P], spread[0:P], spread[0:P], ALU.mult)
            nc.vector.tensor_scalar(var[0:P], var[0:P], 1.0 / D, EPS, ALU.mult, ALU.add)
            dve.drain()
            nc.vector.scalar_tensor_tensor(out=var[0:P], in0=spread[0:P], scalar=0.25, in1=var[0:P],
                                           op0=ALU.mult, op1=ALU.add).then_inc(var_ready, 1)
            dve.wait_ge(std_ready, 1)
            nc.vector.reciprocal(rstd[0:P], std[0:P])
            dve.drain()
            nc.vector.scalar_tensor_tensor(out=shift[0:P], in0=mean[0:P], scalar=-1.0, in1=rstd[0:P],
                                           op0=ALU.mult, op1=ALU.mult).then_inc(shift_ready, 1)
            for t in range(T // 2 + 1):
                nc.vector.tensor_scalar(dst[0:P, t, :], src[0:P, t, :], mean[0:P, t:t + 1],
                                        rstd[0:P, t:t + 1], ALU.subtract, ALU.mult)

        @block.scalar
        def _(act):
            act.wait_ge(var_ready, 1)
            nc.scalar.activation(std[0:P], var[0:P], ACT.Sqrt).then_inc(std_ready, 1)
            act.wait_ge(shift_ready, 1)
            for t in range(T // 2 + 1, T):
                nc.scalar.activation(dst[0:P, t, :], src[0:P, t, :], ACT.Identity, bias=shift[0:P, t:t + 1],
                                     scale=rstd[0:P, t:t + 1])



def linear(nc, g, tag, src, width, w_dram, bias_dram, nout, finish, prepare=None, turn=None, table=None):
    kc = [min(128, width - k) for k in range(0, width, 128)]
    nk, rows = len(kc), kc[0]
    SKEW, BANKS, PLACES = 2, 3, 4
    with ExitStack() as ctx:
        sb, ps, sem = bufs(nc, ctx, tag)
        in_sbuf = w_dram.shape[0] == 128 and len(w_dram.shape) == 3
        w = w_dram if in_sbuf else sb("w", [128, nk, nout])
        bias = sb("bias", [128, nout]) if bias_dram is not None else None
        function, scale_dram, shift_dram = turn or (ACT.Copy, None, None)
        columns = sb("columns", [128, 2, nk]) if turn else None
        xT = sb("xT", [128, PLACES, nk, P])
        psT = ps("psT", [128, BANKS, 512])
        psO = ps("psO", [128, BANKS, 512])
        w_loaded, b_loaded, c_loaded, prepared = (sem(m) for m in ("w_loaded", "b_loaded", "c_loaded", "prepared"))
        turned, turn_read, multiplied, put_away = (sem(m) for m in ("turned", "turn_read", "multiplied", "put_away"))
        stored = sem("stored")
        block = ctx.enter_context(stage(nc, g))

        @block.sync
        def _(sp):
            column_loads = 0
            with nc.allow_non_contiguous_dma("a few hundred values"):
                for k, dram in enumerate((scale_dram, shift_dram)):
                    if dram is not None:
                        sp.dma_start(columns[0:rows, k, :], dram.rearrange("(k p) -> p k", p=rows)).then_inc(c_loaded, 16)
                        column_loads += 1
            if not in_sbuf:
                sp.dma_start(w[0:rows], w_dram.rearrange("(k p) n -> p k n", p=rows)).then_inc(w_loaded, 16)
            if bias is not None:
                sp.dma_start(bias[:, :], bias_dram.partition_broadcast(128)).then_inc(b_loaded, 16)
            if table is not None:
                out = table[0].rearrange("(p t) d -> p t d", p=P)
                for t in range(0, T, G):
                    sp.wait_ge(put_away, t + G)
                    sp.dma_start(out[:, t:t + G, :], table[1][0:P, t:t + G, 0:nout]).then_inc(stored, 16)
                sp.wait_ge(stored, 16 * (T // G))
            for loads, loaded in ((column_loads, c_loaded), (not in_sbuf, w_loaded), (bias is not None, b_loaded)):
                if loads:
                    sp.wait_ge(loaded, 16 * loads)

        @block.tensor
        def _(pe):
            if prepare is not None:
                pe.wait_ge(prepared, 1)
            for t in range(T + SKEW):
                if t < T:
                    if t >= BANKS:
                        pe.wait_ge(turn_read, t - BANKS + 1)
                    for k in range(nk):
                        last = nc.tensor.transpose(psT[0:kc[k], t % BANKS, k * P:(k + 1) * P],
                                                   src[0:P, t, k * 128:k * 128 + kc[k]], g.ident[0:P, 0:P])
                    last.then_inc(turned, 1)
                m = t - SKEW
                if m >= 0:
                    if m == 0 and not in_sbuf:
                        pe.wait_ge(w_loaded, 16)
                    pe.wait_ge(turn_read, m + 1)
                    if m >= BANKS:
                        pe.wait_ge(put_away, m - BANKS + 1)
                    for k in range(nk):
                        last = nc.tensor.matmul(psO[0:P, m % BANKS, 0:nout], xT[0:kc[k], m % PLACES, k, :],
                                                w[0:kc[k], k, :], start=(k == 0), stop=(k == nk - 1))
                    last.then_inc(multiplied, 1)

        @block.scalar
        def _(act):
            if turn:
                act.wait_ge(c_loaded, 16 * ((scale_dram is not None) + (shift_dram is not None)))
            for t in range(T):
                act.wait_ge(turned, t + 1)
                if t >= PLACES:
                    act.wait_ge(multiplied, t - PLACES + 1)
                if turn:
                    for k in range(nk):
                        last = nc.scalar.activation(xT[0:rows, t % PLACES, k, :], psT[0:rows, t % BANKS, k * P:(k + 1) * P], function,
                                                    bias=columns[0:rows, 1, k:k + 1],
                                                    scale=columns[0:rows, 0, k:k + 1] if scale_dram is not None else 1.0)
                else:
                    last = nc.scalar.copy(xT[0:rows, t % PLACES, :, :], psT[0:rows, t % BANKS, 0:nk * P].rearrange(
                        "p (k r) -> p k r", k=nk))
                last.then_inc(turn_read, 1)

        @block.vector
        def _(dve):
            if prepare is not None:
                prepare(dve)
                dve.drain().then_inc(prepared, 1)
            if bias is not None:
                dve.wait_ge(b_loaded, 16)
            for t in range(T):
                dve.wait_ge(multiplied, t + 1)
                finish(dve, t, psO[0:P, t % BANKS, 0:nout], bias).then_inc(put_away, 1)



def counting_sort(nc, g, tag, key, p, keys, n, pos, hot, base=None, kmap=None, slots=0, tiles=None):
    with ExitStack() as ctx:
        sb, ps, sem = bufs(nc, ctx, tag)
        seen = sb("seen", [128, keys, n])
        total = sb("total", [128, keys])
        nt, ends, starts, off = (sb(m, [128, keys]) for m in ("nt", "ends", "starts", "off"))
        pE, pC = ps("pE", [128, 512]), ps("pC", [128, 512])
        counted, summed = sem("counted"), sem("summed")
        block = ctx.enter_context(stage(nc, g))

        @block.vector
        def _(dve):
            nc.vector.tensor_tensor(hot[0:p], wide(key[0:p, 0:n], p, keys, n),
                                    deep(g.iota[0:p, 0:keys], p, keys, n), ALU.is_equal)
            dve.drain()
            with dve.Fori(0, keys) as k:
                nc.vector.tensor_tensor_scan(row(seen, k, p=p), g.ones[0:p, 0:n], row(hot, k, 0, n, p=p), 0.0,
                                             ALU.mult, ALU.add)
            dve.drain()
            nc.vector.tensor_copy(total[0:p], seen[0:p, :, n - 1]).then_inc(counted, 1)
            dve.wait_ge(summed, 1)
            nc.vector.tensor_scalar(off[0:p], pE[0:p, 0:keys], -1.0, None, ALU.add)
            if base is None:
                nc.vector.tensor_scalar(nt[0:p], pC[0:p, 0:keys], 1.0 / 128, 63.5 / 128, ALU.mult, ALU.add)
                dve.drain()
                nc.vector.tensor_scalar(nt[0:p], nt[0:p], ROUND, None, ALU.add)
                dve.drain()
                nc.vector.tensor_scalar(nt[0:p], nt[0:p], -ROUND, None, ALU.add)
                dve.drain()
                nc.vector.tensor_tensor_scan(ends[0:p], g.ones[0:p, 0:keys], nt[0:p], 0.0, ALU.mult, ALU.add)
                nc.vector.memset(tiles[0:1, :], -1.0)
                dve.drain()
                nc.vector.tensor_tensor(starts[0:p], ends[0:p], nt[0:p], ALU.subtract)
                dve.drain()
                nc.vector.scalar_tensor_tensor(out=off[0:p], in0=starts[0:p], scalar=128.0, in1=off[0:p],
                                               op0=ALU.mult, op1=ALU.add)
                with dve.Fori(0, keys) as k:
                    nc.vector.scalar_tensor_tensor(out=tiles[0:1, :], in0=g.iota[0:1, 0:slots],
                                                   scalar=starts[0:1, bass.ds(k, 1)], in1=tiles[0:1, :],
                                                   op0=ALU.is_ge, op1=ALU.add)
                    dve.drain()
                nc.vector.tensor_copy(kmap[0:1, 0:slots], tiles[0:1, :])
            dve.drain()
            nc.vector.tensor_tensor(seen[0:p], seen[0:p], deep(off[0:p], p, keys, n), ALU.add)
            dve.drain()
            nc.vector.tensor_tensor(seen[0:p], seen[0:p], hot[0:p], ALU.mult)
            dve.drain()
            nc.vector.tensor_reduce(pos[0:p, 0:n], seen[0:p].rearrange("p k n -> p n k"), AX, ALU.add)

        @block.tensor
        def _(pe):
            pe.wait_ge(counted, 1)
            nc.tensor.matmul(pE[0:p, 0:keys], g.tri[0:p, 0:p], total[0:p], start=True, stop=True)
            nc.tensor.matmul(pC[0:p, 0:keys], g.ones[0:p, 0:p], total[0:p], start=True,
                             stop=True).then_inc(summed, 1)



def scatter_edges(nc, g, first, last):
    @g.block.gpsimd
    def _(pool):
        for c in range(first, last):
            pool.indirect_dma_start(out=g.slots_dram[:, :],
                                    out_offset=bass.IndirectOffsetOnAxis(ap=g.rec_row[:, c:c + 1], axis=0),
                                    in_=g.rec[:, c, :], in_offset=None).then_inc(g.moved[1], 16)
        if last == ET:
            pool.wait_ge(g.moved[1], g.count(1, 16 * ET))


def load_slots(nc, g):
    with ExitStack() as ctx:
        slots_back = ctx.enter_context(nc.semaphore("slots_back"))
        block = ctx.enter_context(stage(nc, g))

        @block.sync
        def _(sp):
            sp.dma_start(g.slots[:, 0:ST, :], g.slots_dram[0:128 * ST, :].rearrange(
                "(p t) f -> p t f", p=128)).then_inc(slots_back, 16)
            sp.wait_ge(slots_back, 16)


def prepare_graph(nc, g, src, dst, etype, eweight):
    with ExitStack() as ctx:
        sb, ps, sem = bufs(nc, ctx, "edges")
        raw = sb("raw", [128, 3, ET], I32)
        rec = g.rec
        hot = sb("hot", [128, 2, T, ET])
        key, pos, pad, tmp = (sb(m, [128, ET]) for m in ("key", "pos", "pad", "tmp"))
        tiles = sb("tiles", [128, ST])
        padrow = sb("padrow", [128, 1])
        cleared, loaded, blank, filled = sem("cleared"), sem("loaded"), sem("blank"), sem("filled")

        with stage(nc, g) as block:
            @block.vector
            def _(dve):
                nc.vector.memset(raw[:, :, :], 0).then_inc(cleared, 1)
                nc.vector.memset(rec[:, :, :], 0.0).then_inc(cleared, 1)
                nc.vector.memset(g.slots[:, :, :], 0.0)
                dve.drain()
                nc.vector.memset(g.slots[:, :, 1], -1.0).then_inc(blank, 1)
                nc.vector.memset(pad[:, :], 0.0)
                dve.drain()
                nc.vector.memset(pad[:, EC + 1:ET], 1.0)
                nc.vector.tensor_scalar(pad[:, EC:EC + 1], g.iota_p[:, :], float(EREST), None, ALU.is_ge)

            @block.sync
            def _(sp):
                sp.wait_ge(cleared, 2)
                for k, a in enumerate((src, dst, etype)):
                    sp.dma_start(raw[:, k, 0:EC], a[0:128 * EC].rearrange("(p t) -> p t", p=128)).then_inc(loaded, 16)
                    sp.dma_start(raw[0:EREST, k, EC:EC + 1],
                                 a[128 * EC:E].rearrange("(p t) -> p t", t=1)).then_inc(loaded, 16)
                sp.dma_start(tmp[:, 0:EC], eweight[0:128 * EC].rearrange("(p t) -> p t", p=128)).then_inc(loaded, 16)
                sp.dma_start(rec[0:EREST, EC, 2:3], eweight[128 * EC:E].rearrange("(p t) -> p t", t=1)).then_inc(loaded, 16)
                sp.wait_ge(blank, 1)
                sp.dma_start(g.slots_dram[0:128 * ST, :].rearrange("(p t) f -> p t f", p=128),
                             g.slots[:, 0:ST, :]).then_inc(filled, 16)
                sp.wait_ge(loaded, 128)
                sp.wait_ge(filled, 16)
                sp.dma_start(g.bins.rearrange("(p r) d -> p r d", p=128),
                             wide(g.zeros[:, 0:D], 128, g.bins.shape[0] // 128, D)).then_inc(g.cleared, 16)

        with stage(nc, g) as block:
            @block.vector
            def _(dve):
                nc.vector.tensor_copy(rec[:, 0:EC, 2], tmp[:, 0:EC])
                nc.vector.tensor_copy(rec[:, :, 0], raw[:, 0, :])
                nc.vector.tensor_copy(key[:, :], raw[:, 1, :])
                nc.vector.tensor_copy(rec[:, :, 3], raw[:, 2, :])
                dve.drain()
                nc.vector.scalar_tensor_tensor(out=rec[:, :, 3], in0=rec[:, :, 3], scalar=float(N),
                                               in1=rec[:, :, 0], op0=ALU.mult, op1=ALU.add)
                nc.vector.tensor_scalar(tmp[:, :], key[:, :], 1.0 / T, -(T // 2) / T, ALU.mult, ALU.add)
                dve.drain()
                nc.vector.tensor_scalar(tmp[:, :], tmp[:, :], ROUND, None, ALU.add)
                dve.drain()
                nc.vector.tensor_scalar(rec[:, :, 1], tmp[:, :], -ROUND, None, ALU.add)
                dve.drain()
                nc.vector.scalar_tensor_tensor(out=key[:, :], in0=rec[:, :, 1], scalar=-float(T),
                                               in1=key[:, :], op0=ALU.mult, op1=ALU.add)
                nc.vector.tensor_scalar(padrow[:, :], g.iota_p[:, :], float(128 * ST), None, ALU.add)
                dve.drain()
                nc.vector.scalar_tensor_tensor(out=key[:, :], in0=pad[:, :], scalar=100.0, in1=key[:, :],
                                               op0=ALU.mult, op1=ALU.add)

        counting_sort(nc, g, "sort", key, 128, T, ET, pos, hot[:, 0], kmap=g.kmap, slots=ST, tiles=tiles)

        ohl = sb("ohl", [128, 2, U, P])
        hots = sb("hots", [128, 2, U, 2 * T])
        pdeg = ps("pdeg", [128, 512])
        weighted, hot_ready, hot_used, opened = sem("weighted"), sem("hot_ready"), sem("hot_used"), sem("opened")
        tiles_ready = sem("tiles_ready")
        with stage(nc, g) as block:
            @block.vector
            def _(dve):
                nc.vector.tensor_scalar(tmp[:, :], pos[:, :], 1.0 / 128, -63.5 / 128, ALU.mult, ALU.add)
                dve.drain()
                nc.vector.tensor_scalar(tmp[:, :], tmp[:, :], ROUND, None, ALU.add)
                dve.drain()
                nc.vector.tensor_scalar(tmp[:, :], tmp[:, :], -ROUND, None, ALU.add)
                dve.drain()
                nc.vector.scalar_tensor_tensor(out=pos[:, :], in0=tmp[:, :], scalar=-128.0, in1=pos[:, :],
                                               op0=ALU.mult, op1=ALU.add)
                dve.drain()
                nc.vector.scalar_tensor_tensor(out=pos[:, :], in0=pos[:, :], scalar=float(ST), in1=tmp[:, :],
                                               op0=ALU.mult, op1=ALU.add)
                nc.vector.tensor_scalar(pad[:, :], pad[:, :], padrow[:, :], None, ALU.mult)
                dve.drain()
                for c in range(EC + 1, ET):
                    nc.vector.tensor_scalar(pad[:, c:c + 1], pad[:, c:c + 1], float(128 * (c - EC)), None, ALU.add)
                dve.drain()
                nc.vector.tensor_tensor(pos[:, :], pos[:, :], pad[:, :], ALU.add)
                dve.drain()
                nc.vector.tensor_copy(g.rec_row[:, :], pos[:, :])
                nc.vector.tensor_tensor(hot[:, 1], hot[:, 0], rec[:, :, 2:3].rearrange("p t a -> p a t").broadcast_to([128, T, ET]),
                                        ALU.mult).then_inc(weighted, 1)
                dve.sem_inc(hot_used, 2)
                iota = wide(g.iota[:, 0:P], 128, U, P)

                def one_hot(n, j):
                    dve.wait_ge(hot_used, n + 1)
                    nc.vector.tensor_tensor(ohl[:, j], iota, rec[:, bass.ds(n * U, U), 1:2].broadcast_to([128, U, P]),
                                            ALU.is_equal).then_inc(hot_ready, 1)

                one_hot(0, 0)
                with dve.Fori(0, ET // U // 2) as i:
                    one_hot(2 * i + 1, 1)
                    one_hot(2 * i + 2, 0)
                dve.wait_ge(opened, 1)
                nc.vector.tensor_scalar(g.dinv1[0:P], pdeg[0:P, 0:T], 1.0, 1e-12, ALU.add, ALU.max)
                nc.vector.tensor_scalar(g.dinv2[0:P], pdeg[0:P, T:2 * T], 1.0, None, ALU.add)

            @block.scalar
            def _(act):
                act.wait_ge(weighted, 1)

                def stage_tiles(n, j):
                    act.wait_ge(hot_used, n + 1)
                    nc.scalar.copy(hots[:, j].rearrange("p u (a k) -> p a k u", a=2),
                                   hot[:, :, :, bass.ds(n * U, U)]).then_inc(tiles_ready, 1)

                stage_tiles(0, 0)
                with act.Fori(0, ET // U // 2) as i:
                    stage_tiles(2 * i + 1, 1)
                    stage_tiles(2 * i + 2, 0)

            @block.tensor
            def _(pe):
                nc.tensor.matmul(pdeg[0:P, 0:2 * T], g.zeros[:, 0:P], g.zeros[:, 0:2 * T], start=True, stop=False)

                def add_edges(n, j):
                    pe.wait_ge(hot_ready, n + 1)
                    pe.wait_ge(tiles_ready, n + 1)
                    for u in range(U):
                        last = nc.tensor.matmul(pdeg[0:P, 0:2 * T], ohl[:, j, u, :],
                                                hots[:, j, u, :],
                                                start=False, stop=False, skip_group_check=True)
                    last.then_inc(hot_used, 1)

                add_edges(0, 0)
                with pe.Fori(0, ET // U // 2) as i:
                    add_edges(2 * i + 1, 1)
                    add_edges(2 * i + 2, 0)
                nc.tensor.matmul(pdeg[0:P, 0:2 * T], g.zeros[:, 0:P], g.zeros[:, 0:2 * T], start=False,
                                 stop=True).then_inc(opened, 1)

        positive, d1, d2 = sb("positive", [128, T]), sem("d1"), sem("d2")
        with stage(nc, g) as block:
            @block.vector
            def _(dve):
                nc.vector.tensor_scalar(positive[0:P], g.dinv2[0:P], 0.0, None, ALU.is_gt)
                dve.drain()
                nc.vector.tensor_tensor(g.dinv2[0:P], g.dinv2[0:P], positive[0:P], ALU.mult)
                dve.drain()
                nc.vector.scalar_tensor_tensor(out=g.dinv2[0:P], in0=g.dinv2[0:P], scalar=1.0, in1=positive[0:P],
                                               op0=ALU.add, op1=ALU.subtract).then_inc(d1, 1)
                dve.wait_ge(d2, 2)
                nc.vector.reciprocal(g.dinv1[0:P], g.dinv1[0:P])
                nc.vector.reciprocal(g.dinv2[0:P], g.dinv2[0:P])
                dve.drain()
                nc.vector.tensor_tensor(g.dinv2[0:P], g.dinv2[0:P], positive[0:P], ALU.mult)

            @block.scalar
            def _(act):
                act.wait_ge(d1, 1)
                nc.scalar.activation(g.dinv1[0:P], g.dinv1[0:P], ACT.Sqrt).then_inc(d2, 1)
                nc.scalar.activation(g.dinv2[0:P], g.dinv2[0:P], ACT.Sqrt).then_inc(d2, 1)


def aggregate(nc, g, tag, acc, table, width, weighted=False, field=0):
    AHEAD, BANKS = R // 2, 8
    with ExitStack() as ctx:
        sb, ps, sem = bufs(nc, ctx, tag)
        idx = sb("idx", [128, R], I32)
        got = sb("got", [128, R, width])
        hot = sb("hot", [128, R, P])
        pp = ps("pp", [128, BANKS, 512])
        staged, hot_ready, multiplied = sem("staged"), sem("hot_ready"), sem("multiplied")
        added, turn = sem("added"), sem("turn")
        gathered = g.moved
        before = [g.count(j, 16 * (ST // R)) - 16 * (ST // R) for j in range(R)]
        block = ctx.enter_context(stage(nc, g))

        @block.scalar
        def _(act):
            act.sem_inc(multiplied, R)
            with act.Fori(0, ST // R) as i:
                for j in range(R):
                    act.wait_ge(multiplied, i * R + j + 1)
                    nc.scalar.copy(idx[:, j:j + 1], row(g.slots, i * R + j, field, field + 1, p=128)).then_inc(staged, 1)

        @block.gpsimd
        def _(pool):
            with pool.Fori(0, ST // R) as i:
                for j in range(R):
                    hold(pool, staged, i * R + j + 1, turn)
                    pool.indirect_dma_start(out=got[:, j, :], out_offset=None, in_=table[:, :],
                                            in_offset=bass.IndirectOffsetOnAxis(ap=idx[:, j:j + 1], axis=0)
                                            ).then_inc(gathered[j], 16)

        @block.tensor
        def _(pe):
            pe.sem_inc(added, BANKS)
            with pe.Fori(0, ST // R) as i:
                for j in range(R):
                    pe.wait_ge(gathered[j], (i + 1) * 16 + before[j])
                    pe.wait_ge(hot_ready, i * R + j + 1)
                    pe.wait_ge(added, i * R + j + 1)
                    nc.tensor.matmul(pp[0:P, j % BANKS, 0:width], hot[:, j, :], got[:, j, :], start=True,
                                     stop=True).then_inc(multiplied, 1)

        def one_hot(n, j):
            dst = row(g.slots, n, 1, 2, p=128)
            if weighted:
                ins = nc.vector.tensor_scalar(hot[:, j, :], g.iota[:, 0:P], dst, row(g.slots, n, 2, 3, p=128),
                                              ALU.is_equal, ALU.mult)
            else:
                ins = nc.vector.tensor_scalar(hot[:, j, :], g.iota[:, 0:P], dst, None, ALU.is_equal)
            ins.then_inc(hot_ready, 1)

        @block.vector
        def _(dve):
            for j in range(AHEAD):
                one_hot(j, j)
            with dve.Fori(0, ST // R) as i:
                for j in range(R):
                    if j % 4 == 0:
                        tile4 = load_keys(nc, mybir.EngineType.DVE, g.kmap, i * R + j, 4, T)
                    k = tile4[j % 4]
                    dve.drain()
                    dve.wait_ge(multiplied, i * R + j + 1 + R)
                    part = row(acc, k, 0, width)
                    nc.vector.tensor_tensor(part, part, pp[0:P, j % BANKS, 0:width], ALU.add).then_inc(added, 1)
                    one_hot(i * R + j + AHEAD, (j + AHEAD) % R)


def store(nc, g, tag, dram, src, width, done=None, value=16):
    with ExitStack() as ctx:
        stored = done or ctx.enter_context(nc.semaphore(f"{tag}_stored"))
        block = ctx.enter_context(stage(nc, g))

        @block.sync
        def _(sp):
            sp.dma_start(dram.rearrange("(p t) d -> p t d", p=P), src[0:P, :, 0:width]).then_inc(stored, 16)
            sp.wait_ge(stored, value)



def layer0_gnn(nc, g, a):
    layer_norm(nc, g, "l0n", g.X, g.XN)
    with ExitStack() as ctx:
        sb, ps, sem = bufs(nc, ctx, "l0g")
        XT = sb("XT", [128, T, D + 4])
        AL = sb("AL", [128, T, 4])
        prod = sb("prod", [128, T, D])
        att = sb("att", [128, 2, D])
        i_dst, i_src = sb("i_dst", [128, T], I32), sb("i_src", [128, T], I32)

        def put(dve, i, product, bias):
            return nc.vector.tensor_copy(row(XT, i, 0, D), product)

        linear(nc, g, "l0w", g.XN, D, a["L0_gnn_weight"], None, D, put)

        att_loaded = sem("att_loaded")
        with stage(nc, g) as block:
            @block.sync
            def _(sp):
                sp.dma_start(att[:, 0, :], a["L0_gnn_attn_l"].rearrange("h d -> (h d)").partition_broadcast(128)).then_inc(att_loaded, 16)
                sp.dma_start(att[:, 1, :], a["L0_gnn_attn_r"].rearrange("h d -> (h d)").partition_broadcast(128)).then_inc(att_loaded, 16)
                sp.dma_start(i_src[0:P], a["src"][0:N].rearrange("(p t) -> p t", p=P)).then_inc(att_loaded, 16)
                sp.dma_start(i_dst[0:P], a["dst"][0:N].rearrange("(p t) -> p t", p=P)).then_inc(att_loaded, 16)
                sp.wait_ge(att_loaded, 64)

            @block.vector
            def _(dve):
                dve.wait_ge(att_loaded, 64)
                for k, out in ((0, AL[0:P]), (1, XT[0:P, :, D:D + 4])):
                    nc.vector.tensor_tensor(prod[0:P], XT[0:P, :, 0:D], wide(att[0:P, k, :], P, T, D), ALU.mult)
                    dve.drain()
                    nc.vector.tensor_reduce(out, prod[0:P].rearrange("p t (h d) -> p t h d", h=4), AX, ALU.add)
                    dve.drain()

        store(nc, g, "l0s", g.table260, XT, D + 4, g.tables_stored, 16)
        store(nc, g, "l0s2", g.table4, AL, 4, g.tables_stored, 32)
        gathered = g.moved[0]
        done = g.count(0, 32 * T)
        with stage(nc, g) as block:
            @block.gpsimd
            def _(pool):
                pool.wait_ge(att_loaded, 64)
                pool.wait_ge(g.tables_stored, 32)
                for t in range(T):
                    pool.indirect_dma_start(out=XT[0:P, t, :], out_offset=None, in_=g.table260[:, :],
                                            in_offset=bass.IndirectOffsetOnAxis(ap=i_dst[0:P, t:t + 1], axis=0)
                                            ).then_inc(gathered, 16)
                    pool.indirect_dma_start(out=AL[0:P, t, :], out_offset=None, in_=g.table4[:, :],
                                            in_offset=bass.IndirectOffsetOnAxis(ap=i_src[0:P, t:t + 1], axis=0)
                                            ).then_inc(gathered, 16)
                pool.wait_ge(gathered, done)

        small = sb("small", [128, 3, T])
        raw = sb("raw", [128, T, 4])
        centred, powers = sem("centred"), sem("powers")
        with stage(nc, g) as block:
            @block.vector
            def _(dve):
                dve.wait_ge(gathered, done)
                nc.vector.tensor_tensor(raw[0:P], AL[0:P], XT[0:P, :, D:D + 4], ALU.add)
                dve.drain()
                nc.vector.tensor_scalar(AL[0:P], raw[0:P], 0.01, None, ALU.mult)
                dve.drain()
                nc.vector.tensor_tensor(AL[0:P], AL[0:P], raw[0:P], ALU.max)
                dve.drain()
                nc.vector.tensor_reduce(small[0:P, 0], AL[0:P], AX, ALU.max)
                dve.drain()
                nc.vector.tensor_tensor(AL[0:P], AL[0:P], deep(small[0:P, 0], P, T, 4), ALU.subtract).then_inc(centred, 1)
                dve.wait_ge(powers, 1)
                nc.vector.tensor_reduce(small[0:P, 1], AL[0:P], AX, ALU.add)
                dve.drain()
                nc.vector.reciprocal(small[0:P, 2], small[0:P, 1])
                dve.drain()
                nc.vector.tensor_tensor(AL[0:P], AL[0:P], deep(small[0:P, 2], P, T, 4), ALU.mult)
                dve.drain()
                nc.vector.tensor_tensor(prod[0:P].rearrange("p t (h d) -> p t h d", h=4),
                                        XT[0:P, :, 0:D].rearrange("p t (h d) -> p t h d", h=4),
                                        AL[0:P].rearrange("p t (h a) -> p t h a", a=1).broadcast_to([P, T, 4, 64]), ALU.mult)
                dve.drain()
                nc.vector.tensor_reduce(XT[0:P, :, 0:64], prod[0:P].rearrange("p t (h d) -> p t d h", h=4), AX, ALU.add)
                dve.drain()
                nc.vector.tensor_tensor(g.X[0:P].rearrange("p t (h d) -> p t h d", h=4),
                                        g.X[0:P].rearrange("p t (h d) -> p t h d", h=4),
                                        XT[0:P, :, 0:64].rearrange("p t (a d) -> p t a d", a=1).broadcast_to([P, T, 4, 64]), ALU.add)

            @block.scalar
            def _(act):
                act.wait_ge(centred, 1)
                nc.scalar.activation(AL[0:P], AL[0:P], ACT.Exp).then_inc(powers, 1)

HEADS, GROUPS = 8, 64
C4 = HEADS * GROUPS // 128


def layer0_ffn(nc, g, a):
    layer_norm(nc, g, "f0n", g.X, g.XN)
    with ExitStack() as ctx:
        sb, ps, sem = bufs(nc, ctx, "f0")
        SW = sb("SW", [128, T, HEADS * GROUPS])
        wxs = sb("wxs", [128, K2, HEADS * GROUPS])
        bxs = sb("bxs", [128, HEADS * GROUPS])
        M = sb("M", [128, C4, D])
        with ExitStack() as sub:
            sb1, ps1, sem1 = bufs(nc, sub, "f0a")
            wxT = sb1("wxT", [64, HEADS, D])
            wsl = sb1("wsl", [64, GROUPS])
            bx, bsl, temp = sb1("bx", [64, HEADS]), sb1("bsl", [128, GROUPS]), sb1("temp", [128, HEADS])
            bxw = sb1("bxw", [64, HEADS, 128])
            pw, pb = ps1("pw", [128, K2, 512]), ps1("pb", [128, 512])
            loaded, spread, made = sem1("loaded"), sem1("spread"), sem1("made")
            block = sub.enter_context(stage(nc, g))

            @block.sync
            def _(sp):
                sp.dma_start(wxT[:, :, :], a["L0_ffn_W_x"].rearrange("(h c) d -> c h d", c=64)).then_inc(loaded, 16)
                sp.dma_start(wsl[:, :], a["L0_ffn_W_slice"]).then_inc(loaded, 16)
                with nc.allow_non_contiguous_dma("a few hundred values"):
                    sp.dma_start(bx[:, :], a["L0_ffn_b_x"].rearrange("(h c) -> c h", c=64)).then_inc(loaded, 16)
                sp.dma_start(bsl[:, :], a["L0_ffn_b_slice"].partition_broadcast(128)).then_inc(loaded, 16)
                sp.dma_start(temp[:, :], a["L0_ffn_temperature"].rearrange("a h b c -> (a h b c)").partition_broadcast(128)).then_inc(loaded, 16)
                sp.wait_ge(loaded, 80)

            @block.vector
            def _(dve):
                dve.wait_ge(loaded, 80)
                nc.vector.tensor_copy(bxw[:, :, :], deep(bx[:, :], 64, HEADS, 128)).then_inc(spread, 1)
                nc.vector.tensor_scalar(temp[:, :], temp[:, :], 0.1, 5.0, ALU.max, ALU.min)
                dve.drain()
                nc.vector.reciprocal(temp[:, :], temp[:, :])
                dve.wait_ge(made, 1)
                dve.drain()
                scale = deep(temp[:, :], 128, HEADS, GROUPS)
                for k in range(K2):
                    nc.vector.tensor_tensor(wxs[:, k, :].rearrange("p (h s) -> p h s", h=HEADS),
                                            pw[:, k, :].rearrange("p (h s) -> p h s", h=HEADS), scale, ALU.mult)
                b3 = bxs[:, :].rearrange("p (h s) -> p h s", h=HEADS)
                nc.vector.tensor_tensor(b3, pb[:, :].rearrange("p (h s) -> p h s", h=HEADS),
                                        wide(bsl[:, :], 128, HEADS, GROUPS), ALU.add)
                dve.drain()
                nc.vector.tensor_tensor(b3, b3, scale, ALU.mult)

            @block.tensor
            def _(pe):
                pe.wait_ge(loaded, 80)
                pe.wait_ge(spread, 1)
                for h in range(HEADS):
                    cols = slice(h * GROUPS, (h + 1) * GROUPS)
                    for k in range(K2):
                        nc.tensor.matmul(pw[:, k, cols], wxT[:, h, k * 128:(k + 1) * 128], wsl[:, :],
                                         start=True, stop=True)
                    last = nc.tensor.matmul(pb[:, cols], bxw[:, h, :], wsl[:, :], start=True, stop=True)
                last.then_inc(made, 1)

        def put(dve, i, product, bias):
            return nc.vector.tensor_tensor(row(SW, i), product, bxs[0:P, :], ALU.add)

        linear(nc, g, "f0l", g.XN, D, wxs, None, HEADS * GROUPS, put)

        with ExitStack() as sub:
            sb1, ps1, sem1 = bufs(nc, sub, "f0s")
            top = sb1("top", [128, T * HEADS])
            centred, powers = sem1("centred"), sem1("powers")
            block = sub.enter_context(stage(nc, g))
            sw = SW[0:P].rearrange("p t (h s) -> p (t h) s", h=HEADS)

            @block.vector
            def _(dve):
                nc.vector.tensor_reduce(top[0:P], sw, AX, ALU.max)
                dve.drain()
                nc.vector.tensor_tensor(sw, sw, deep(top[0:P], P, T * HEADS, GROUPS), ALU.subtract).then_inc(centred, 1)
                dve.wait_ge(powers, 1)
                nc.vector.tensor_reduce(top[0:P], sw, AX, ALU.add)
                dve.drain()
                nc.vector.reciprocal(top[0:P], top[0:P])
                dve.drain()
                nc.vector.tensor_tensor(sw, sw, deep(top[0:P], P, T * HEADS, GROUPS), ALU.mult)

            @block.scalar
            def _(act):
                act.wait_ge(centred, 1)
                nc.scalar.activation(sw, sw, ACT.Exp).then_inc(powers, 1)

        with ExitStack() as sub:
            sb1, ps1, sem1 = bufs(nc, sub, "f0t")
            S = sb1("S", [128, C4, D + 1])
            with ExitStack() as inner:
                sb2, ps2, sem2 = bufs(nc, inner, "f0u")
                xs, xe = sb2("xs", [128, G, HEADS * GROUPS]), sb2("xe", [128, G, D + 1])
                pS = ps2("pS", [128, C4, 512])
                staged, staged_x, used, opened = (sem2(m) for m in ("staged", "staged_x", "used", "opened"))
                block = inner.enter_context(stage(nc, g))

                @block.scalar
                def _(act):
                    act.sem_inc(used, G)
                    with act.Fori(0, T // G) as i:
                        for j in range(G):
                            act.wait_ge(used, i * G + j + 1)
                            nc.scalar.copy(xs[0:P, j, :], row(SW, i * G + j)).then_inc(staged, 1)

                @block.tensor
                def _(pe):
                    for c in range(C4):
                        nc.tensor.matmul(pS[:, c, 0:D + 1], g.zeros[:, 0:128], g.zeros[:, 0:D + 1], start=True, stop=False)
                    with pe.Fori(0, T // G) as i:
                        for j in range(G):
                            pe.wait_ge(staged, i * G + j + 1)
                            pe.wait_ge(staged_x, i * G + j + 1)
                            for c in range(C4):
                                last = nc.tensor.matmul(pS[:, c, 0:D + 1], xs[0:P, j, c * 128:(c + 1) * 128],
                                                        xe[0:P, j, :], start=False, stop=False, skip_group_check=True)
                            last.then_inc(used, 1)
                    for c in range(C4):
                        last = nc.tensor.matmul(pS[:, c, 0:D + 1], g.zeros[:, 0:128], g.zeros[:, 0:D + 1], start=False, stop=True)
                    last.then_inc(opened, 1)

                @block.vector
                def _(dve):
                    nc.vector.memset(xe[:, :, D:D + 1], 1.0)
                    with dve.Fori(0, T // G) as i:
                        for j in range(G):
                            dve.wait_ge(used, i * G + j + 1)
                            nc.vector.tensor_copy(xe[0:P, j, 0:D], row(g.XN, i * G + j)).then_inc(staged_x, 1)
                    dve.wait_ge(opened, 1)
                    nc.vector.tensor_copy(S[:, :, :], pS[:, :, 0:D + 1])

            slice_attention(nc, g, a, S, M)

        def put2(dve, i, product, bias):
            nc.vector.tensor_tensor(row(g.XN, i), product, bias[0:P, :], ALU.add)
            dve.drain()
            return nc.vector.tensor_tensor(row(g.X, i), row(g.XN, i), row(g.X, i), ALU.add)

        linear(nc, g, "f0o", SW, HEADS * GROUPS, M, a["L0_ffn_b_out"], D, put2)


def slice_attention(nc, g, a, S, M):
    HG = HEADS * GROUPS
    with ExitStack() as ctx:
        sb, ps, sem = bufs(nc, ctx, "sa")
        wfx, bfx = sb("wfx", [128, K2, HG]), sb("bfx", [1, HG])
        wqkv, wout = sb("wqkv", [64, 3, 64]), sb("wout", [64, HEADS, D])
        rn, nrow = sb("rn", [128, C4]), sb("nrow", [1, HG])
        ST_ = sb("ST", [128, K2, HG])
        tok, q, k, v = (sb(m, [64, HG]) for m in ("tok", "q", "k", "v"))
        att, attT = sb("att", [64, HEADS, 64]), sb("attT", [64, HEADS, 64])
        vw, m64, top = sb("vw", [64, HEADS, D]), sb("m64", [64, HEADS, D]), sb("top", [64, HEADS])
        pA, pB = ps("pA", [128, 4, 512]), ps("pB", [128, 4, 512])
        loaded, pe_done, dve_done, act_done, moved = (sem(m) for m in ("loaded", "pe_done", "dve_done", "act_done", "moved"))
        block = ctx.enter_context(stage(nc, g))

        @block.sync
        def _(sp):
            sp.dma_start(wfx[:, :, :], a["L0_ffn_W_fx"].rearrange("(k p) n -> p k n", p=128)).then_inc(loaded, 16)
            sp.dma_start(bfx[:, :], a["L0_ffn_b_fx"].rearrange("(a n) -> a n", a=1)).then_inc(loaded, 16)
            for i, w in enumerate(("W_q", "W_k", "W_v")):
                sp.dma_start(wqkv[:, i, :], a["L0_ffn_" + w]).then_inc(loaded, 16)
            sp.dma_start(wout[:, :, :], a["L0_ffn_W_out"].rearrange("(h c) n -> c h n", c=64)).then_inc(loaded, 16)
            sp.wait_ge(loaded, 96)
            sp.wait_ge(dve_done, 8)
            sp.dma_start(M[0:64, :, :], m64[:, 0:HEADS:2, :]).then_inc(moved, 16)
            sp.dma_start(M[64:128, :, :], m64[:, 1:HEADS:2, :]).then_inc(moved, 16)
            sp.wait_ge(moved, 32)

        @block.vector
        def _(dve):
            nc.vector.tensor_scalar(rn[:, :], S[:, :, D], 1e-5, None, ALU.add)
            dve.drain()
            nc.vector.reciprocal(rn[:, :], rn[:, :])
            dve.drain()
            nc.vector.tensor_tensor(S[:, :, :], S[:, :, :], deep(rn[:, :], 128, C4, D + 1), ALU.mult).then_inc(dve_done, 1)
            dve.wait_ge(pe_done, 1)
            nc.vector.tensor_copy(ST_[:, :, :], pA[:, 0:K2, :])
            nc.vector.tensor_copy(nrow[:, :], pB[0:1, 0, :]).then_inc(dve_done, 1)
            dve.wait_ge(pe_done, 2)
            nc.vector.tensor_copy(tok[:, :], pB[0:64, 1, :]).then_inc(dve_done, 1)
            dve.wait_ge(pe_done, 3)
            nc.vector.tensor_copy(q[:, :], pA[0:64, 0, :])
            nc.vector.tensor_copy(k[:, :], pA[0:64, 1, :])
            nc.vector.tensor_copy(v[:, :], pA[0:64, 2, :]).then_inc(dve_done, 1)
            dve.wait_ge(pe_done, 4)
            scores = pB[0:64, 0, :].rearrange("p (h s) -> p h s", h=HEADS)
            nc.vector.tensor_reduce(top[:, :], scores, AX, ALU.max)
            dve.drain()
            nc.vector.tensor_tensor(att[:, :, :], scores, deep(top[:, :], 64, HEADS, 64), ALU.subtract).then_inc(dve_done, 1)
            dve.wait_ge(act_done, 1)
            nc.vector.tensor_reduce(top[:, :], att[:, :, :], AX, ALU.add)
            dve.drain()
            nc.vector.reciprocal(top[:, :], top[:, :])
            dve.drain()
            nc.vector.tensor_tensor(att[:, :, :], att[:, :, :], deep(top[:, :], 64, HEADS, 64), ALU.mult).then_inc(dve_done, 1)
            dve.wait_ge(pe_done, 5)
            nc.vector.tensor_copy(attT[:, :, :], pB[0:64, 2, :].rearrange("p (h s) -> p h s", h=HEADS))
            nc.vector.tensor_copy(vw[:, :, :], pA[0:64, :, :].rearrange("p b (h n) -> p (b h) n", n=D)).then_inc(dve_done, 1)
            dve.wait_ge(pe_done, 6)
            nc.vector.tensor_copy(m64[:, :, :], pB[0:64, :, :].rearrange("p b (h n) -> p (b h) n", n=D)).then_inc(dve_done, 1)

        @block.scalar
        def _(act):
            act.wait_ge(dve_done, 5)
            nc.scalar.activation(att[:, :, :], att[:, :, :], ACT.Exp, scale=64 ** -0.5).then_inc(act_done, 1)

        @block.tensor
        def _(pe):
            pe.wait_ge(dve_done, 1)
            for c in range(C4):
                for kk in range(K2):
                    nc.tensor.transpose(pA[:, kk, c * 128:(c + 1) * 128], S[:, c, kk * 128:(kk + 1) * 128], g.ident[:, :])
                last = nc.tensor.transpose(pB[0:1, 0, c * 128:(c + 1) * 128], S[:, c, D:D + 1], g.ident[:, :])
            last.then_inc(pe_done, 1)
            pe.wait_ge(dve_done, 2)
            pe.wait_ge(loaded, 96)
            for h in range(HEADS):
                cols = slice(h * 64, (h + 1) * 64)
                nc.tensor.matmul(pB[0:64, 1, cols], wfx[:, 0, cols], ST_[:, 0, cols], start=True, stop=False)
                nc.tensor.matmul(pB[0:64, 1, cols], wfx[:, 1, cols], ST_[:, 1, cols], start=False, stop=False)
                last = nc.tensor.matmul(pB[0:64, 1, cols], bfx[:, cols], nrow[:, cols], start=False, stop=True)
            last.then_inc(pe_done, 1)
            pe.wait_ge(dve_done, 3)
            for i in range(3):
                last = nc.tensor.matmul(pA[0:64, i, :], wqkv[:, i, :], tok[:, :], start=True, stop=True)
            last.then_inc(pe_done, 1)
            pe.wait_ge(dve_done, 4)
            for h in range(HEADS):
                cols = slice(h * 64, (h + 1) * 64)
                last = nc.tensor.matmul(pB[0:64, 0, cols], q[:, cols], k[:, cols], start=True, stop=True)
            last.then_inc(pe_done, 1)
            for h in range(HEADS):
                nc.tensor.matmul(pA[0:64, h // 2, (h % 2) * D:(h % 2 + 1) * D], v[:, h * 64:(h + 1) * 64], wout[:, h, :],
                                 start=True, stop=True)
            pe.wait_ge(dve_done, 6)
            for h in range(HEADS):
                last = nc.tensor.transpose(pB[0:64, 2, h * 64:(h + 1) * 64], att[:, h, :], g.ident[0:64, 0:64])
            last.then_inc(pe_done, 1)
            pe.wait_ge(dve_done, 7)
            for h in range(HEADS):
                last = nc.tensor.matmul(pB[0:64, h // 2, (h % 2) * D:(h % 2 + 1) * D], attT[:, h, :], vw[:, h, :],
                                        start=True, stop=True)
            last.then_inc(pe_done, 1)



def scale_rows(nc, acc, width, factor):
    return lambda dve: nc.vector.tensor_tensor(acc[0:P], acc[0:P], deep(factor[0:P], P, T, width), ALU.mult)


def gcn_finish(nc, g, tag, acc, width, dinv, bias_dram, out, residual=None, table=None):
    with ExitStack() as ctx:
        sb, ps, sem = bufs(nc, ctx, tag)
        loaded, finished, stored = sem("loaded"), sem("finished"), sem("stored")
        bias = sb("bias", [128, width])
        block = ctx.enter_context(stage(nc, g))

        @block.sync
        def _(sp):
            sp.dma_start(bias[:, :], bias_dram.partition_broadcast(128)).then_inc(loaded, 16)
            sp.wait_ge(loaded, 16)
            if table is not None:
                sp.wait_ge(finished, 1)
                sp.dma_start(table.rearrange("(p t) d -> p t d", p=P), out[0:P]).then_inc(stored, 16)
                sp.wait_ge(stored, 16)

        @block.vector
        def _(dve):
            dve.wait_ge(loaded, 16)
            for t in range(T):
                nc.vector.scalar_tensor_tensor(out=acc[0:P, t, :], in0=acc[0:P, t, :], scalar=dinv[0:P, t:t + 1],
                                               in1=bias[0:P, :], op0=ALU.mult, op1=ALU.add)
            dve.drain()
            if table is not None:
                last = nc.vector.scalar_tensor_tensor(out=out[0:P], in0=acc[0:P], scalar=0.0,
                                                      in1=deep(dinv[0:P], P, T, width), op0=ALU.max, op1=ALU.mult)
            else:
                last = nc.vector.scalar_tensor_tensor(out=out[0:P], in0=acc[0:P], scalar=0.0, in1=residual[0:P],
                                                      op0=ALU.max, op1=ALU.add)
            last.then_inc(finished, 1)


def add_affine(nc, g, tag, a3, scale_dram, shift_dram, dst):
    with ExitStack() as ctx:
        sb, ps, sem = bufs(nc, ctx, tag)
        loaded = sem("loaded")
        both = sb("both", [128, 2, D])
        block = ctx.enter_context(stage(nc, g))

        @block.sync
        def _(sp):
            sp.dma_start(both[:, 0, :], scale_dram.partition_broadcast(128)).then_inc(loaded, 16)
            sp.dma_start(both[:, 1, :], shift_dram.partition_broadcast(128)).then_inc(loaded, 16)
            sp.wait_ge(loaded, 32)

        @block.vector
        def _(dve):
            dve.wait_ge(loaded, 32)
            nc.vector.tensor_tensor(a3[0:P], a3[0:P], wide(both[0:P, 0, :], P, T, D), ALU.mult)
            nc.vector.tensor_tensor(dst[0:P], dst[0:P], wide(both[0:P, 1, :], P, T, D), ALU.add)
            dve.drain()
            nc.vector.tensor_tensor(dst[0:P], dst[0:P], a3[0:P], ALU.add)


def add_biased(nc, dst, tmp):
    def put(dve, i, product, bias):
        nc.vector.tensor_tensor(row(tmp, i, 0, D), product, bias[0:P, :], ALU.add)
        dve.drain()
        return nc.vector.tensor_tensor(row(dst, i), row(tmp, i, 0, D), row(dst, i), ALU.add)
    return put


def layer1_gnn(nc, g, a):
    layer_norm(nc, g, "g1n", g.X, g.XN)
    with ExitStack() as ctx:
        sb, ps, sem = bufs(nc, ctx, "g1")
        Z128, Z64 = g.XN[:, :, 0:128], g.XN[:, :, 128:192]

        def scaled(out):
            return lambda dve, i, product, bias: nc.vector.tensor_scalar(
                row(out, i), product, g.dinv1[0:P, bass.ds(i, 1)], None, ALU.mult)

        linear(nc, g, "g1a", g.XN, D, a["L1_gnn_W1"], None, 128, scaled(Z128), table=(g.table128, Z128))
        aggregate(nc, g, "g1ag", Z128, g.table128, 128)

        linear(nc, g, "g1b", Z128, 128, a["L1_gnn_W2"], None, 64, scaled(Z64),
               prepare=scale_rows(nc, Z128, 128, g.dinv1), turn=(ACT.Relu, None, a["L1_gnn_b1"]), table=(g.table64, Z64))
        aggregate(nc, g, "g1bg", Z64, g.table64, 64)

        gcn_finish(nc, g, "g1bf", Z64, 64, g.dinv1, a["L1_gnn_b2"], Z64, table=g.table64)
        aggregate(nc, g, "g1cg", Z64, g.table64, 64)

        def hidden(dve, i, product, bias):
            nc.vector.tensor_tensor(row(Z128, i), product, bias[0:P, :], ALU.add)
            dve.drain()
            return nc.vector.tensor_scalar(row(Z128, i), row(Z128, i), 0.0, g.dinv1[0:P, bass.ds(i, 1)],
                                           ALU.max, ALU.mult)

        linear(nc, g, "g1d", Z64, 64, a["L1_gnn_W3"], a["L1_gnn_b3"], 128, hidden,
               prepare=scale_rows(nc, Z64, 64, g.dinv1), table=(g.table128, Z128))
        aggregate(nc, g, "g1dg", Z128, g.table128, 128)
        linear(nc, g, "g1e", Z128, 128, a["L1_gnn_W4"], a["L1_gnn_b4"], D, add_biased(nc, g.X, g.XN),
               prepare=scale_rows(nc, Z128, 128, g.dinv1))


def layer2_gnn(nc, g, a):
    layer_norm(nc, g, "g2n", g.X, g.XN)
    with ExitStack() as ctx:
        sb, ps, sem = bufs(nc, ctx, "g2")
        H = sb("H", [128, T, D])
        for n in ("6", "7"):
            layer_norm(nc, g, f"g2n{n}", g.XN, H)

            def scaled(dve, i, product, bias):
                return nc.vector.tensor_scalar(row(H, i), product, g.dinv2[0:P, bass.ds(i, 1)], None, ALU.mult)

            linear(nc, g, f"g2l{n}", H, D, a[f"L2_gnn_W{n}"], None, D, scaled,
                   turn=(ACT.Identity, a[f"L2_gnn_ln{n}_g"], a[f"L2_gnn_ln{n}_b"]), table=(g.table256, H))
            aggregate(nc, g, f"g2g{n}", H, g.table256, D, weighted=True)
            gcn_finish(nc, g, f"g2f{n}", H, D, g.dinv2, a[f"L2_gnn_b{n}"], g.XN, residual=g.XN)
        linear(nc, g, "g2p", g.XN, D, a["L2_gnn_Wp"], a["L2_gnn_bp"], D, add_biased(nc, g.X, H))


def layer3_gnn(nc, g, a):
    layer_norm(nc, g, "g3n", g.X, g.XN)
    NR = a["L3_gnn_weight"].shape[0]
    NC = NR * D // 512
    with ExitStack() as ctx:
        sb, ps, sem = bufs(nc, ctx, "g3")
        w = sb("w", [128, K2, NR, D])
        bias = sb("bias", [128, D])
        xs, xT, ys = sb("xs", [128, G, D]), sb("xT", [128, G, K2, P]), sb("ys", [128, G, NR * D])
        psT, psO = ps("psT", [128, 3, 512]), ps("psO", [128, NC, 512])
        w_loaded, b_loaded, staged, turned, turn_read = (sem(m) for m in ("w_loaded", "b_loaded", "staged", "turned", "turn_read"))
        multiplied, put_away, turn = sem("multiplied"), sem("put_away"), sem("turn")
        stored = [sem(f"stored{j}") for j in range(G)]
        relations = g.relations.rearrange("(r p t) d -> t p r d", r=NR, p=P)
        block = ctx.enter_context(stage(nc, g))

        @block.sync
        def _(sp):
            for k in range(K2):
                sp.dma_start(w[:, k, :, :], a["L3_gnn_weight"][:, k * 128:(k + 1) * 128, :].rearrange("r p n -> p r n")).then_inc(w_loaded, 16)
            sp.dma_start(bias[:, :], a["L3_gnn_bias"].partition_broadcast(128)).then_inc(b_loaded, 16)
            with sp.Fori(0, T // G) as i:
                for j in range(G):
                    sp.wait_ge(put_away, (i * G + j + 2) * NC)
                    sp.dma_start(relations[bass.ds(i * G + j, 1)].rearrange("a p r d -> p (a r) d"),
                                 ys[0:P, j, :].rearrange("p (r d) -> p r d", d=D)).then_inc(stored[j], 16)
            for j in range(G):
                sp.wait_ge(stored[j], 16 * (T // G + 1))

        @block.tensor
        def _(pe):
            pe.wait_ge(w_loaded, 16 * K2)
            with pe.Fori(0, T // G) as i:
                for j in range(G):
                    pe.wait_ge(staged, i * G + j + 1)
                    pe.wait_ge(turn_read, i * G + j + 1)
                    for k in range(K2):
                        last = nc.tensor.transpose(psT[:, j % 3, k * P:(k + 1) * P], xs[0:P, j, k * 128:(k + 1) * 128],
                                                   g.ident[0:P, 0:P])
                    last.then_inc(turned, 1)
                for j in range(G):
                    pe.wait_ge(turn_read, i * G + j + 3)
                    for c in range(NC):
                        pe.wait_ge(put_away, (i * G + j) * NC + c + 1)
                        for k in range(K2):
                            last = nc.tensor.matmul(psO[0:P, c, :], xT[:, j, k, :],
                                                    w[:, k, 2 * c:2 * c + 2, :].rearrange("p r n -> p (r n)"),
                                                    start=(k == 0), stop=(k == K2 - 1))
                        last.then_inc(multiplied, 1)

        @block.scalar
        def _(act):
            act.sem_inc(turned, G)
            act.sem_inc(turn_read, 2)
            with act.Fori(0, T // G) as i:
                for j in range(G):
                    act.wait_ge(turned, i * G + j + 1)
                    nc.scalar.copy(xs[0:P, j, :], row(g.XN, i * G + j)).then_inc(staged, 1)
                for j in range(G):
                    act.wait_ge(turned, i * G + j + 1 + G)
                    nc.scalar.copy(xT[:, j, :, :], psT[:, j % 3, 0:K2 * P].rearrange("p (k r) -> p k r", k=K2)).then_inc(turn_read, 1)

        @block.vector
        def _(dve):
            dve.sem_inc(put_away, NC)
            for j in range(G):
                dve.sem_inc(stored[j], 16)
            dve.wait_ge(b_loaded, 16)
            nc.vector.tensor_tensor(g.X[0:P], g.X[0:P], wide(bias[0:P, :], P, T, D), ALU.add)
            with dve.Fori(0, T // G) as i:
                for j in range(G):
                    dve.wait_ge(stored[j], (i + 1) * 16)
                    for c in range(NC):
                        dve.wait_ge(multiplied, (i * G + j) * NC + c + 1)
                        nc.vector.tensor_copy(ys[0:P, j, c * 512:(c + 1) * 512], psO[0:P, c, :]).then_inc(put_away, 1)

    aggregate(nc, g, "g3g", g.X, g.relations, D, field=3)


def route(nc, g, tag, logits, n, first, softmax_first=False, hot=None, weight=None):
    with ExitStack() as ctx:
        sb, ps, sem = bufs(nc, ctx, tag)
        low = sb("low", [128, T, n])
        hots = hot if hot is not None else sb("hots", [128, T, 2, n])
        top = sb("top", [128, 2, T])
        centred, powers = sem("centred"), sem("powers")
        block = ctx.enter_context(stage(nc, g))
        iota = wide(g.iota[0:P, 0:n], P, T, n)
        L = logits[0:P]

        @block.vector
        def _(dve):
            if softmax_first:
                nc.vector.tensor_reduce(top[0:P, 0], L, AX, ALU.max)
                dve.drain()
                nc.vector.tensor_tensor(L, L, deep(top[0:P, 0], P, T, n), ALU.subtract).then_inc(centred, 1)
                dve.wait_ge(powers, 1)
                nc.vector.tensor_reduce(top[0:P, 0], L, AX, ALU.add)
                dve.drain()
                nc.vector.reciprocal(top[0:P, 0], top[0:P, 0])
                dve.drain()
                nc.vector.tensor_tensor(L, L, deep(top[0:P, 0], P, T, n), ALU.mult)
                dve.drain()
            for k in range(2):
                nc.vector.tensor_reduce(top[0:P, k], L, AX, ALU.max)
                dve.drain()
                nc.vector.tensor_tensor(low[0:P], L, deep(top[0:P, k], P, T, n), ALU.is_lt)
                dve.drain()
                nc.vector.scalar_tensor_tensor(out=low[0:P], in0=low[0:P], scalar=100.0, in1=iota, op0=ALU.mult, op1=ALU.add)
                dve.drain()
                nc.vector.tensor_reduce(first[0:P, :, k], low[0:P], AX, ALU.min)
                dve.drain()
                nc.vector.tensor_tensor(hots[0:P, :, k, :], iota, first[0:P, :, k:k + 1].broadcast_to([P, T, n]), ALU.is_equal)
                if k == 0:
                    dve.drain()
                    nc.vector.scalar_tensor_tensor(out=L, in0=hots[0:P, :, 0, :], scalar=-BIG, in1=L, op0=ALU.mult, op1=ALU.add)
                    dve.drain()
            nc.vector.tensor_tensor(weight[0:P, :, 1], top[0:P, 1], top[0:P, 0], ALU.subtract).then_inc(centred, 1)
            dve.wait_ge(powers, 2 if softmax_first else 1)
            nc.vector.tensor_scalar(weight[0:P, :, 0], weight[0:P, :, 1], 1.0, None, ALU.add)
            dve.drain()
            nc.vector.reciprocal(weight[0:P, :, 0], weight[0:P, :, 0])
            dve.drain()
            nc.vector.tensor_tensor(weight[0:P, :, 1], weight[0:P, :, 1], weight[0:P, :, 0], ALU.mult)

        @block.scalar
        def _(act):
            if softmax_first:
                act.wait_ge(centred, 1)
                nc.scalar.activation(L, L, ACT.Exp).then_inc(powers, 1)
            act.wait_ge(centred, 2 if softmax_first else 1)
            nc.scalar.activation(weight[0:P, :, 1], weight[0:P, :, 1], ACT.Exp).then_inc(powers, 1)


def gate(nc, g, tag, w, b, n, out):
    def put(dve, i, product, bias):
        return nc.vector.tensor_tensor(row(out, i), product, bias[0:P, :], ALU.add)
    linear(nc, g, tag, g.XN, D, w, b, n, put)


def load_expert_weights(nc, g, a):
    NE, _, F = a["L1_ffn_w1"].shape
    KF = F // 128
    w1 = g.w1[:, :].rearrange("p (e k n) -> p e k n", e=NE, k=K2)
    w2 = g.w2[:, :].rearrange("p (e k n) -> p e k n", e=NE, k=KF)
    with stage(nc, g) as block:
        @block.sync
        def _(sp):
            for e in range(NE):
                sp.dma_start(w1[:, e], a["L1_ffn_w1"][e].rearrange("(k p) n -> p k n", p=128)).then_inc(g.w_loaded, 16)
                sp.dma_start(w2[:, e], a["L1_ffn_w2"][e].rearrange("(k p) n -> p k n", p=128)).then_inc(g.w_loaded, 16)


def layer1_ffn(nc, g, a):
    NE, _, F = a["L1_ffn_w1"].shape
    KF = F // 128
    SLOTS = (2 * N + NE * 127) // 128
    AHEAD = 2
    assert SLOTS % 2 == 0
    layer_norm(nc, g, "f1n", g.X, g.XN)
    with ExitStack() as ctx:
        sb, ps, sem = bufs(nc, ctx, "f1")
        logits, chosen, weight = sb("logits", [128, T, NE]), sb("chosen", [128, T, 2]), sb("weight", [128, T, 2])
        posf, posi = sb("posf", [128, 2 * T]), sb("posi", [128, 2 * T], I32)
        kmap = sb("kmap", [1, SLOTS + AHEAD], I32)
        gate(nc, g, "f1g", a["L1_ffn_gate_w"], a["L1_ffn_gate_b"], NE, logits)
        route(nc, g, "f1r", logits, NE, chosen, weight=weight)
        with ExitStack() as sub:
            sb1, ps1, sem1 = bufs(nc, sub, "f1s")
            hot, tiles = sb1("hot", [128, NE, 2 * T]), sb1("tiles", [1, SLOTS + AHEAD])
            counting_sort(nc, g, "f1c", chosen[:, :, :].rearrange("p t k -> p (t k)"), P, NE, 2 * T, posf, hot,
                          kmap=kmap, slots=SLOTS + AHEAD, tiles=tiles)
            placed, kept = sem1("placed"), sem1("kept")
            scattered, done = g.moved[0], g.count(0, 32 * T)
            block = sub.enter_context(stage(nc, g))

            @block.sync
            def _(sp):
                sp.dma_start(g.table256.rearrange("(p t) d -> p t d", p=P), g.XN[0:P]).then_inc(kept, 16)
                sp.wait_ge(kept, 16)

            @block.vector
            def _(dve):
                nc.vector.tensor_copy(posi[0:P], posf[0:P]).then_inc(placed, 1)

            @block.gpsimd
            def _(pool):
                pool.wait_ge(g.cleared, 16)
                pool.wait_ge(placed, 1)
                for t in range(T):
                    for k in range(2):
                        pool.indirect_dma_start(out=g.bins[:, :],
                                                out_offset=bass.IndirectOffsetOnAxis(ap=posi[0:P, 2 * t + k:2 * t + k + 1], axis=0),
                                                in_=g.XN[0:P, t, :], in_offset=None).then_inc(scattered, 16)
                pool.wait_ge(scattered, done)

        with ExitStack() as sub:
            sb1, ps1, sem1 = bufs(nc, sub, "f1e")
            w1f, w2f = g.w1[:, :], g.w2[:, :]
            b = sb1("b", [128, 2, F + D])
            room = g.XN[:, :, :].rearrange("p t d -> p (t d)")
            xs = room[:, 0:2 * D].rearrange("p (j d) -> p j d", j=2)
            xT = room[:, 2 * D:4 * D].rearrange("p (j k r) -> p j k r", j=2, k=K2)
            ys = room[:, 4 * D:6 * D].rearrange("p (j d) -> p j d", j=2)
            h = room[:, 6 * D:6 * D + 2 * F].rearrange("p (j n) -> p j n", j=2)
            hT = room[:, 6 * D + 2 * F:6 * D + 4 * F].rearrange("p (j k r) -> p j k r", j=2, k=KF)
            pT, pH, pU, pY = (ps1(m, [128, 2, 512]) for m in ("pT", "pH", "pU", "pY"))
            x_loaded, b_loaded, stored = ([sem1(f"{m}{j}") for j in range(2)] for m in ("x_loaded", "b_loaded", "stored"))
            x_turned, x_read, h_made, h_put, h_turned, h_read, y_made, y_put = (
                sem1(m) for m in ("x_turned", "x_read", "h_made", "h_put", "h_turned", "h_read", "y_made", "y_put"))
            bins = g.bins.rearrange("(s p) d -> s p d", p=128)
            results = g.results.rearrange("(s p) d -> s p d", p=128)
            block = sub.enter_context(stage(nc, g))

            @block.sync
            def _(sp):
                def load_rows(n, j):
                    sp.dma_start(xs[:, j, :], bins[bass.ds(n, 1)].rearrange("a p d -> (a p) d")).then_inc(x_loaded[j], 16)

                def load_bias(e, j):
                    for name, lo, hi in (("L1_ffn_b1", 0, F), ("L1_ffn_b2", F, F + D)):
                        sp.dma_start(b[:, j, lo:hi], a[name][bass.ds(e, 1), :].rearrange("a n -> (a n)")
                                     .partition_broadcast(128)).then_inc(b_loaded[j], 16)

                e = load_keys(nc, mybir.EngineType.SP, kmap, 0, 2, NE)
                for j in range(2):
                    load_rows(j, j)
                    load_bias(e[j], j)
                with sp.Fori(0, SLOTS // 2) as i:
                    e = load_keys(nc, mybir.EngineType.SP, kmap, 2 * i + 2, 2, NE)
                    for j in range(2):
                        sp.wait_ge(x_turned, 2 * i + j + 1)
                        load_rows(2 * i + 2 + j, j)
                    for j in range(2):
                        sp.wait_ge(y_put, 2 * i + j + 3)
                        load_bias(e[j], j)
                for j in range(2):
                    sp.wait_ge(x_loaded[j], 16 * (SLOTS // 2 + 1))
                    sp.wait_ge(b_loaded[j], 32 * (SLOTS // 2 + 1))

            @block.tensor
            def _(pe):
                def turn_rows(loads, j):
                    pe.wait_ge(x_loaded[j], loads * 16)
                    for k in range(K2):
                        last = nc.tensor.transpose(pT[:, j, k * 128:(k + 1) * 128], xs[:, j, k * 128:(k + 1) * 128], g.ident[:, :])
                    last.then_inc(x_turned, 1)

                pe.wait_ge(g.w_loaded, 32 * NE)
                for j in range(2):
                    turn_rows(1, j)
                with pe.Fori(0, SLOTS // 2) as i:
                    expert = load_keys(nc, mybir.EngineType.PE, kmap, 2 * i, 2, NE)
                    for j in range(2):
                        pe.wait_ge(x_read, 2 * i + j + 1)
                        for k in range(K2):
                            last = nc.tensor.matmul(pH[:, j, :], xT[:, j, k, :],
                                                    w1f[:, bass.ds(expert[j] * (K2 * F) + k * F, F)],
                                                    start=(k == 0), stop=(k == K2 - 1))
                        last.then_inc(h_made, 1)
                    for j in range(2):
                        turn_rows(i + 2, j)
                    for j in range(2):
                        pe.wait_ge(h_put, 2 * i + j + 1)
                        for k in range(KF):
                            last = nc.tensor.transpose(pU[:, j, k * 128:(k + 1) * 128], h[:, j, k * 128:(k + 1) * 128], g.ident[:, :])
                        last.then_inc(h_turned, 1)
                    for j in range(2):
                        pe.wait_ge(h_read, 2 * i + j + 1)
                        pe.wait_ge(y_put, 2 * i + j + 1)
                        for k in range(KF):
                            last = nc.tensor.matmul(pY[:, j, 0:D], hT[:, j, k, :], w2f[:, bass.ds(expert[j] * (KF * D) + k * D, D)],
                                                    start=(k == 0), stop=(k == KF - 1))
                        last.then_inc(y_made, 1)

            @block.scalar
            def _(act):
                def read_rows(n, j):
                    act.wait_ge(x_turned, n + 1)
                    nc.scalar.copy(xT[:, j, :, :], pT[:, j, 0:K2 * 128].rearrange("p (k r) -> p k r", k=K2)).then_inc(x_read, 1)

                for j in range(2):
                    act.sem_inc(stored[j], 16)
                    read_rows(j, j)
                with act.Fori(0, SLOTS // 2) as i:
                    for j in range(2):
                        read_rows(2 * i + j + 2, j)
                    for j in range(2):
                        act.wait_ge(h_turned, 2 * i + j + 1)
                        nc.scalar.activation(hT[:, j, :, :], pU[:, j, :].rearrange("p (k r) -> p k r", k=KF),
                                             ACT.Relu).then_inc(h_read, 1)
                    for j in range(2):
                        act.wait_ge(y_put, 2 * i + j + 3)
                        act.dma_start(results[bass.ds(2 * i + j, 1)].rearrange("a p d -> (a p) d"), ys[:, j, :]).then_inc(stored[j], 16)
                for j in range(2):
                    act.wait_ge(stored[j], 16 * (SLOTS // 2 + 1))

            @block.vector
            def _(dve):
                dve.sem_inc(y_put, 2)
                with dve.Fori(0, SLOTS // 2) as i:
                    for j in range(2):
                        dve.wait_ge(b_loaded[j], (i + 1) * 32)
                        dve.wait_ge(h_made, 2 * i + j + 1)
                        nc.vector.tensor_tensor(h[:, j, :], pH[:, j, :], b[:, j, 0:F], ALU.add).then_inc(h_put, 1)
                    for j in range(2):
                        dve.wait_ge(stored[j], (i + 1) * 16)
                        dve.wait_ge(y_made, 2 * i + j + 1)
                        nc.vector.tensor_tensor(ys[:, j, :], pY[:, j, 0:D], b[:, j, F:F + D], ALU.add).then_inc(y_put, 1)

        with ExitStack() as sub:
            sb1, ps1, sem1 = bufs(nc, sub, "f1y")
            Y = [g.w1[:, k * T * D:(k + 1) * T * D].rearrange("p (t d) -> p t d", t=T) for k in range(2)]
            C = T // G
            gathered, done = g.moved[0:C], [g.count(c, 32 * G) for c in range(C)]
            reloaded = sem1("reloaded")
            with stage(nc, g) as block:
                @block.sync
                def _(sp):
                    sp.dma_start(g.XN[0:P], g.table256.rearrange("(p t) d -> p t d", p=P)).then_inc(reloaded, 16)

                @block.gpsimd
                def _(pool):
                    for t in range(T):
                        for k in range(2):
                            pool.indirect_dma_start(out=Y[k][0:P, t, :], out_offset=None, in_=g.results[:, :],
                                                    in_offset=bass.IndirectOffsetOnAxis(ap=posi[0:P, 2 * t + k:2 * t + k + 1], axis=0)
                                                    ).then_inc(gathered[t // G], 16)

                @block.vector
                def _(dve):
                    dve.wait_ge(reloaded, 16)
                    for c in range(C):
                        dve.wait_ge(gathered[c], done[c])
                        for k in range(2):
                            for t in range(c * G, (c + 1) * G):
                                nc.vector.scalar_tensor_tensor(out=g.XN[0:P, t, :], in0=Y[k][0:P, t, :],
                                                               scalar=weight[0:P, t, k:k + 1], in1=g.XN[0:P, t, :],
                                                               op0=ALU.mult, op1=ALU.add)
                            dve.drain()
            layer_norm(nc, g, "f1m", g.XN, Y[0])
            add_affine(nc, g, "f1a", Y[0], a["L1_ffn_gamma"], a["L1_ffn_beta"], g.X)


def layer2_ffn(nc, g, a):
    NE, _, H1 = a["L2_ffn_eW1"].shape
    H2 = a["L2_ffn_eW2"].shape[2]
    layer_norm(nc, g, "f2n", g.X, g.XN)
    with ExitStack() as ctx:
        sb, ps, sem = bufs(nc, ctx, "f2")
        logits, chosen, weight = sb("logits", [128, T, NE]), sb("chosen", [128, T, 2]), sb("weight", [128, T, 2])
        hot, coef = sb("hot", [128, T, 2, NE]), sb("coef", [128, T, NE])
        gate(nc, g, "f2g", a["L2_ffn_gW"], a["L2_ffn_gb"], NE, logits)
        route(nc, g, "f2r", logits, NE, chosen, softmax_first=True, hot=hot, weight=weight)
        with stage(nc, g) as block:
            @block.vector
            def _(dve):
                nc.vector.tensor_tensor(hot[0:P], hot[0:P], weight[0:P].rearrange("p t (k a) -> p t k a", a=1)
                                        .broadcast_to([P, T, 2, NE]), ALU.mult)
                dve.drain()
                nc.vector.tensor_tensor(coef[0:P], hot[0:P, :, 0, :], hot[0:P, :, 1, :], ALU.add)

        s1, s2, s3 = sb("s1", [128, K2, 256]), sb("s2", [128, 2, 128]), sb("s3", [128, D])
        e1, e2, e3 = sb("e1", [128, K2, NE, H1]), sb("e2", [128, NE, H2]), sb("e3", [H2 + 1, NE, D])
        sb1_, sb2_, sb3_ = sb("sb1", [128, 2]), sb("sb2", [128, 1]), sb("sb3", [128, D])
        eb1, eb2 = sb("eb1", [128, NE]), sb("eb2", [H2, NE])
        GROUPS_ = ((0, 3), (3, 2))
        WIDE = 3 * P
        xs, xT = sb("xs", [128, G, D]), sb("xT", [128, K2, G * P])
        hs, he = sb("hs", [128, 2, WIDE]), sb("he", [128, NE, WIDE])
        h2s, h2e = sb("h2s", [128, WIDE]), sb("h2e", [H2 + 1, NE, WIDE])
        acc = sb("acc", [128, D])
        pT, pR, pO = ps("pT", [128, 2, 512]), ps("pR", [128, 3, 512]), ps("pO", [128, 3, 512])
        loaded, set1, staged, turned, turn_read = (sem(m) for m in ("loaded", "set1", "staged", "turned", "turn_read"))
        made, put_away, outs, outs_read = (sem(m) for m in ("made", "put_away", "outs", "outs_read"))
        NH = 2 + NE + 1 + NE
        block = ctx.enter_context(stage(nc, g))

        @block.sync
        def _(sp):
            for out, src in ((s1[:, :, :], a["L2_ffn_sW1"].rearrange("(k p) n -> p k n", p=128)),
                             (s2[:, :, :], a["L2_ffn_sW2"].rearrange("(k p) n -> p k n", p=128)),
                             (s3[:, :], a["L2_ffn_sW3"]),
                             (e1[:, 0], a["L2_ffn_eW1"][:, 0:128, :].rearrange("e p n -> p e n")),
                             (e1[:, 1], a["L2_ffn_eW1"][:, 128:256, :].rearrange("e p n -> p e n")),
                             (e2[:, :, :], a["L2_ffn_eW2"].rearrange("e p n -> p e n")),
                             (e3[0:H2], a["L2_ffn_eW3"].rearrange("e p n -> p e n")),
                             (e3[H2:H2 + 1, :, :], a["L2_ffn_eb3"].rearrange("(a e) n -> a e n", a=1)),
                             (sb3_[:, :], a["L2_ffn_sb3"].partition_broadcast(128))):
                sp.dma_start(out, src).then_inc(loaded, 16)
            with nc.allow_non_contiguous_dma("a few hundred values"):
                sp.dma_start(sb1_[:, :], a["L2_ffn_sb1"].rearrange("(k p) -> p k", p=128)).then_inc(loaded, 16)
                sp.dma_start(sb2_[:, :], a["L2_ffn_sb2"].rearrange("(p k) -> p k", k=1)).then_inc(loaded, 16)
                sp.dma_start(eb1[:, :], a["L2_ffn_eb1"].rearrange("e p -> p e")).then_inc(loaded, 16)
                sp.dma_start(eb2[:, :], a["L2_ffn_eb2"].rearrange("e p -> p e")).then_inc(loaded, 16)
            sp.wait_ge(loaded, 208)

        @block.tensor
        def _(pe):
            pe.wait_ge(loaded, 208)
            pe.wait_ge(set1, 1)
            with pe.Fori(0, T // G) as i:
                for j in range(G):
                    pe.wait_ge(staged, i * G + j + 1)
                    pe.wait_ge(turn_read, i * G + j + (1 if j else 2))
                    for k in range(K2):
                        last = nc.tensor.transpose(pT[:, j % 2, k * P:(k + 1) * P], xs[0:P, j, k * 128:(k + 1) * 128], g.ident[0:P, 0:P])
                    last.then_inc(turned, 1)
                pe.wait_ge(turn_read, (i + 1) * G + 2)
                for m, (t0, nt) in enumerate(GROUPS_):
                    cols, w = slice(t0 * P, (t0 + nt) * P), nt * P
                    pieces = [[(s1[:, k, c * 128:(c + 1) * 128], xT[:, k, cols]) for k in range(K2)] for c in range(2)]
                    pieces += [[(e1[:, k, e, :], xT[:, k, cols]) for k in range(K2)] for e in range(NE)]
                    pieces += [[(s2[:, k, :], hs[:, k, 0:w]) for k in range(2)]]
                    pieces += [[(e2[:, e, :], he[:, e, 0:w])] for e in range(NE)]
                    for q, pairs in enumerate(pieces):
                        at = m * NH + q
                        rows = H2 if q > 2 + NE else 128
                        pe.wait_ge(put_away, i * (2 * NH) + at + (1 if at else 2))
                        for k, (lhs, rhs) in enumerate(pairs):
                            last = nc.tensor.matmul(pR[0:rows, at % 3, 0:w], lhs, rhs, start=(k == 0), stop=(k == len(pairs) - 1))
                        last.then_inc(made, 1)
                    pe.wait_ge(put_away, i * (2 * NH) + (m + 1) * NH + 2)
                    for t in range(nt):
                        n = i * G + t0 + t
                        rows = slice(t * P, (t + 1) * P)
                        parts = [(h2s[:, rows], s3[:, :])] + [(h2e[:, e, rows], e3[:, e, :]) for e in range(NE)]
                        for q, (lhs, rhs) in enumerate(parts):
                            if q % 2 == 0:
                                pe.wait_ge(outs_read, n * 3 + q // 2 + 1)
                            last = nc.tensor.matmul(pO[0:P, q // 2, (q % 2) * D:(q % 2 + 1) * D], lhs, rhs, start=True, stop=True)
                            if q % 2 or q == NE:
                                last.then_inc(outs, 1)

        @block.scalar
        def _(act):
            act.wait_ge(loaded, 208)
            act.sem_inc(turned, G)
            act.sem_inc(turn_read, 2)
            act.sem_inc(put_away, 2)
            with act.Fori(0, T // G) as i:
                for j in range(G):
                    act.wait_ge(turned, i * G + j + 1)
                    nc.scalar.copy(xs[0:P, j, :], row(g.XN, i * G + j)).then_inc(staged, 1)
                for j in range(G):
                    act.wait_ge(turned, i * G + j + 1 + G)
                    nc.scalar.copy(xT[:, :, j * P:(j + 1) * P], pT[:, j % 2, 0:K2 * P].rearrange("p (k r) -> p k r", k=K2)).then_inc(turn_read, 1)
                for m, (t0, nt) in enumerate(GROUPS_):
                    w = nt * P
                    places = [(hs[:, c, 0:w], sb1_[:, c:c + 1]) for c in range(2)]
                    places += [(he[:, e, 0:w], eb1[:, e:e + 1]) for e in range(NE)]
                    places += [(h2s[:, 0:w], sb2_[:, :])]
                    places += [(h2e[0:H2, e, 0:w], eb2[:, e:e + 1]) for e in range(NE)]
                    for q, (place, bias) in enumerate(places):
                        at = m * NH + q
                        rows = H2 if q > 2 + NE else 128
                        act.wait_ge(made, i * (2 * NH) + at + 1)
                        nc.scalar.activation(place, pR[0:rows, at % 3, 0:w], ACT.Relu, bias=bias).then_inc(put_away, 1)

        @block.vector
        def _(dve):
            nc.vector.memset(h2e[H2:H2 + 1, :, :], 1.0).then_inc(set1, 1)
            dve.sem_inc(outs_read, 3)
            dve.wait_ge(loaded, 208)
            nc.vector.tensor_tensor(g.X[0:P], g.X[0:P], wide(sb3_[0:P, :], P, T, D), ALU.add)
            with dve.Fori(0, T // G) as i:
                for j in range(G):
                    n = i * G + j
                    for q in range(NE + 1):
                        dve.drain()
                        if q % 2 == 0:
                            dve.wait_ge(outs, n * 3 + q // 2 + 1)
                        part = pO[0:P, q // 2, (q % 2) * D:(q % 2 + 1) * D]
                        if q == 0:
                            last = nc.vector.tensor_tensor(acc[0:P, :], part, row(g.X, n), ALU.add)
                        else:
                            last = nc.vector.scalar_tensor_tensor(
                                out=acc[0:P, :] if q < NE else row(g.X, n), in0=part, scalar=row(coef, n, q - 1, q),
                                in1=acc[0:P, :], op0=ALU.mult, op1=ALU.add)
                        if q % 2 or q == NE:
                            last.then_inc(outs_read, 1)


def layer3_ffn(nc, g, a):
    NE, _, F = a["L3_ffn_w1"].shape
    KF = F // 128
    C = -(-(5 * N) // (4 * NE))
    CS = 4
    layer_norm(nc, g, "f3n", g.X, g.XN)
    with ExitStack() as ctx:
        sb, ps, sem = bufs(nc, ctx, "f3")
        logits = sb("logits", [128, T, NE])
        low = sb("low", [128, T, NE])
        best, total, pos, kept, slot, away = (sb(m, [128, T]) for m in ("best", "total", "pos", "kept", "slot", "away"))
        to, back = sb("to", [128, T], I32), sb("back", [128, T], I32)
        gate(nc, g, "f3g", a["L3_ffn_gate_w"], a["L3_ffn_gate_b"], NE, logits)
        centred, powers = sem("centred"), sem("powers")
        with stage(nc, g) as block:
            L = logits[0:P]

            @block.vector
            def _(dve):
                nc.vector.tensor_reduce(total[0:P], L, AX, ALU.max)
                dve.drain()
                nc.vector.tensor_tensor(L, L, deep(total[0:P], P, T, NE), ALU.subtract).then_inc(centred, 1)
                dve.wait_ge(powers, 1)
                nc.vector.tensor_reduce(total[0:P], L, AX, ALU.add)
                nc.vector.tensor_reduce(best[0:P], L, AX, ALU.max)
                dve.drain()
                nc.vector.reciprocal(total[0:P], total[0:P])
                nc.vector.tensor_tensor(low[0:P], L, deep(best[0:P], P, T, NE), ALU.is_lt)
                dve.drain()
                nc.vector.scalar_tensor_tensor(out=low[0:P], in0=low[0:P], scalar=100.0,
                                               in1=wide(g.iota[0:P, 0:NE], P, T, NE), op0=ALU.mult, op1=ALU.add)
                dve.drain()
                nc.vector.tensor_reduce(best[0:P], low[0:P], AX, ALU.min)

            @block.scalar
            def _(act):
                act.wait_ge(centred, 1)
                nc.scalar.activation(L, L, ACT.Exp).then_inc(powers, 1)

        with ExitStack() as sub:
            sb1, ps1, sem1 = bufs(nc, sub, "f3s")
            hot = sb1("hot", [128, NE, T])
            counting_sort(nc, g, "f3c", best, P, NE, T, pos, hot, base=0)
            placed = sem1("placed")
            scattered, done = g.moved[0], g.count(0, 16 * T)
            block = sub.enter_context(stage(nc, g))

            @block.vector
            def _(dve):
                nc.vector.tensor_scalar(kept[0:P], pos[0:P], float(C), None, ALU.is_lt)
                nc.vector.tensor_scalar(pos[0:P], pos[0:P], float(C - 1), None, ALU.min)
                nc.vector.tensor_scalar(away[0:P], g.iota[0:P, 0:T], float(NE * CS * 128), None, ALU.add)
                nc.vector.tensor_scalar(low[0:P, 0, 0:1], g.iota_p[0:P, :], float(T), None, ALU.mult)
                dve.drain()
                nc.vector.scalar_tensor_tensor(out=slot[0:P], in0=best[0:P], scalar=float(CS * 128), in1=pos[0:P],
                                               op0=ALU.mult, op1=ALU.add)
                nc.vector.tensor_scalar(away[0:P], away[0:P], low[0:P, 0, 0:1], None, ALU.add)
                nc.vector.tensor_tensor(total[0:P], total[0:P], kept[0:P], ALU.mult)
                dve.drain()
                nc.vector.tensor_copy(back[0:P], slot[0:P])
                nc.vector.tensor_tensor(pos[0:P], slot[0:P], away[0:P], ALU.subtract)
                dve.drain()
                nc.vector.tensor_tensor(pos[0:P], pos[0:P], kept[0:P], ALU.mult)
                dve.drain()
                nc.vector.tensor_tensor(to[0:P], pos[0:P], away[0:P], ALU.add).then_inc(placed, 1)

            @block.gpsimd
            def _(pool):
                pool.wait_ge(placed, 1)
                for t in range(T):
                    pool.indirect_dma_start(out=g.bins[:, :],
                                            out_offset=bass.IndirectOffsetOnAxis(ap=to[0:P, t:t + 1], axis=0),
                                            in_=g.XN[0:P, t, :], in_offset=None).then_inc(scattered, 16)
                pool.wait_ge(scattered, done)

        with ExitStack() as sub:
            sb1, ps1, sem1 = bufs(nc, sub, "f3e")
            w1, w2 = sb1("w1", [128, 2, K2, F]), sb1("w2", [128, 2, KF, D])
            b1, b2 = sb1("b1", [128, NE, KF]), sb1("b2", [128, 2, D])
            xs, xT = sb1("xs", [128, 2, CS, D]), sb1("xT", [128, K2, CS * 128])
            hT, ys = sb1("hT", [128, KF, CS * 128]), sb1("ys", [128, 2, CS, D])
            pT, pH, pY = (ps1(m, [128, 2, 512]) for m in ("pT", "pH", "pY"))
            b_loaded = sem1("b_loaded")
            loaded, stored = [sem1(f"loaded{j}") for j in range(2)], [sem1(f"stored{j}") for j in range(2)]
            x_turned, x_read, h_made, h_read, y_made, y_put, used = (
                sem1(m) for m in ("x_turned", "x_read", "h_made", "h_read", "y_made", "y_put", "used"))
            bins = g.bins[0:NE * CS * 128, :].rearrange("(e s p) d -> e p s d", p=128, s=CS)
            results = g.results[0:NE * CS * 128, :].rearrange("(e s p) d -> e p s d", p=128, s=CS)
            block = sub.enter_context(stage(nc, g))

            @block.sync
            def _(sp):
                with nc.allow_non_contiguous_dma("the biases, once"):
                    for e in range(NE):
                        sp.dma_start(b1[:, e, :], a["L3_ffn_b1"][e].rearrange("(k p) -> p k", p=128)).then_inc(b_loaded, 16)
                sp.sem_inc(used, 2)
                with sp.Fori(0, NE // 2) as i:
                    for j in range(2):
                        ex = bass.ds(2 * i + j, 1)
                        sp.wait_ge(used, 2 * i + j + 1)
                        sp.dma_start(xs[:, j, :, :], bins[ex].rearrange("a p s d -> p (a s) d")).then_inc(loaded[j], 16)
                        sp.dma_start(w1[:, j, :, :], a["L3_ffn_w1"][ex].rearrange("a (k p) n -> p (a k) n", p=128)).then_inc(loaded[j], 16)
                        sp.dma_start(w2[:, j, :, :], a["L3_ffn_w2"][ex].rearrange("a (k p) n -> p (a k) n", p=128)).then_inc(loaded[j], 16)
                        sp.dma_start(b2[:, j, :], a["L3_ffn_b2"][ex, :].rearrange("a n -> (a n)").partition_broadcast(128)).then_inc(loaded[j], 16)

            @block.tensor
            def _(pe):
                with pe.Fori(0, NE // 2) as i:
                    for j in range(2):
                        n = 2 * i + j
                        pe.wait_ge(loaded[j], (i + 1) * 64)
                        for k in range(K2):
                            for s in range(CS):
                                last = nc.tensor.transpose(pT[:, k, s * 128:(s + 1) * 128], xs[:, j, s, k * 128:(k + 1) * 128], g.ident[:, :])
                            last.then_inc(x_turned, 1)
                        pe.wait_ge(x_read, 2 * n + 2)
                        for f in range(KF):
                            pe.wait_ge(h_read, n * KF + f + 1)
                            for k in range(K2):
                                last = nc.tensor.matmul(pH[:, f % 2, :], w1[:, j, k, f * 128:(f + 1) * 128], xT[:, k, :],
                                                        start=(k == 0), stop=(k == K2 - 1))
                            last.then_inc(h_made, 1)
                        pe.wait_ge(h_read, (n + 1) * KF + 2)
                        for s in range(CS):
                            pe.wait_ge(y_put, n * CS + s + 1)
                            for f in range(KF):
                                last = nc.tensor.matmul(pY[:, s % 2, 0:D], hT[:, f, s * 128:(s + 1) * 128], w2[:, j, f, :],
                                                        start=(f == 0), stop=(f == KF - 1))
                            last.then_inc(y_made, 1)

            @block.scalar
            def _(act):
                act.wait_ge(b_loaded, 16 * NE)
                act.sem_inc(h_read, 2)
                with act.Fori(0, NE // 2) as i:
                    for j in range(2):
                        n = 2 * i + j
                        for k in range(K2):
                            act.wait_ge(x_turned, 2 * n + k + 1)
                            nc.scalar.copy(xT[:, k, :], pT[:, k, :]).then_inc(x_read, 1)
                        for f in range(KF):
                            act.wait_ge(h_made, n * KF + f + 1)
                            nc.scalar.activation(hT[:, f, :], pH[:, f % 2, :], ACT.Relu,
                                                 bias=row(b1, n, f, f + 1, p=128)).then_inc(h_read, 1)
                        act.wait_ge(y_put, (n + 1) * CS + 2)
                        act.dma_start(results[bass.ds(n, 1)].rearrange("a p s d -> p (a s) d"), ys[:, j, :, :]).then_inc(stored[j], 16)
                for j in range(2):
                    act.wait_ge(stored[j], 16 * (NE // 2 + 1))

            @block.vector
            def _(dve):
                dve.sem_inc(y_put, 2)
                for j in range(2):
                    dve.sem_inc(stored[j], 16)
                with dve.Fori(0, NE // 2) as i:
                    for j in range(2):
                        n = 2 * i + j
                        dve.wait_ge(stored[j], (i + 1) * 16)
                        for s in range(CS):
                            dve.wait_ge(y_made, n * CS + s + 1)
                            nc.vector.tensor_tensor(ys[:, j, s, :], pY[:, s % 2, 0:D], b2[:, j, :], ALU.add).then_inc(y_put, 1)
                        dve.drain().then_inc(used, 1)

        with ExitStack() as sub:
            sb1, ps1, sem1 = bufs(nc, sub, "f3y")
            Y, flag, const = sb1("Y", [128, T, D]), sb1("flag", [128, T, D], I32), sb1("const", [128, 3])
            GROUPED = T // G
            gathered, done = g.moved[0:GROUPED], [g.count(c, 16 * G) for c in range(GROUPED)]
            block = sub.enter_context(stage(nc, g))

            @block.gpsimd
            def _(pool):
                for t in range(T):
                    pool.indirect_dma_start(out=Y[0:P, t, :], out_offset=None, in_=g.results[:, :],
                                            in_offset=bass.IndirectOffsetOnAxis(ap=back[0:P, t:t + 1], axis=0)
                                            ).then_inc(gathered[t // G], 16)

            @block.vector
            def _(dve):
                for k, value in enumerate((0.0, 1e4, -1e4)):
                    nc.vector.memset(const[:, k:k + 1], value)
                largest = 3.4028234663852886e38
                for c in range(GROUPED):
                    dve.wait_ge(gathered[c], done[c])
                    tiles = slice(c * G, (c + 1) * G)
                    y, f, x = Y[0:P, tiles], flag[0:P, tiles], g.X[0:P, tiles]
                    nc.vector.tensor_tensor(y, y, deep(total[0:P, tiles], P, G, D), ALU.mult)
                    dve.drain()
                    nc.vector.tensor_tensor(f, y, y, ALU.not_equal)
                    dve.drain()
                    for k in range(3):
                        if k:
                            nc.vector.tensor_scalar(f, y, largest if k == 1 else -largest, None,
                                                    ALU.is_gt if k == 1 else ALU.is_lt)
                            dve.drain()
                        nc.vector.copy_predicated(y, f, const[0:P, k:k + 1].rearrange("p (a b) -> p a b", a=1).broadcast_to([P, G, D]))
                        dve.drain()
                    nc.vector.tensor_tensor(x, x, y, ALU.add)


def build(nc, a, out, stop=99):
    with ExitStack() as ctx:
        def sb(name, shape, dt=F32):
            return ctx.enter_context(nc.sbuf_tensor(name, shape, dt))

        def dram(name, shape, dt=F32):
            return nc.dram_tensor(name, shape, dt, kind="Internal").ap()

        g = Shared()
        g.X = sb("X", [128, T, D])
        g.XN = sb("XN", [128, T, D])
        g.ident = sb("ident", [128, 128])
        g.tri = sb("tri", [128, 128])
        g.iota = sb("iota", [128, ST])
        g.iota_p = sb("iota_p", [128, 1])
        g.ones = sb("ones", [128, ST])
        g.zeros = sb("zeros", [128, 264])
        g.slots = sb("slots", [128, ST + R // 2, 4])
        g.kmap = sb("kmap", [1, ST], I32)
        g.dinv1 = sb("dinv1", [128, T])
        g.dinv2 = sb("dinv2", [128, T])
        g.slots_dram = dram("slots_dram", (128 * (ST + ET - EC), 4))
        g.table260 = dram("table260", (N, D + 4))
        g.table4 = dram("table4", (N, 4))
        g.table64 = dram("table64", (N, 64))
        g.table128 = dram("table128", (N, 128))
        g.table256 = dram("table256", (N, D))
        g.relations = dram("relations", (8 * N, D))
        g.bins = dram("bins", (66 * 128, D))
        g.results = dram("results", (64 * 128, D))
        g.moved = [ctx.enter_context(nc.semaphore(f"moved{j}")) for j in range(R)]
        sent = [0] * R

        def count(j, n):
            sent[j] += n
            return sent[j]

        g.count = count
        g.block, g.phase = None, 0
        g.cleared, g.w_loaded, g.tables_stored = (
            ctx.enter_context(nc.semaphore(m)) for m in ("cleared", "w_loaded", "tables_stored"))
        g.phase_done = ctx.enter_context(nc.semaphore("phase_done"))
        constants(nc, g, a["x"])
        with ExitStack() as early:
            g.rec = early.enter_context(nc.sbuf_tensor("rec", [128, ET, 4], F32))
            g.rec_row = early.enter_context(nc.sbuf_tensor("rec_row", [128, ET], I32))
            prepare_graph(nc, g, a["src"], a["dst"], a["edge_type_8"], a["edge_weight"])
            with nc.Block() as block:
                g.block = block
                scatter_edges(nc, g, 0, ET // 4)
                layer0_gnn(nc, g, a)
                scatter_edges(nc, g, ET // 4, ET)
                layer0_ffn(nc, g, a)
            g.block = None
        load_slots(nc, g)
        clear_semaphores(nc)
        with ExitStack() as early:
            NE, _, F = a["L1_ffn_w1"].shape
            g.w1 = early.enter_context(nc.sbuf_tensor("w1", [128, NE * K2 * F], F32))
            g.w2 = early.enter_context(nc.sbuf_tensor("w2", [128, NE * F // 128 * D], F32))
            load_expert_weights(nc, g, a)
            layer1_gnn(nc, g, a)
            clear_semaphores(nc)
            layer1_ffn(nc, g, a)
            clear_semaphores(nc)
        for layer in (layer2_gnn, layer2_ffn, layer3_gnn, layer3_ffn)[:max(0, stop - 4)]:
            layer(nc, g, a)
            clear_semaphores(nc)
        store(nc, g, "out", out, g.X, D)


TURNED = ("L0_ffn_W_x", "L2_gnn_W6", "L2_gnn_W7", "L2_gnn_Wp", "L3_gnn_weight")
STOP = 99

def kernel(**inputs):
    import numpy as np
    import concourse.bacc as bacc
    from concourse.bass_utils import run_bass_kernel_spmd as run

    nc = bacc.Bacc("TRN2", target_bir_lowering=False, num_devices=1)
    arrays, args = {}, {}
    for name, value in inputs.items():
        v = np.ascontiguousarray(value)
        if name in TURNED:
            v = np.ascontiguousarray(np.swapaxes(v, -1, -2))
        arrays[f"in_{name}"] = v
        args[name] = nc.dram_tensor(f"in_{name}", v.shape, mybir.dt.from_np(v.dtype), kind="ExternalInput").ap()
    out = nc.dram_tensor("out_x", (N, D), F32, kind="ExternalOutput").ap()
    build(nc, args, out, STOP)
    return run(nc, [arrays], core_ids=[0]).results[0]["out_x"]
```

```python
from contextlib import ExitStack, contextmanager

import concourse.bass as bass
from concourse import mybir

F32 = mybir.dt.float32
I32 = mybir.dt.int32
BF16 = mybir.dt.bfloat16
ALU = mybir.AluOpType
ACT = mybir.ActivationFunctionType
AX = mybir.AxisListType.X

N = 3125
T = 25
P = N // T
D = 256
K2 = D // 128
E = 50000
EC = E // 128
EREST = E - 128 * EC
U = 8
ET = -(-(EC + 1) // U) * U
R = 16
ST = -(-((E + T * 127) // 128) // R) * R
G = 5
EPS = 1e-5
ROUND = 12582912.0
BIG = 1e30


class Shared:
    pass


def row(a, i, lo=None, hi=None, p=P):
    lo, hi = lo or 0, hi if hi is not None else a.shape[2]
    return a[0:p, bass.ds(i, 1), lo:hi].rearrange("p a d -> p (a d)")


def wide(a, p, k, n):
    return a.rearrange("p (a n) -> p a n", a=1).broadcast_to([p, k, n])


def deep(a, p, k, n):
    return a.rearrange("p (k a) -> p k a", a=1).broadcast_to([p, k, n])


def hold(eng, sem, value, turn):
    eng.wait_ge(sem, value)
    eng.sem_inc(turn, 1)


def load_keys(nc, engine, kmap, at, n, keys):
    _, values = nc.values_load_multi_w_load_instructions(
        kmap[0:1, bass.ds(at, n)], engines=(engine,), min_val=0, max_val=keys - 1,
        skip_runtime_bounds_check_because="counting_sort makes keys of 0..keys-1")
    return values


@contextmanager
def stage(nc, g):
    if g.block is None:
        with nc.Block() as block:
            yield block
        return
    yield g.block
    g.phase += 1
    everyone = 4 * g.phase

    def leave(eng):
        eng.drain().then_inc(g.phase_done, 1)
        eng.wait_ge(g.phase_done, everyone)

    for engine in (g.block.sync, g.block.scalar, g.block.tensor, g.block.vector):
        engine(leave)


def bufs(nc, ctx, tag):
    def sb(name, shape, dt=F32):
        return ctx.enter_context(nc.sbuf_tensor(f"{tag}_{name}", shape, dt))

    def ps(name, shape, dt=F32):
        return ctx.enter_context(nc.psum_tensor(f"{tag}_{name}", shape, dt))

    def sem(name):
        return ctx.enter_context(nc.semaphore(f"{tag}_{name}"))

    return sb, ps, sem



def constants(nc, g, x_dram):
    with ExitStack() as ctx:
        sb, ps, sem = bufs(nc, ctx, "const")
        loaded, filled, shaped = sem("loaded"), sem("filled"), sem("shaped")
        block = ctx.enter_context(stage(nc, g))

        @block.sync
        def _(sp):
            sp.dma_start(g.X[0:P], x_dram.rearrange("(p t) d -> p t d", p=P)).then_inc(loaded, 16)
            sp.wait_ge(loaded, 16)

        @block.gpsimd
        def _(pool):
            pool.memset(g.ident[:, :], 0.0).then_inc(filled, 1)
            pool.memset(g.tri[:, :], 1.0).then_inc(filled, 1)
            pool.iota(g.iota[:, :], pattern=[[1, ST]], base=0, channel_multiplier=0,
                      allow_small_or_imprecise_dtypes=True)
            pool.iota(g.iota_p[:, :], pattern=[[1, 1]], base=0, channel_multiplier=1,
                      allow_small_or_imprecise_dtypes=True)
            pool.wait_ge(filled, 2)
            pool.affine_select(out=g.ident[:, :], in_=g.ident[:, :], compare_op=ALU.not_equal, fill=1.0,
                               base=0, pattern=[[-1, 128]], channel_multiplier=1).then_inc(shaped, 1)
            pool.affine_select(out=g.tri[:, :], in_=g.tri[:, :], compare_op=ALU.is_gt, fill=0.0,
                               base=0, pattern=[[1, 128]], channel_multiplier=-1).then_inc(shaped, 1)
            pool.wait_ge(shaped, 2)

        @block.vector
        def _(dve):
            nc.vector.memset(g.ones[:, :], 1.0)
            nc.vector.memset(g.zeros[:, :], 0.0)


def clear_semaphores(nc):
    free = sorted(nc.free_semaphores)
    with nc.Block() as block:
        @block.gpsimd
        def _(pool):
            pool.sem_clear(range(free[0], free[-1] + 1))



class Norm:
    DVE_TILES = T // 2 + 1

    def __init__(self, nc, sb, sem, src, dst):
        self.nc, self.src, self.dst = nc, src, dst
        self.st = sb("st", [128, T, 6])
        self.mean, self.spread, self.var, self.std, self.rstd, self.shift = (
            sb(n, [128, T]) for n in ("mean", "spread", "var", "std", "rstd", "shift"))
        self.var_ready, self.std_ready, self.shift_ready, self.by_dve, self.by_act = (
            sem(n) for n in ("var_ready", "std_ready", "shift_ready", "by_dve", "by_act"))

    def start_dve(self, dve):
        nc, st, mean, spread, var = self.nc, self.st, self.mean, self.spread, self.var
        for t in range(T):
            nc.vector.bn_stats(st[0:P, t, :], self.src[0:P, t, :])
        dve.drain()
        nc.vector.tensor_tensor(mean[0:P], st[0:P, :, 1], st[0:P, :, 4], ALU.add)
        nc.vector.tensor_tensor(spread[0:P], st[0:P, :, 1], st[0:P, :, 4], ALU.subtract)
        nc.vector.tensor_tensor(var[0:P], st[0:P, :, 2], st[0:P, :, 5], ALU.add)
        dve.drain()
        nc.vector.tensor_scalar(mean[0:P], mean[0:P], 0.5, None, ALU.mult)
        nc.vector.tensor_tensor(spread[0:P], spread[0:P], spread[0:P], ALU.mult)
        nc.vector.tensor_scalar(var[0:P], var[0:P], 1.0 / D, EPS, ALU.mult, ALU.add)
        dve.drain()
        nc.vector.scalar_tensor_tensor(out=var[0:P], in0=spread[0:P], scalar=0.25, in1=var[0:P],
                                       op0=ALU.mult, op1=ALU.add).then_inc(self.var_ready, 1)
        dve.wait_ge(self.std_ready, 1)
        nc.vector.reciprocal(self.rstd[0:P], self.std[0:P])
        dve.drain()
        nc.vector.scalar_tensor_tensor(out=self.shift[0:P], in0=mean[0:P], scalar=-1.0, in1=self.rstd[0:P],
                                       op0=ALU.mult, op1=ALU.mult).then_inc(self.shift_ready, 1)

    def tile_dve(self, t):
        self.nc.vector.tensor_scalar(self.dst[0:P, t, :], self.src[0:P, t, :], self.mean[0:P, t:t + 1],
                                     self.rstd[0:P, t:t + 1], ALU.subtract, ALU.mult).then_inc(self.by_dve, 1)

    def start_act(self, act):
        act.wait_ge(self.var_ready, 1)
        self.nc.scalar.activation(self.std[0:P], self.var[0:P], ACT.Sqrt).then_inc(self.std_ready, 1)
        act.wait_ge(self.shift_ready, 1)

    def tile_act(self, t):
        self.nc.scalar.activation(self.dst[0:P, t, :], self.src[0:P, t, :], ACT.Identity, bias=self.shift[0:P, t:t + 1],
                                  scale=self.rstd[0:P, t:t + 1]).then_inc(self.by_act, 1)

    def wait_tile(self, eng, t):
        if t < self.DVE_TILES:
            eng.wait_ge(self.by_dve, t + 1)
        else:
            eng.wait_ge(self.by_act, t - self.DVE_TILES + 1)


def layer_norm(nc, g, tag, src, dst):
    with ExitStack() as ctx:
        sb, ps, sem = bufs(nc, ctx, tag)
        norm = Norm(nc, sb, sem, src, dst)
        block = ctx.enter_context(stage(nc, g))

        @block.vector
        def _(dve):
            norm.start_dve(dve)
            for t in range(norm.DVE_TILES):
                norm.tile_dve(t)

        @block.scalar
        def _(act):
            norm.start_act(act)
            for t in range(norm.DVE_TILES, T):
                norm.tile_act(t)



def linear(nc, g, tag, src, width, w_dram, bias_dram, nout, finish, prepare=None, turn=None, table=None,
           norm_of=None):
    kc = [min(128, width - k) for k in range(0, width, 128)]
    nk, rows = len(kc), kc[0]
    SKEW, BANKS, PLACES = 2, 3, 4
    with ExitStack() as ctx:
        sb, ps, sem = bufs(nc, ctx, tag)
        in_sbuf = w_dram.shape[0] == 128 and len(w_dram.shape) == 3
        w = w_dram if in_sbuf else sb("w", [128, nk, nout])
        bias = sb("bias", [128, nout]) if bias_dram is not None else None
        function, scale_dram, shift_dram = turn or (ACT.Copy, None, None)
        columns = sb("columns", [128, 2, nk]) if turn else None
        xT = sb("xT", [128, PLACES, nk, P])
        psT = ps("psT", [128, BANKS, 512])
        psO = ps("psO", [128, BANKS, 512])
        w_loaded, b_loaded, c_loaded, prepared = (sem(m) for m in ("w_loaded", "b_loaded", "c_loaded", "prepared"))
        turned, turn_read, multiplied, put_away = (sem(m) for m in ("turned", "turn_read", "multiplied", "put_away"))
        stored = sem("stored")
        norm = Norm(nc, sb, sem, norm_of, src) if norm_of is not None else None
        block = ctx.enter_context(stage(nc, g))

        @block.sync
        def _(sp):
            column_loads = 0
            with nc.allow_non_contiguous_dma("a few hundred values"):
                for k, dram in enumerate((scale_dram, shift_dram)):
                    if dram is not None:
                        sp.dma_start(columns[0:rows, k, :], dram.rearrange("(k p) -> p k", p=rows)).then_inc(c_loaded, 16)
                        column_loads += 1
            if not in_sbuf:
                sp.dma_start(w[0:rows], w_dram.rearrange("(k p) n -> p k n", p=rows)).then_inc(w_loaded, 16)
            if bias is not None:
                sp.dma_start(bias[:, :], bias_dram.partition_broadcast(128)).then_inc(b_loaded, 16)
            if table is not None:
                out = table[0].rearrange("(p t) d -> p t d", p=P)
                for t in range(0, T, G):
                    sp.wait_ge(put_away, t + G)
                    sp.dma_start(out[:, t:t + G, :], table[1][0:P, t:t + G, 0:nout]).then_inc(stored, 16)
                sp.wait_ge(stored, 16 * (T // G))
            for loads, loaded in ((column_loads, c_loaded), (not in_sbuf, w_loaded), (bias is not None, b_loaded)):
                if loads:
                    sp.wait_ge(loaded, 16 * loads)

        @block.tensor
        def _(pe):
            if prepare is not None:
                pe.wait_ge(prepared, 1)
            for t in range(T + SKEW):
                if t < T:
                    if t >= BANKS:
                        pe.wait_ge(turn_read, t - BANKS + 1)
                    if norm is not None:
                        norm.wait_tile(pe, t)
                    for k in range(nk):
                        last = nc.tensor.transpose(psT[0:kc[k], t % BANKS, k * P:(k + 1) * P],
                                                   src[0:P, t, k * 128:k * 128 + kc[k]], g.ident[0:P, 0:P])
                    last.then_inc(turned, 1)
                m = t - SKEW
                if m >= 0:
                    if m == 0 and not in_sbuf:
                        pe.wait_ge(w_loaded, 16)
                    pe.wait_ge(turn_read, m + 1)
                    if m >= BANKS:
                        pe.wait_ge(put_away, m - BANKS + 1)
                    for k in range(nk):
                        last = nc.tensor.matmul(psO[0:P, m % BANKS, 0:nout], xT[0:kc[k], m % PLACES, k, :],
                                                w[0:kc[k], k, :], start=(k == 0), stop=(k == nk - 1))
                    last.then_inc(multiplied, 1)

        @block.scalar
        def _(act):
            if norm is not None:
                norm.start_act(act)
            if turn:
                act.wait_ge(c_loaded, 16 * ((scale_dram is not None) + (shift_dram is not None)))
            for t in range(T):
                if norm is not None and norm.DVE_TILES + t < T:
                    norm.tile_act(norm.DVE_TILES + t)
                act.wait_ge(turned, t + 1)
                if t >= PLACES:
                    act.wait_ge(multiplied, t - PLACES + 1)
                if turn:
                    for k in range(nk):
                        last = nc.scalar.activation(xT[0:rows, t % PLACES, k, :], psT[0:rows, t % BANKS, k * P:(k + 1) * P], function,
                                                    bias=columns[0:rows, 1, k:k + 1],
                                                    scale=columns[0:rows, 0, k:k + 1] if scale_dram is not None else 1.0)
                else:
                    last = nc.scalar.copy(xT[0:rows, t % PLACES, :, :], psT[0:rows, t % BANKS, 0:nk * P].rearrange(
                        "p (k r) -> p k r", k=nk))
                last.then_inc(turn_read, 1)

        @block.vector
        def _(dve):
            if prepare is not None:
                prepare(dve)
                dve.drain().then_inc(prepared, 1)
            if norm is not None:
                norm.start_dve(dve)
                for t in range(norm.DVE_TILES):
                    norm.tile_dve(t)
            if bias is not None:
                dve.wait_ge(b_loaded, 16)
            for t in range(T):
                dve.wait_ge(multiplied, t + 1)
                finish(dve, t, psO[0:P, t % BANKS, 0:nout], bias).then_inc(put_away, 1)



def counting_sort(nc, g, tag, key, p, keys, n, pos, hot, base=None, kmap=None, slots=0, tiles=None, beside=None):
    with ExitStack() as ctx:
        sb, ps, sem = bufs(nc, ctx, tag)
        seen = sb("seen", [128, keys, n])
        total = sb("total", [128, keys])
        nt, ends, starts, off = (sb(m, [128, keys]) for m in ("nt", "ends", "starts", "off"))
        pE, pC = ps("pE", [128, 512]), ps("pC", [128, 512])
        counted, summed, hot_made = sem("counted"), sem("summed"), sem("hot_made")
        block = ctx.enter_context(stage(nc, g))

        @block.vector
        def _(dve):
            nc.vector.tensor_tensor(hot[0:p], wide(key[0:p, 0:n], p, keys, n),
                                    deep(g.iota[0:p, 0:keys], p, keys, n), ALU.is_equal).then_inc(hot_made, 1)
            dve.drain()
            for k in range(keys):
                nc.vector.tensor_tensor_scan(seen[0:p, k, :], g.ones[0:p, 0:n], hot[0:p, k, :], 0.0,
                                             ALU.mult, ALU.add)
            dve.drain()
            nc.vector.tensor_copy(total[0:p], seen[0:p, :, n - 1]).then_inc(counted, 1)
            dve.wait_ge(summed, 1)
            nc.vector.tensor_scalar(off[0:p], pE[0:p, 0:keys], -1.0, None, ALU.add)
            if base is None:
                nc.vector.tensor_scalar(nt[0:p], pC[0:p, 0:keys], 1.0 / 128, 63.5 / 128, ALU.mult, ALU.add)
                dve.drain()
                nc.vector.tensor_scalar(nt[0:p], nt[0:p], ROUND, None, ALU.add)
                dve.drain()
                nc.vector.tensor_scalar(nt[0:p], nt[0:p], -ROUND, None, ALU.add)
                dve.drain()
                nc.vector.tensor_tensor_scan(ends[0:p], g.ones[0:p, 0:keys], nt[0:p], 0.0, ALU.mult, ALU.add)
                nc.vector.memset(tiles[0:1, :], -1.0)
                dve.drain()
                nc.vector.tensor_tensor(starts[0:p], ends[0:p], nt[0:p], ALU.subtract)
                dve.drain()
                nc.vector.scalar_tensor_tensor(out=off[0:p], in0=starts[0:p], scalar=128.0, in1=off[0:p],
                                               op0=ALU.mult, op1=ALU.add)
                for k in range(keys):
                    nc.vector.scalar_tensor_tensor(out=tiles[0:1, :], in0=g.iota[0:1, 0:slots],
                                                   scalar=starts[0:1, k:k + 1], in1=tiles[0:1, :],
                                                   op0=ALU.is_ge, op1=ALU.add)
                    dve.drain()
                nc.vector.tensor_copy(kmap[0:1, 0:slots], tiles[0:1, :])
            dve.drain()
            for k in range(keys):
                nc.vector.scalar_tensor_tensor(out=seen[0:p, k, :], in0=seen[0:p, k, :], scalar=off[0:p, k:k + 1],
                                               in1=hot[0:p, k, :], op0=ALU.add, op1=ALU.mult)
            dve.drain()
            nc.vector.tensor_reduce(pos[0:p, 0:n], seen[0:p].rearrange("p k n -> p n k"), AX, ALU.add)

        @block.gpsimd
        def _(pool):
            if beside is not None:
                pool.wait_ge(hot_made, 1)
                beside(pool)

        @block.tensor
        def _(pe):
            pe.wait_ge(counted, 1)
            nc.tensor.matmul(pE[0:p, 0:keys], g.tri[0:p, 0:p], total[0:p], start=True, stop=True)
            nc.tensor.matmul(pC[0:p, 0:keys], g.ones[0:p, 0:p], total[0:p], start=True,
                             stop=True).then_inc(summed, 1)



def scatter_edges(nc, g, first, last):
    @g.block.gpsimd
    def _(pool):
        for c in range(first, last):
            pool.indirect_dma_start(out=g.slots_dram[:, :],
                                    out_offset=bass.IndirectOffsetOnAxis(ap=g.rec_row[:, c:c + 1], axis=0),
                                    in_=g.rec[:, c, :], in_offset=None).then_inc(g.moved[1], 16)
        if last == ET:
            g.scattered = g.count(1, 16 * ET)
            pool.wait_ge(g.moved[1], g.scattered)


def load_slots(nc, g):
    @g.block.sync
    def _(sp):
        sp.wait_ge(g.moved[1], g.scattered)
        sp.dma_start(g.slots[:, 0:ST, :], g.slots_dram[0:128 * ST, :].rearrange(
            "(p t) f -> p t f", p=128)).then_inc(g.slots_back, 16)


def prepare_graph(nc, g, src, dst, etype, eweight):
    with ExitStack() as ctx:
        sb, ps, sem = bufs(nc, ctx, "edges")
        raw = sb("raw", [128, 3, ET], I32)
        rec = g.rec
        PARTS = 4
        hot = sb("hot", [128, PARTS, T, ET], BF16)
        part, rest = sb("part", [128, PARTS - 1, ET], BF16), sb("rest", [128, ET])
        key, pos, pad, tmp = (sb(m, [128, ET]) for m in ("key", "pos", "pad", "tmp"))
        tiles = sb("tiles", [128, ST])
        padrow = sb("padrow", [128, 1])
        cleared, loaded, blank, filled = sem("cleared"), sem("loaded"), sem("blank"), sem("filled")

        with stage(nc, g) as block:
            @block.vector
            def _(dve):
                nc.vector.memset(raw[:, :, :], 0).then_inc(cleared, 1)
                nc.vector.memset(rec[:, :, :], 0.0).then_inc(cleared, 1)
                nc.vector.memset(g.slots[:, :, :], 0.0)
                dve.drain()
                nc.vector.memset(g.slots[:, :, 1], -1.0).then_inc(blank, 1)
                nc.vector.memset(pad[:, :], 0.0)
                dve.drain()
                nc.vector.memset(pad[:, EC + 1:ET], 1.0)
                nc.vector.tensor_scalar(pad[:, EC:EC + 1], g.iota_p[:, :], float(EREST), None, ALU.is_ge)

            @block.sync
            def _(sp):
                sp.wait_ge(cleared, 2)
                for k, a in enumerate((src, dst, etype)):
                    sp.dma_start(raw[:, k, 0:EC], a[0:128 * EC].rearrange("(p t) -> p t", p=128)).then_inc(loaded, 16)
                    sp.dma_start(raw[0:EREST, k, EC:EC + 1],
                                 a[128 * EC:E].rearrange("(p t) -> p t", t=1)).then_inc(loaded, 16)
                sp.dma_start(tmp[:, 0:EC], eweight[0:128 * EC].rearrange("(p t) -> p t", p=128)).then_inc(loaded, 16)
                sp.dma_start(rec[0:EREST, EC, 2:3], eweight[128 * EC:E].rearrange("(p t) -> p t", t=1)).then_inc(loaded, 16)
                sp.wait_ge(blank, 1)
                sp.dma_start(g.slots_dram[0:128 * ST, :].rearrange("(p t) f -> p t f", p=128),
                             g.slots[:, 0:ST, :]).then_inc(filled, 16)
                sp.wait_ge(loaded, 128)
                sp.wait_ge(filled, 16)
                sp.dma_start(g.bins.rearrange("(p r) d -> p r d", p=128),
                             wide(g.zeros[:, 0:D], 128, g.bins.shape[0] // 128, D)).then_inc(g.cleared, 16)

        with stage(nc, g) as block:
            @block.vector
            def _(dve):
                nc.vector.tensor_copy(rec[:, 0:EC, 2], tmp[:, 0:EC])
                nc.vector.tensor_copy(rec[:, :, 0], raw[:, 0, :])
                nc.vector.tensor_copy(key[:, :], raw[:, 1, :])
                nc.vector.tensor_copy(rec[:, :, 3], raw[:, 2, :])
                dve.drain()
                nc.vector.scalar_tensor_tensor(out=rec[:, :, 3], in0=rec[:, :, 3], scalar=float(N),
                                               in1=rec[:, :, 0], op0=ALU.mult, op1=ALU.add)
                nc.vector.tensor_scalar(tmp[:, :], key[:, :], 1.0 / T, -(T // 2) / T, ALU.mult, ALU.add)
                dve.drain()
                nc.vector.tensor_scalar(tmp[:, :], tmp[:, :], ROUND, None, ALU.add)
                dve.drain()
                nc.vector.tensor_scalar(rec[:, :, 1], tmp[:, :], -ROUND, None, ALU.add)
                dve.drain()
                nc.vector.scalar_tensor_tensor(out=key[:, :], in0=rec[:, :, 1], scalar=-float(T),
                                               in1=key[:, :], op0=ALU.mult, op1=ALU.add)
                nc.vector.tensor_scalar(padrow[:, :], g.iota_p[:, :], float(128 * ST), None, ALU.add)
                dve.drain()
                for k in range(PARTS - 1):
                    value = rec[:, :, 2] if k == 0 else rest[:, :]
                    nc.vector.tensor_copy(part[:, k, :], value)
                    dve.drain()
                    if k < PARTS - 2:
                        nc.vector.tensor_tensor(rest[:, :], value, part[:, k, :], ALU.subtract)
                        dve.drain()
                nc.vector.scalar_tensor_tensor(out=key[:, :], in0=pad[:, :], scalar=100.0, in1=key[:, :],
                                               op0=ALU.mult, op1=ALU.add)

        weighted = sem("weighted")

        def weigh(pool):
            for k in range(PARTS - 1):
                last = nc.gpsimd.tensor_tensor(hot[:, k + 1], hot[:, 0], wide(part[:, k, :], 128, T, ET), ALU.mult)
            last.then_inc(weighted, 1)

        counting_sort(nc, g, "sort", key, 128, T, ET, pos, hot[:, 0], kmap=g.kmap, slots=ST, tiles=tiles, beside=weigh)

        ohl = sb("ohl", [128, 2, U, P], BF16)
        hots = sb("hots", [128, 2, U, PARTS * T], BF16)
        nothing = sb("nothing", [128, 128], BF16)
        pdeg = ps("pdeg", [128, 512])
        hot_ready, hot_used, opened, tiles_ready, cleared2 = (
            sem(m) for m in ("hot_ready", "hot_used", "opened", "tiles_ready", "cleared2"))
        with stage(nc, g) as block:
            @block.vector
            def _(dve):
                nc.vector.memset(nothing[:, :], 0.0).then_inc(cleared2, 1)
                nc.vector.tensor_scalar(tmp[:, :], pos[:, :], 1.0 / 128, -63.5 / 128, ALU.mult, ALU.add)
                dve.drain()
                nc.vector.tensor_scalar(tmp[:, :], tmp[:, :], ROUND, None, ALU.add)
                dve.drain()
                nc.vector.tensor_scalar(tmp[:, :], tmp[:, :], -ROUND, None, ALU.add)
                dve.drain()
                nc.vector.scalar_tensor_tensor(out=pos[:, :], in0=tmp[:, :], scalar=-128.0, in1=pos[:, :],
                                               op0=ALU.mult, op1=ALU.add)
                dve.drain()
                nc.vector.scalar_tensor_tensor(out=pos[:, :], in0=pos[:, :], scalar=float(ST), in1=tmp[:, :],
                                               op0=ALU.mult, op1=ALU.add)
                nc.vector.tensor_scalar(pad[:, :], pad[:, :], padrow[:, :], None, ALU.mult)
                dve.drain()
                for c in range(EC + 1, ET):
                    nc.vector.tensor_scalar(pad[:, c:c + 1], pad[:, c:c + 1], float(128 * (c - EC)), None, ALU.add)
                dve.drain()
                nc.vector.tensor_tensor(pos[:, :], pos[:, :], pad[:, :], ALU.add)
                dve.drain()
                nc.vector.tensor_copy(g.rec_row[:, :], pos[:, :])
                dve.sem_inc(hot_used, 2)
                iota = wide(g.iota[:, 0:P], 128, U, P)

                def one_hot(n, j):
                    dve.wait_ge(hot_used, n + 1)
                    nc.vector.tensor_tensor(ohl[:, j], iota, rec[:, bass.ds(n * U, U), 1:2].broadcast_to([128, U, P]),
                                            ALU.is_equal).then_inc(hot_ready, 1)

                one_hot(0, 0)
                with dve.Fori(0, ET // U // 2) as i:
                    one_hot(2 * i + 1, 1)
                    one_hot(2 * i + 2, 0)
                dve.wait_ge(opened, 1)
                nc.vector.tensor_scalar(g.dinv1[0:P], pdeg[0:P, 0:T], 1.0, 1e-12, ALU.add, ALU.max)
                nc.vector.tensor_reduce(g.dinv2[0:P], pdeg[0:P, T:PARTS * T].rearrange("p (a t) -> p t a", t=T), AX, ALU.add)
                dve.drain()
                nc.vector.tensor_scalar(g.dinv2[0:P], g.dinv2[0:P], 1.0, None, ALU.add)

            @block.scalar
            def _(act):
                act.wait_ge(weighted, 1)

                def stage_tiles(n, j):
                    act.wait_ge(hot_used, n + 1)
                    nc.scalar.copy(hots[:, j].rearrange("p u (a k) -> p a k u", a=PARTS),
                                   hot[:, :, :, bass.ds(n * U, U)]).then_inc(tiles_ready, 1)

                stage_tiles(0, 0)
                with act.Fori(0, ET // U // 2) as i:
                    stage_tiles(2 * i + 1, 1)
                    stage_tiles(2 * i + 2, 0)

            @block.tensor
            def _(pe):
                pe.wait_ge(cleared2, 1)
                nc.tensor.matmul(pdeg[0:P, 0:PARTS * T], nothing[:, 0:P], nothing[:, 0:PARTS * T], start=True, stop=False)

                def add_edges(n, j):
                    pe.wait_ge(hot_ready, n + 1)
                    pe.wait_ge(tiles_ready, n + 1)
                    for u in range(U):
                        last = nc.tensor.matmul(pdeg[0:P, 0:PARTS * T], ohl[:, j, u, :],
                                                hots[:, j, u, :],
                                                start=False, stop=False, skip_group_check=True)
                    last.then_inc(hot_used, 1)

                add_edges(0, 0)
                with pe.Fori(0, ET // U // 2) as i:
                    add_edges(2 * i + 1, 1)
                    add_edges(2 * i + 2, 0)
                nc.tensor.matmul(pdeg[0:P, 0:PARTS * T], nothing[:, 0:P], nothing[:, 0:PARTS * T], start=False,
                                 stop=True).then_inc(opened, 1)

        positive, d1, d2 = sb("positive", [128, T]), sem("d1"), sem("d2")
        with stage(nc, g) as block:
            @block.vector
            def _(dve):
                nc.vector.tensor_scalar(positive[0:P], g.dinv2[0:P], 0.0, None, ALU.is_gt)
                dve.drain()
                nc.vector.tensor_tensor(g.dinv2[0:P], g.dinv2[0:P], positive[0:P], ALU.mult)
                dve.drain()
                nc.vector.scalar_tensor_tensor(out=g.dinv2[0:P], in0=g.dinv2[0:P], scalar=1.0, in1=positive[0:P],
                                               op0=ALU.add, op1=ALU.subtract).then_inc(d1, 1)
                dve.wait_ge(d2, 2)
                nc.vector.reciprocal(g.dinv1[0:P], g.dinv1[0:P])
                nc.vector.reciprocal(g.dinv2[0:P], g.dinv2[0:P])
                dve.drain()
                nc.vector.tensor_tensor(g.dinv2[0:P], g.dinv2[0:P], positive[0:P], ALU.mult)

            @block.scalar
            def _(act):
                act.wait_ge(d1, 1)
                nc.scalar.activation(g.dinv1[0:P], g.dinv1[0:P], ACT.Sqrt).then_inc(d2, 1)
                nc.scalar.activation(g.dinv2[0:P], g.dinv2[0:P], ACT.Sqrt).then_inc(d2, 1)


def aggregate(nc, g, tag, acc, table, width, weighted=False, field=0, loads=()):
    AHEAD, BANKS = R // 2, 8
    with ExitStack() as ctx:
        sb, ps, sem = bufs(nc, ctx, tag)
        idx = sb("idx", [128, R], I32)
        got = sb("got", [128, R, width])
        hot = sb("hot", [128, R, P])
        pp = ps("pp", [128, BANKS, 512])
        staged, hot_ready, multiplied = sem("staged"), sem("hot_ready"), sem("multiplied")
        added, turn = sem("added"), sem("turn")
        gathered = g.moved
        before = [g.count(j, 16 * (ST // R)) - 16 * (ST // R) for j in range(R)]
        block = ctx.enter_context(stage(nc, g))

        @block.sync
        def _(sp):
            for k, load in enumerate(loads):
                sp.wait_ge(multiplied, R + ST * (2 * k + 1) // (2 * len(loads)))
                load(sp)

        @block.scalar
        def _(act):
            act.sem_inc(multiplied, R)
            with act.Fori(0, ST // R) as i:
                for j in range(R):
                    act.wait_ge(multiplied, i * R + j + 1)
                    nc.scalar.copy(idx[:, j:j + 1], row(g.slots, i * R + j, field, field + 1, p=128)).then_inc(staged, 1)

        @block.gpsimd
        def _(pool):
            with pool.Fori(0, ST // R) as i:
                for j in range(R):
                    hold(pool, staged, i * R + j + 1, turn)
                    pool.indirect_dma_start(out=got[:, j, :], out_offset=None, in_=table[:, :],
                                            in_offset=bass.IndirectOffsetOnAxis(ap=idx[:, j:j + 1], axis=0)
                                            ).then_inc(gathered[j], 16)

        @block.tensor
        def _(pe):
            pe.sem_inc(added, BANKS)
            with pe.Fori(0, ST // R) as i:
                for j in range(R):
                    pe.wait_ge(gathered[j], (i + 1) * 16 + before[j])
                    pe.wait_ge(hot_ready, i * R + j + 1)
                    pe.wait_ge(added, i * R + j + 1)
                    nc.tensor.matmul(pp[0:P, j % BANKS, 0:width], hot[:, j, :], got[:, j, :], start=True,
                                     stop=True).then_inc(multiplied, 1)

        def one_hot(n, j):
            dst = row(g.slots, n, 1, 2, p=128)
            if weighted:
                ins = nc.vector.tensor_scalar(hot[:, j, :], g.iota[:, 0:P], dst, row(g.slots, n, 2, 3, p=128),
                                              ALU.is_equal, ALU.mult)
            else:
                ins = nc.vector.tensor_scalar(hot[:, j, :], g.iota[:, 0:P], dst, None, ALU.is_equal)
            ins.then_inc(hot_ready, 1)

        @block.vector
        def _(dve):
            for j in range(AHEAD):
                one_hot(j, j)
            with dve.Fori(0, ST // R) as i:
                for j in range(R):
                    if j % 4 == 0:
                        tile4 = load_keys(nc, mybir.EngineType.DVE, g.kmap, i * R + j, 4, T)
                    k = tile4[j % 4]
                    dve.drain()
                    dve.wait_ge(multiplied, i * R + j + 1 + R)
                    part = row(acc, k, 0, width)
                    nc.vector.tensor_tensor(part, part, pp[0:P, j % BANKS, 0:width], ALU.add).then_inc(added, 1)
                    one_hot(i * R + j + AHEAD, (j + AHEAD) % R)


def store(nc, g, tag, dram, src, width, done=None, value=16):
    with ExitStack() as ctx:
        stored = done or ctx.enter_context(nc.semaphore(f"{tag}_stored"))
        block = ctx.enter_context(stage(nc, g))

        @block.sync
        def _(sp):
            sp.dma_start(dram.rearrange("(p t) d -> p t d", p=P), src[0:P, :, 0:width]).then_inc(stored, 16)
            sp.wait_ge(stored, value)



def layer0_gnn(nc, g, a):
    with ExitStack() as ctx:
        sb, ps, sem = bufs(nc, ctx, "l0g")
        XT = sb("XT", [128, T, D + 4])
        AL = sb("AL", [128, T, 4])
        prod = sb("prod", [128, T, D])
        att = sb("att", [128, 2, D])
        i_dst, i_src = sb("i_dst", [128, T], I32), sb("i_src", [128, T], I32)

        def put(dve, i, product, bias):
            return nc.vector.tensor_copy(row(XT, i, 0, D), product)

        linear(nc, g, "l0w", g.XN, D, a["L0_gnn_weight"], None, D, put, norm_of=g.X)

        att_loaded = sem("att_loaded")
        with stage(nc, g) as block:
            @block.sync
            def _(sp):
                sp.dma_start(att[:, 0, :], a["L0_gnn_attn_l"].rearrange("h d -> (h d)").partition_broadcast(128)).then_inc(att_loaded, 16)
                sp.dma_start(att[:, 1, :], a["L0_gnn_attn_r"].rearrange("h d -> (h d)").partition_broadcast(128)).then_inc(att_loaded, 16)
                sp.dma_start(i_src[0:P], a["src"][0:N].rearrange("(p t) -> p t", p=P)).then_inc(att_loaded, 16)
                sp.dma_start(i_dst[0:P], a["dst"][0:N].rearrange("(p t) -> p t", p=P)).then_inc(att_loaded, 16)
                sp.wait_ge(att_loaded, 64)

            @block.vector
            def _(dve):
                dve.wait_ge(att_loaded, 64)
                for k, out in ((0, AL[0:P]), (1, XT[0:P, :, D:D + 4])):
                    nc.vector.tensor_tensor(prod[0:P], XT[0:P, :, 0:D], wide(att[0:P, k, :], P, T, D), ALU.mult)
                    dve.drain()
                    nc.vector.tensor_reduce(out, prod[0:P].rearrange("p t (h d) -> p t h d", h=4), AX, ALU.add)
                    dve.drain()

        store(nc, g, "l0s", g.table260, XT, D + 4, g.tables_stored, 16)
        store(nc, g, "l0s2", g.table4, AL, 4, g.tables_stored, 32)
        gathered = g.moved[0]
        done = g.count(0, 32 * T)
        with stage(nc, g) as block:
            @block.gpsimd
            def _(pool):
                pool.wait_ge(att_loaded, 64)
                pool.wait_ge(g.tables_stored, 32)
                for t in range(T):
                    pool.indirect_dma_start(out=XT[0:P, t, :], out_offset=None, in_=g.table260[:, :],
                                            in_offset=bass.IndirectOffsetOnAxis(ap=i_dst[0:P, t:t + 1], axis=0)
                                            ).then_inc(gathered, 16)
                    pool.indirect_dma_start(out=AL[0:P, t, :], out_offset=None, in_=g.table4[:, :],
                                            in_offset=bass.IndirectOffsetOnAxis(ap=i_src[0:P, t:t + 1], axis=0)
                                            ).then_inc(gathered, 16)
                pool.wait_ge(gathered, done)

        small = sb("small", [128, 3, T])
        raw = sb("raw", [128, T, 4])
        centred, powers = sem("centred"), sem("powers")
        with stage(nc, g) as block:
            @block.vector
            def _(dve):
                dve.wait_ge(gathered, done)
                nc.vector.tensor_tensor(raw[0:P], AL[0:P], XT[0:P, :, D:D + 4], ALU.add)
                dve.drain()
                nc.vector.tensor_scalar(AL[0:P], raw[0:P], 0.01, None, ALU.mult)
                dve.drain()
                nc.vector.tensor_tensor(AL[0:P], AL[0:P], raw[0:P], ALU.max)
                dve.drain()
                nc.vector.tensor_reduce(small[0:P, 0], AL[0:P], AX, ALU.max)
                dve.drain()
                nc.vector.tensor_tensor(AL[0:P], AL[0:P], deep(small[0:P, 0], P, T, 4), ALU.subtract).then_inc(centred, 1)
                dve.wait_ge(powers, 1)
                nc.vector.tensor_reduce(small[0:P, 1], AL[0:P], AX, ALU.add)
                dve.drain()
                nc.vector.reciprocal(small[0:P, 2], small[0:P, 1])
                dve.drain()
                nc.vector.tensor_tensor(AL[0:P], AL[0:P], deep(small[0:P, 2], P, T, 4), ALU.mult)
                dve.drain()
                nc.vector.tensor_tensor(prod[0:P].rearrange("p t (h d) -> p t h d", h=4),
                                        XT[0:P, :, 0:D].rearrange("p t (h d) -> p t h d", h=4),
                                        AL[0:P].rearrange("p t (h a) -> p t h a", a=1).broadcast_to([P, T, 4, 64]), ALU.mult)
                dve.drain()
                nc.vector.tensor_reduce(XT[0:P, :, 0:64], prod[0:P].rearrange("p t (h d) -> p t d h", h=4), AX, ALU.add)
                dve.drain()
                nc.vector.tensor_tensor(g.X[0:P].rearrange("p t (h d) -> p t h d", h=4),
                                        g.X[0:P].rearrange("p t (h d) -> p t h d", h=4),
                                        XT[0:P, :, 0:64].rearrange("p t (a d) -> p t a d", a=1).broadcast_to([P, T, 4, 64]), ALU.add)

            @block.scalar
            def _(act):
                act.wait_ge(centred, 1)
                nc.scalar.activation(AL[0:P], AL[0:P], ACT.Exp).then_inc(powers, 1)

HEADS, GROUPS = 8, 64
C4 = HEADS * GROUPS // 128


def layer0_ffn(nc, g, a):
    with ExitStack() as ctx:
        sb, ps, sem = bufs(nc, ctx, "f0")
        SW = sb("SW", [128, T, HEADS * GROUPS])
        wxs = sb("wxs", [128, K2, HEADS * GROUPS])
        bxs = sb("bxs", [128, HEADS * GROUPS])
        M = sb("M", [128, C4, D])
        with ExitStack() as sub:
            sb1, ps1, sem1 = bufs(nc, sub, "f0a")
            wxT = sb1("wxT", [64, HEADS, D])
            wsl = sb1("wsl", [64, GROUPS])
            bx, bsl, temp = sb1("bx", [64, HEADS]), sb1("bsl", [128, GROUPS]), sb1("temp", [128, HEADS])
            bxw = sb1("bxw", [64, HEADS, 128])
            pw, pb = ps1("pw", [128, K2, 512]), ps1("pb", [128, 512])
            loaded, spread, made = sem1("loaded"), sem1("spread"), sem1("made")
            block = sub.enter_context(stage(nc, g))

            @block.sync
            def _(sp):
                sp.dma_start(wxT[:, :, :], a["L0_ffn_W_x"].rearrange("(h c) d -> c h d", c=64)).then_inc(loaded, 16)
                sp.dma_start(wsl[:, :], a["L0_ffn_W_slice"]).then_inc(loaded, 16)
                with nc.allow_non_contiguous_dma("a few hundred values"):
                    sp.dma_start(bx[:, :], a["L0_ffn_b_x"].rearrange("(h c) -> c h", c=64)).then_inc(loaded, 16)
                sp.dma_start(bsl[:, :], a["L0_ffn_b_slice"].partition_broadcast(128)).then_inc(loaded, 16)
                sp.dma_start(temp[:, :], a["L0_ffn_temperature"].rearrange("a h b c -> (a h b c)").partition_broadcast(128)).then_inc(loaded, 16)
                sp.wait_ge(loaded, 80)

            @block.vector
            def _(dve):
                dve.wait_ge(loaded, 80)
                nc.vector.tensor_copy(bxw[:, :, :], deep(bx[:, :], 64, HEADS, 128)).then_inc(spread, 1)
                nc.vector.tensor_scalar(temp[:, :], temp[:, :], 0.1, 5.0, ALU.max, ALU.min)
                dve.drain()
                nc.vector.reciprocal(temp[:, :], temp[:, :])
                dve.wait_ge(made, 1)
                dve.drain()
                scale = deep(temp[:, :], 128, HEADS, GROUPS)
                for k in range(K2):
                    nc.vector.tensor_tensor(wxs[:, k, :].rearrange("p (h s) -> p h s", h=HEADS),
                                            pw[:, k, :].rearrange("p (h s) -> p h s", h=HEADS), scale, ALU.mult)
                b3 = bxs[:, :].rearrange("p (h s) -> p h s", h=HEADS)
                nc.vector.tensor_tensor(b3, pb[:, :].rearrange("p (h s) -> p h s", h=HEADS),
                                        wide(bsl[:, :], 128, HEADS, GROUPS), ALU.add)
                dve.drain()
                nc.vector.tensor_tensor(b3, b3, scale, ALU.mult)

            @block.tensor
            def _(pe):
                pe.wait_ge(loaded, 80)
                pe.wait_ge(spread, 1)
                for h in range(HEADS):
                    cols = slice(h * GROUPS, (h + 1) * GROUPS)
                    for k in range(K2):
                        nc.tensor.matmul(pw[:, k, cols], wxT[:, h, k * 128:(k + 1) * 128], wsl[:, :],
                                         start=True, stop=True)
                    last = nc.tensor.matmul(pb[:, cols], bxw[:, h, :], wsl[:, :], start=True, stop=True)
                last.then_inc(made, 1)

        def put(dve, i, product, bias):
            return nc.vector.tensor_tensor(row(SW, i), product, bxs[0:P, :], ALU.add)

        linear(nc, g, "f0l", g.XN, D, wxs, None, HEADS * GROUPS, put, norm_of=g.X)

        with ExitStack() as sub:
            sb1, ps1, sem1 = bufs(nc, sub, "f0s")
            top = sb1("top", [128, T * HEADS])
            centred, powers = sem1("centred"), sem1("powers")
            block = sub.enter_context(stage(nc, g))

            def group(c):
                lo, hi = c * G * HEADS, (c + 1) * G * HEADS
                return SW[0:P].rearrange("p t (h s) -> p (t h) s", h=HEADS)[:, lo:hi, :], top[0:P, lo:hi]

            @block.vector
            def _(dve):
                for c in range(T // G):
                    sw, m = group(c)
                    nc.vector.tensor_reduce(m, sw, AX, ALU.max)
                    dve.drain()
                    nc.vector.tensor_tensor(sw, sw, deep(m, P, G * HEADS, GROUPS), ALU.subtract).then_inc(centred, 1)
                for c in range(T // G):
                    sw, m = group(c)
                    dve.wait_ge(powers, c + 1)
                    nc.vector.tensor_reduce(m, sw, AX, ALU.add)
                    dve.drain()
                    nc.vector.reciprocal(m, m)
                    dve.drain()
                    nc.vector.tensor_tensor(sw, sw, deep(m, P, G * HEADS, GROUPS), ALU.mult)

            @block.scalar
            def _(act):
                for c in range(T // G):
                    sw, _ = group(c)
                    act.wait_ge(centred, c + 1)
                    nc.scalar.activation(sw, sw, ACT.Exp).then_inc(powers, 1)

        with ExitStack() as sub:
            sb1, ps1, sem1 = bufs(nc, sub, "f0t")
            S = sb1("S", [128, C4, D + 1])
            with ExitStack() as inner:
                sb2, ps2, sem2 = bufs(nc, inner, "f0u")
                xs, xe = sb2("xs", [128, G, HEADS * GROUPS]), sb2("xe", [128, G, D + 1])
                pS = ps2("pS", [128, C4, 512])
                staged, staged_x, used, opened = (sem2(m) for m in ("staged", "staged_x", "used", "opened"))
                block = inner.enter_context(stage(nc, g))

                @block.scalar
                def _(act):
                    act.sem_inc(used, G)
                    with act.Fori(0, T // G) as i:
                        for j in range(G):
                            act.wait_ge(used, i * G + j + 1)
                            nc.scalar.copy(xs[0:P, j, :], row(SW, i * G + j)).then_inc(staged, 1)

                @block.tensor
                def _(pe):
                    for c in range(C4):
                        nc.tensor.matmul(pS[:, c, 0:D + 1], g.zeros[:, 0:128], g.zeros[:, 0:D + 1], start=True, stop=False)
                    with pe.Fori(0, T // G) as i:
                        for j in range(G):
                            pe.wait_ge(staged, i * G + j + 1)
                            pe.wait_ge(staged_x, i * G + j + 1)
                            for c in range(C4):
                                last = nc.tensor.matmul(pS[:, c, 0:D + 1], xs[0:P, j, c * 128:(c + 1) * 128],
                                                        xe[0:P, j, :], start=False, stop=False, skip_group_check=True)
                            last.then_inc(used, 1)
                    for c in range(C4):
                        last = nc.tensor.matmul(pS[:, c, 0:D + 1], g.zeros[:, 0:128], g.zeros[:, 0:D + 1], start=False, stop=True)
                    last.then_inc(opened, 1)

                @block.vector
                def _(dve):
                    nc.vector.memset(xe[:, :, D:D + 1], 1.0)
                    with dve.Fori(0, T // G) as i:
                        for j in range(G):
                            dve.wait_ge(used, i * G + j + 1)
                            nc.vector.tensor_copy(xe[0:P, j, 0:D], row(g.XN, i * G + j)).then_inc(staged_x, 1)
                    dve.wait_ge(opened, 1)
                    nc.vector.tensor_copy(S[:, :, :], pS[:, :, 0:D + 1])

            slice_attention(nc, g, a, S, M)

        def put2(dve, i, product, bias):
            nc.vector.tensor_tensor(row(g.XN, i), product, bias[0:P, :], ALU.add)
            dve.drain()
            return nc.vector.tensor_tensor(row(g.X, i), row(g.XN, i), row(g.X, i), ALU.add)

        linear(nc, g, "f0o", SW, HEADS * GROUPS, M, a["L0_ffn_b_out"], D, put2)


def slice_attention(nc, g, a, S, M):
    HG = HEADS * GROUPS
    with ExitStack() as ctx:
        sb, ps, sem = bufs(nc, ctx, "sa")
        wfx, bfx = sb("wfx", [128, K2, HG]), sb("bfx", [1, HG])
        wqkv, wout = sb("wqkv", [64, 3, 64]), sb("wout", [64, HEADS, D])
        rn, nrow = sb("rn", [128, C4]), sb("nrow", [1, HG])
        ST_ = sb("ST", [128, K2, HG])
        tok, q, k, v = (sb(m, [64, HG]) for m in ("tok", "q", "k", "v"))
        att, attT = sb("att", [64, HEADS, 64]), sb("attT", [64, HEADS, 64])
        vw, m64, top = sb("vw", [64, HEADS, D]), sb("m64", [64, HEADS, D]), sb("top", [64, HEADS])
        pA, pB = ps("pA", [128, 4, 512]), ps("pB", [128, 4, 512])
        loaded, pe_done, dve_done, act_done, moved = (sem(m) for m in ("loaded", "pe_done", "dve_done", "act_done", "moved"))
        block = ctx.enter_context(stage(nc, g))

        @block.sync
        def _(sp):
            sp.dma_start(wfx[:, :, :], a["L0_ffn_W_fx"].rearrange("(k p) n -> p k n", p=128)).then_inc(loaded, 16)
            sp.dma_start(bfx[:, :], a["L0_ffn_b_fx"].rearrange("(a n) -> a n", a=1)).then_inc(loaded, 16)
            for i, w in enumerate(("W_q", "W_k", "W_v")):
                sp.dma_start(wqkv[:, i, :], a["L0_ffn_" + w]).then_inc(loaded, 16)
            sp.dma_start(wout[:, :, :], a["L0_ffn_W_out"].rearrange("(h c) n -> c h n", c=64)).then_inc(loaded, 16)
            sp.wait_ge(loaded, 96)
            sp.wait_ge(dve_done, 8)
            sp.dma_start(M[0:64, :, :], m64[:, 0:HEADS:2, :]).then_inc(moved, 16)
            sp.dma_start(M[64:128, :, :], m64[:, 1:HEADS:2, :]).then_inc(moved, 16)
            sp.wait_ge(moved, 32)

        @block.vector
        def _(dve):
            nc.vector.tensor_scalar(rn[:, :], S[:, :, D], 1e-5, None, ALU.add)
            dve.drain()
            nc.vector.reciprocal(rn[:, :], rn[:, :])
            dve.drain()
            nc.vector.tensor_tensor(S[:, :, :], S[:, :, :], deep(rn[:, :], 128, C4, D + 1), ALU.mult).then_inc(dve_done, 1)
            dve.wait_ge(pe_done, 1)
            nc.vector.tensor_copy(ST_[:, :, :], pA[:, 0:K2, :])
            nc.vector.tensor_copy(nrow[:, :], pB[0:1, 0, :]).then_inc(dve_done, 1)
            dve.wait_ge(pe_done, 2)
            nc.vector.tensor_copy(tok[:, :], pB[0:64, 1, :]).then_inc(dve_done, 1)
            dve.wait_ge(pe_done, 3)
            nc.vector.tensor_copy(q[:, :], pA[0:64, 0, :])
            nc.vector.tensor_copy(k[:, :], pA[0:64, 1, :])
            nc.vector.tensor_copy(v[:, :], pA[0:64, 2, :]).then_inc(dve_done, 1)
            dve.wait_ge(pe_done, 4)
            scores = pB[0:64, 0, :].rearrange("p (h s) -> p h s", h=HEADS)
            nc.vector.tensor_reduce(top[:, :], scores, AX, ALU.max)
            dve.drain()
            nc.vector.tensor_tensor(att[:, :, :], scores, deep(top[:, :], 64, HEADS, 64), ALU.subtract).then_inc(dve_done, 1)
            dve.wait_ge(act_done, 1)
            nc.vector.tensor_reduce(top[:, :], att[:, :, :], AX, ALU.add)
            dve.drain()
            nc.vector.reciprocal(top[:, :], top[:, :])
            dve.drain()
            nc.vector.tensor_tensor(att[:, :, :], att[:, :, :], deep(top[:, :], 64, HEADS, 64), ALU.mult).then_inc(dve_done, 1)
            dve.wait_ge(pe_done, 5)
            nc.vector.tensor_copy(attT[:, :, :], pB[0:64, 2, :].rearrange("p (h s) -> p h s", h=HEADS))
            nc.vector.tensor_copy(vw[:, :, :], pA[0:64, :, :].rearrange("p b (h n) -> p (b h) n", n=D)).then_inc(dve_done, 1)
            dve.wait_ge(pe_done, 6)
            nc.vector.tensor_copy(m64[:, :, :], pB[0:64, :, :].rearrange("p b (h n) -> p (b h) n", n=D)).then_inc(dve_done, 1)

        @block.scalar
        def _(act):
            act.wait_ge(dve_done, 5)
            nc.scalar.activation(att[:, :, :], att[:, :, :], ACT.Exp, scale=64 ** -0.5).then_inc(act_done, 1)

        @block.tensor
        def _(pe):
            pe.wait_ge(dve_done, 1)
            for c in range(C4):
                for kk in range(K2):
                    nc.tensor.transpose(pA[:, kk, c * 128:(c + 1) * 128], S[:, c, kk * 128:(kk + 1) * 128], g.ident[:, :])
                last = nc.tensor.transpose(pB[0:1, 0, c * 128:(c + 1) * 128], S[:, c, D:D + 1], g.ident[:, :])
            last.then_inc(pe_done, 1)
            pe.wait_ge(dve_done, 2)
            pe.wait_ge(loaded, 96)
            for h in range(HEADS):
                cols = slice(h * 64, (h + 1) * 64)
                nc.tensor.matmul(pB[0:64, 1, cols], wfx[:, 0, cols], ST_[:, 0, cols], start=True, stop=False)
                nc.tensor.matmul(pB[0:64, 1, cols], wfx[:, 1, cols], ST_[:, 1, cols], start=False, stop=False)
                last = nc.tensor.matmul(pB[0:64, 1, cols], bfx[:, cols], nrow[:, cols], start=False, stop=True)
            last.then_inc(pe_done, 1)
            pe.wait_ge(dve_done, 3)
            for i in range(3):
                last = nc.tensor.matmul(pA[0:64, i, :], wqkv[:, i, :], tok[:, :], start=True, stop=True)
            last.then_inc(pe_done, 1)
            pe.wait_ge(dve_done, 4)
            for h in range(HEADS):
                cols = slice(h * 64, (h + 1) * 64)
                last = nc.tensor.matmul(pB[0:64, 0, cols], q[:, cols], k[:, cols], start=True, stop=True)
            last.then_inc(pe_done, 1)
            for h in range(HEADS):
                nc.tensor.matmul(pA[0:64, h // 2, (h % 2) * D:(h % 2 + 1) * D], v[:, h * 64:(h + 1) * 64], wout[:, h, :],
                                 start=True, stop=True)
            pe.wait_ge(dve_done, 6)
            for h in range(HEADS):
                last = nc.tensor.transpose(pB[0:64, 2, h * 64:(h + 1) * 64], att[:, h, :], g.ident[0:64, 0:64])
            last.then_inc(pe_done, 1)
            pe.wait_ge(dve_done, 7)
            for h in range(HEADS):
                last = nc.tensor.matmul(pB[0:64, h // 2, (h % 2) * D:(h % 2 + 1) * D], attT[:, h, :], vw[:, h, :],
                                        start=True, stop=True)
            last.then_inc(pe_done, 1)



def scale_rows(nc, acc, width, factor):
    return lambda dve: nc.vector.tensor_tensor(acc[0:P], acc[0:P], deep(factor[0:P], P, T, width), ALU.mult)


def gcn_finish(nc, g, tag, acc, width, dinv, bias_dram, out, residual=None, table=None):
    with ExitStack() as ctx:
        sb, ps, sem = bufs(nc, ctx, tag)
        loaded, finished, stored = sem("loaded"), sem("finished"), sem("stored")
        bias = sb("bias", [128, width])
        block = ctx.enter_context(stage(nc, g))

        @block.sync
        def _(sp):
            sp.dma_start(bias[:, :], bias_dram.partition_broadcast(128)).then_inc(loaded, 16)
            sp.wait_ge(loaded, 16)
            if table is not None:
                sp.wait_ge(finished, 1)
                sp.dma_start(table.rearrange("(p t) d -> p t d", p=P), out[0:P]).then_inc(stored, 16)
                sp.wait_ge(stored, 16)

        @block.vector
        def _(dve):
            dve.wait_ge(loaded, 16)
            for t in range(T):
                nc.vector.scalar_tensor_tensor(out=acc[0:P, t, :], in0=acc[0:P, t, :], scalar=dinv[0:P, t:t + 1],
                                               in1=bias[0:P, :], op0=ALU.mult, op1=ALU.add)
            dve.drain()
            if table is not None:
                last = nc.vector.scalar_tensor_tensor(out=out[0:P], in0=acc[0:P], scalar=0.0,
                                                      in1=deep(dinv[0:P], P, T, width), op0=ALU.max, op1=ALU.mult)
            else:
                last = nc.vector.scalar_tensor_tensor(out=out[0:P], in0=acc[0:P], scalar=0.0, in1=residual[0:P],
                                                      op0=ALU.max, op1=ALU.add)
            last.then_inc(finished, 1)


def add_biased(nc, dst, tmp):
    def put(dve, i, product, bias):
        nc.vector.tensor_tensor(row(tmp, i, 0, D), product, bias[0:P, :], ALU.add)
        dve.drain()
        return nc.vector.tensor_tensor(row(dst, i), row(tmp, i, 0, D), row(dst, i), ALU.add)
    return put


def scaled(nc, out, factor):
    return lambda dve, t, product, bias: nc.vector.tensor_scalar(
        out[0:P, t, :], product, factor[0:P, t:t + 1], None, ALU.mult)


def layer1_table(nc, g, a):
    Z128 = g.XN[:, :, 0:128]
    linear(nc, g, "g1a", g.XN, D, a["L1_gnn_W1"], None, 128, scaled(nc, Z128, g.dinv1), table=(g.table128, Z128),
           norm_of=g.X)


EXPERT_LOADS = 4


def expert_loads(nc, g, a, c):
    NE, _, F = a["L1_ffn_w1"].shape
    n = NE // EXPERT_LOADS

    def load(w, name, width):
        def start(sp):
            sp.dma_start(w[:, :].rearrange("p (c k n) -> p c k n", c=EXPERT_LOADS, n=width)[:, c],
                         a[name][c * n:(c + 1) * n].rearrange("e (k p) n -> p (e k) n", p=128)).then_inc(g.w_loaded, 16)
        return start

    return [load(g.w1, "L1_ffn_w1", F), load(g.w2, "L1_ffn_w2", D)]


def layer1_gnn(nc, g, a):
    with ExitStack() as ctx:
        sb, ps, sem = bufs(nc, ctx, "g1")
        Z128, Z64 = g.XN[:, :, 0:128], g.XN[:, :, 128:192]

        aggregate(nc, g, "g1ag", Z128, g.table128, 128, loads=expert_loads(nc, g, a, 0))

        linear(nc, g, "g1b", Z128, 128, a["L1_gnn_W2"], None, 64, scaled(nc, Z64, g.dinv1),
               prepare=scale_rows(nc, Z128, 128, g.dinv1), turn=(ACT.Relu, None, a["L1_gnn_b1"]), table=(g.table64, Z64))
        aggregate(nc, g, "g1bg", Z64, g.table64, 64, loads=expert_loads(nc, g, a, 1))

        gcn_finish(nc, g, "g1bf", Z64, 64, g.dinv1, a["L1_gnn_b2"], Z64, table=g.table64)
        aggregate(nc, g, "g1cg", Z64, g.table64, 64, loads=expert_loads(nc, g, a, 2))

        def hidden(dve, i, product, bias):
            nc.vector.tensor_tensor(row(Z128, i), product, bias[0:P, :], ALU.add)
            dve.drain()
            return nc.vector.tensor_scalar(row(Z128, i), row(Z128, i), 0.0, g.dinv1[0:P, bass.ds(i, 1)],
                                           ALU.max, ALU.mult)

        linear(nc, g, "g1d", Z64, 64, a["L1_gnn_W3"], a["L1_gnn_b3"], 128, hidden,
               prepare=scale_rows(nc, Z64, 64, g.dinv1), table=(g.table128, Z128))
        aggregate(nc, g, "g1dg", Z128, g.table128, 128, loads=expert_loads(nc, g, a, 3))
        linear(nc, g, "g1e", Z128, 128, a["L1_gnn_W4"], a["L1_gnn_b4"], D, add_biased(nc, g.X, g.XN),
               prepare=scale_rows(nc, Z128, 128, g.dinv1))


def layer2_gnn(nc, g, a):
    layer_norm(nc, g, "g2n", g.X, g.XN)
    with ExitStack() as ctx:
        sb, ps, sem = bufs(nc, ctx, "g2")
        H = sb("H", [128, T, D])
        for n in ("6", "7"):
            linear(nc, g, f"g2l{n}", H, D, a[f"L2_gnn_W{n}"], None, D, scaled(nc, H, g.dinv2),
                   norm_of=g.XN, turn=(ACT.Identity, a[f"L2_gnn_ln{n}_g"], a[f"L2_gnn_ln{n}_b"]), table=(g.table256, H))
            aggregate(nc, g, f"g2g{n}", H, g.table256, D, weighted=True)
            gcn_finish(nc, g, f"g2f{n}", H, D, g.dinv2, a[f"L2_gnn_b{n}"], g.XN, residual=g.XN)
        linear(nc, g, "g2p", g.XN, D, a["L2_gnn_Wp"], a["L2_gnn_bp"], D, add_biased(nc, g.X, H))


def layer3_gnn(nc, g, a):
    layer_norm(nc, g, "g3n", g.X, g.XN)
    NR = a["L3_gnn_weight"].shape[0]
    NC = NR * D // 512
    with ExitStack() as ctx:
        sb, ps, sem = bufs(nc, ctx, "g3")
        w = sb("w", [128, K2, NR, D])
        bias = sb("bias", [128, D])
        xs, xT, ys = sb("xs", [128, G, D]), sb("xT", [128, G, K2, P]), sb("ys", [128, G, NR * D])
        psT, psO = ps("psT", [128, 3, 512]), ps("psO", [128, NC, 512])
        w_loaded, b_loaded, staged, turned, turn_read = (sem(m) for m in ("w_loaded", "b_loaded", "staged", "turned", "turn_read"))
        multiplied, put_away, turn = sem("multiplied"), sem("put_away"), sem("turn")
        stored = [sem(f"stored{j}") for j in range(G)]
        relations = g.relations.rearrange("(r p t) d -> t p r d", r=NR, p=P)
        block = ctx.enter_context(stage(nc, g))

        @block.sync
        def _(sp):
            for k in range(K2):
                sp.dma_start(w[:, k, :, :], a["L3_gnn_weight"][:, k * 128:(k + 1) * 128, :].rearrange("r p n -> p r n")).then_inc(w_loaded, 16)
            sp.dma_start(bias[:, :], a["L3_gnn_bias"].partition_broadcast(128)).then_inc(b_loaded, 16)
            with sp.Fori(0, T // G) as i:
                for j in range(G):
                    sp.wait_ge(put_away, (i * G + j + 2) * NC)
                    sp.dma_start(relations[bass.ds(i * G + j, 1)].rearrange("a p r d -> p (a r) d"),
                                 ys[0:P, j, :].rearrange("p (r d) -> p r d", d=D)).then_inc(stored[j], 16)
            for j in range(G):
                sp.wait_ge(stored[j], 16 * (T // G + 1))

        @block.tensor
        def _(pe):
            pe.wait_ge(w_loaded, 16 * K2)
            with pe.Fori(0, T // G) as i:
                for j in range(G):
                    pe.wait_ge(staged, i * G + j + 1)
                    pe.wait_ge(turn_read, i * G + j + 1)
                    for k in range(K2):
                        last = nc.tensor.transpose(psT[:, j % 3, k * P:(k + 1) * P], xs[0:P, j, k * 128:(k + 1) * 128],
                                                   g.ident[0:P, 0:P])
                    last.then_inc(turned, 1)
                for j in range(G):
                    pe.wait_ge(turn_read, i * G + j + 3)
                    for c in range(NC):
                        pe.wait_ge(put_away, (i * G + j) * NC + c + 1)
                        for k in range(K2):
                            last = nc.tensor.matmul(psO[0:P, c, :], xT[:, j, k, :],
                                                    w[:, k, 2 * c:2 * c + 2, :].rearrange("p r n -> p (r n)"),
                                                    start=(k == 0), stop=(k == K2 - 1))
                        last.then_inc(multiplied, 1)

        @block.scalar
        def _(act):
            act.sem_inc(turned, G)
            act.sem_inc(turn_read, 2)
            with act.Fori(0, T // G) as i:
                for j in range(G):
                    act.wait_ge(turned, i * G + j + 1)
                    nc.scalar.copy(xs[0:P, j, :], row(g.XN, i * G + j)).then_inc(staged, 1)
                for j in range(G):
                    act.wait_ge(turned, i * G + j + 1 + G)
                    nc.scalar.copy(xT[:, j, :, :], psT[:, j % 3, 0:K2 * P].rearrange("p (k r) -> p k r", k=K2)).then_inc(turn_read, 1)

        @block.vector
        def _(dve):
            dve.sem_inc(put_away, NC)
            for j in range(G):
                dve.sem_inc(stored[j], 16)
            dve.wait_ge(b_loaded, 16)
            nc.vector.tensor_tensor(g.X[0:P], g.X[0:P], wide(bias[0:P, :], P, T, D), ALU.add)
            with dve.Fori(0, T // G) as i:
                for j in range(G):
                    dve.wait_ge(stored[j], (i + 1) * 16)
                    for c in range(NC):
                        dve.wait_ge(multiplied, (i * G + j) * NC + c + 1)
                        nc.vector.tensor_copy(ys[0:P, j, c * 512:(c + 1) * 512], psO[0:P, c, :]).then_inc(put_away, 1)

    aggregate(nc, g, "g3g", g.X, g.relations, D, field=3)


def route(nc, g, tag, logits, n, first, softmax_first=False, hot=None, weight=None):
    with ExitStack() as ctx:
        sb, ps, sem = bufs(nc, ctx, tag)
        low = sb("low", [128, T, n])
        hots = hot if hot is not None else sb("hots", [128, T, 2, n])
        top = sb("top", [128, 2, T])
        centred, powers = sem("centred"), sem("powers")
        block = ctx.enter_context(stage(nc, g))
        iota = wide(g.iota[0:P, 0:n], P, T, n)
        L = logits[0:P]

        @block.vector
        def _(dve):
            if softmax_first:
                nc.vector.tensor_reduce(top[0:P, 0], L, AX, ALU.max)
                dve.drain()
                nc.vector.tensor_tensor(L, L, deep(top[0:P, 0], P, T, n), ALU.subtract).then_inc(centred, 1)
                dve.wait_ge(powers, 1)
                nc.vector.tensor_reduce(top[0:P, 0], L, AX, ALU.add)
                dve.drain()
                nc.vector.reciprocal(top[0:P, 0], top[0:P, 0])
                dve.drain()
                nc.vector.tensor_tensor(L, L, deep(top[0:P, 0], P, T, n), ALU.mult)
                dve.drain()
            for k in range(2):
                nc.vector.tensor_reduce(top[0:P, k], L, AX, ALU.max)
                dve.drain()
                nc.vector.tensor_tensor(low[0:P], L, deep(top[0:P, k], P, T, n), ALU.is_lt)
                dve.drain()
                nc.vector.scalar_tensor_tensor(out=low[0:P], in0=low[0:P], scalar=100.0, in1=iota, op0=ALU.mult, op1=ALU.add)
                dve.drain()
                nc.vector.tensor_reduce(first[0:P, :, k], low[0:P], AX, ALU.min)
                dve.drain()
                nc.vector.tensor_tensor(hots[0:P, :, k, :], iota, first[0:P, :, k:k + 1].broadcast_to([P, T, n]), ALU.is_equal)
                if k == 0:
                    dve.drain()
                    nc.vector.scalar_tensor_tensor(out=L, in0=hots[0:P, :, 0, :], scalar=-BIG, in1=L, op0=ALU.mult, op1=ALU.add)
                    dve.drain()
            nc.vector.tensor_tensor(weight[0:P, :, 1], top[0:P, 1], top[0:P, 0], ALU.subtract).then_inc(centred, 1)
            dve.wait_ge(powers, 2 if softmax_first else 1)
            nc.vector.tensor_scalar(weight[0:P, :, 0], weight[0:P, :, 1], 1.0, None, ALU.add)
            dve.drain()
            nc.vector.reciprocal(weight[0:P, :, 0], weight[0:P, :, 0])
            dve.drain()
            nc.vector.tensor_tensor(weight[0:P, :, 1], weight[0:P, :, 1], weight[0:P, :, 0], ALU.mult)

        @block.scalar
        def _(act):
            if softmax_first:
                act.wait_ge(centred, 1)
                nc.scalar.activation(L, L, ACT.Exp).then_inc(powers, 1)
            act.wait_ge(centred, 2 if softmax_first else 1)
            nc.scalar.activation(weight[0:P, :, 1], weight[0:P, :, 1], ACT.Exp).then_inc(powers, 1)


def gate(nc, g, tag, w, b, n, out):
    def put(dve, i, product, bias):
        return nc.vector.tensor_tensor(row(out, i), product, bias[0:P, :], ALU.add)
    linear(nc, g, tag, g.XN, D, w, b, n, put, norm_of=g.X)


def layer1_ffn(nc, g, a):
    NE, _, F = a["L1_ffn_w1"].shape
    KF = F // 128
    SLOTS = (2 * N + NE * 127) // 128
    AHEAD = 4
    assert SLOTS % AHEAD == 0
    with ExitStack() as ctx:
        sb, ps, sem = bufs(nc, ctx, "f1")
        logits, chosen, weight = sb("logits", [128, T, NE]), sb("chosen", [128, T, 2]), sb("weight", [128, T, 2])
        posf, posi = sb("posf", [128, 2 * T]), sb("posi", [128, 2 * T], I32)
        kmap = sb("kmap", [1, SLOTS + AHEAD], I32)
        gate(nc, g, "f1g", a["L1_ffn_gate_w"], a["L1_ffn_gate_b"], NE, logits)
        route(nc, g, "f1r", logits, NE, chosen, weight=weight)
        with ExitStack() as sub:
            sb1, ps1, sem1 = bufs(nc, sub, "f1s")
            hot, tiles = sb1("hot", [128, NE, 2 * T]), sb1("tiles", [1, SLOTS + AHEAD])
            counting_sort(nc, g, "f1c", chosen[:, :, :].rearrange("p t k -> p (t k)"), P, NE, 2 * T, posf, hot,
                          kmap=kmap, slots=SLOTS + AHEAD, tiles=tiles)
            placed, kept = sem1("placed"), sem1("kept")
            scattered, done = g.moved[0], g.count(0, 32 * T)
            block = sub.enter_context(stage(nc, g))

            @block.sync
            def _(sp):
                sp.dma_start(g.table256.rearrange("(p t) d -> p t d", p=P), g.XN[0:P]).then_inc(kept, 16)
                sp.wait_ge(kept, 16)

            @block.vector
            def _(dve):
                nc.vector.tensor_copy(posi[0:P], posf[0:P]).then_inc(placed, 1)

            @block.gpsimd
            def _(pool):
                pool.wait_ge(g.cleared, 16)
                pool.wait_ge(placed, 1)
                for t in range(T):
                    for k in range(2):
                        pool.indirect_dma_start(out=g.bins[:, :],
                                                out_offset=bass.IndirectOffsetOnAxis(ap=posi[0:P, 2 * t + k:2 * t + k + 1], axis=0),
                                                in_=g.XN[0:P, t, :], in_offset=None).then_inc(scattered, 16)
                pool.wait_ge(scattered, done)

        with ExitStack() as sub:
            sb1, ps1, sem1 = bufs(nc, sub, "f1e")
            w1f, w2f = g.w1[:, :], g.w2[:, :]
            b = sb1("b", [128, AHEAD, F + D])
            room = g.XN[:, :, :].rearrange("p t d -> p (t d)")
            used = 0

            def take(width, places=2):
                nonlocal used
                used += width * places
                return room[:, used - width * places:used].rearrange("p (j d) -> p j d", j=places)

            xs, xT, ys, h, hT = take(D, AHEAD), take(D), take(D), take(F), take(F)
            pT, pH, pU, pY = (ps1(m, [128, 2, 512]) for m in ("pT", "pH", "pU", "pY"))
            x_loaded, b_loaded = ([sem1(f"{m}{j}") for j in range(AHEAD)] for m in ("x_loaded", "b_loaded"))
            stored = [sem1(f"stored{j}") for j in range(2)]
            x_turned, x_read, h_made, h_put, h_turned, h_read, y_made, y_put = (
                sem1(m) for m in ("x_turned", "x_read", "h_made", "h_put", "h_turned", "h_read", "y_made", "y_put"))
            bins = g.bins.rearrange("(s p) d -> s p d", p=128)
            results = g.results.rearrange("(s p) d -> s p d", p=128)
            BODIES = SLOTS // AHEAD
            block = sub.enter_context(stage(nc, g))

            @block.sync
            def _(sp):
                def load_rows(n, j):
                    sp.dma_start(xs[:, j, :], bins[bass.ds(n, 1)].rearrange("a p d -> (a p) d")).then_inc(x_loaded[j], 16)

                def load_bias(e, j):
                    for name, lo, hi in (("L1_ffn_b1", 0, F), ("L1_ffn_b2", F, F + D)):
                        sp.dma_start(b[:, j, lo:hi], a[name][bass.ds(e, 1), :].rearrange("a n -> (a n)")
                                     .partition_broadcast(128)).then_inc(b_loaded[j], 16)

                e = load_keys(nc, mybir.EngineType.SP, kmap, 0, AHEAD, NE)
                for j in range(AHEAD):
                    load_rows(j, j)
                    load_bias(e[j], j)
                with sp.Fori(0, BODIES) as i:
                    e = load_keys(nc, mybir.EngineType.SP, kmap, AHEAD * (i + 1), AHEAD, NE)
                    for j in range(AHEAD):
                        n = AHEAD * i + j
                        sp.wait_ge(x_turned, n + 1)
                        load_rows(n + AHEAD, j)
                        sp.wait_ge(y_put, n + 3)
                        load_bias(e[j], j)
                for j in range(AHEAD):
                    sp.wait_ge(x_loaded[j], 16 * (BODIES + 1))
                    sp.wait_ge(b_loaded[j], 32 * (BODIES + 1))

            @block.tensor
            def _(pe):
                def turn_rows(loads, j):
                    pe.wait_ge(x_loaded[j], loads * 16)
                    for k in range(K2):
                        last = nc.tensor.transpose(pT[:, j % 2, k * 128:(k + 1) * 128], xs[:, j, k * 128:(k + 1) * 128], g.ident[:, :])
                    last.then_inc(x_turned, 1)

                def hidden(n, expert, j):
                    pe.wait_ge(x_read, n + 1)
                    for k in range(K2):
                        last = nc.tensor.matmul(pH[:, j % 2, :], xT[:, j % 2, k * 128:(k + 1) * 128],
                                                w1f[:, bass.ds(expert * (K2 * F) + k * F, F)],
                                                start=(k == 0), stop=(k == K2 - 1))
                    last.then_inc(h_made, 1)

                pe.wait_ge(g.w_loaded, 32 * EXPERT_LOADS)
                for j in range(2):
                    turn_rows(1, j)
                expert = load_keys(nc, mybir.EngineType.PE, kmap, 0, 4, NE)
                hidden(0, expert[0], 0)
                with pe.Fori(0, BODIES) as i:
                    expert = load_keys(nc, mybir.EngineType.PE, kmap, AHEAD * i, AHEAD, NE)
                    expert = list(expert) + list(load_keys(nc, mybir.EngineType.PE, kmap, AHEAD * (i + 1), 1, NE))
                    for j in range(AHEAD):
                        n = AHEAD * i + j
                        hidden(n + 1, expert[j + 1], j + 1)
                        pe.wait_ge(h_put, n + 1)
                        for k in range(KF):
                            last = nc.tensor.transpose(pU[:, j % 2, k * 128:(k + 1) * 128], h[:, j % 2, k * 128:(k + 1) * 128], g.ident[:, :])
                        last.then_inc(h_turned, 1)
                        turn_rows(i + (1 if j + 2 < AHEAD else 2), (j + 2) % AHEAD)
                        pe.wait_ge(h_read, n + 1)
                        pe.wait_ge(y_put, n + 1)
                        for k in range(KF):
                            last = nc.tensor.matmul(pY[:, j % 2, 0:D], hT[:, j % 2, k * 128:(k + 1) * 128],
                                                    w2f[:, bass.ds(expert[j] * (KF * D) + k * D, D)],
                                                    start=(k == 0), stop=(k == KF - 1))
                        last.then_inc(y_made, 1)

            @block.scalar
            def _(act):
                def read_rows(n, j):
                    act.wait_ge(x_turned, n + 1)
                    nc.scalar.copy(xT[:, j % 2, :], pT[:, j % 2, 0:K2 * 128]).then_inc(x_read, 1)

                for j in range(2):
                    act.sem_inc(stored[j], 16)
                    read_rows(j, j)
                with act.Fori(0, BODIES) as i:
                    for j in range(AHEAD):
                        n = AHEAD * i + j
                        act.wait_ge(h_turned, n + 1)
                        nc.scalar.activation(hT[:, j % 2, :], pU[:, j % 2, :], ACT.Relu).then_inc(h_read, 1)
                        read_rows(n + 2, j)
                        act.wait_ge(y_put, n + 3)
                        act.dma_start(results[bass.ds(n, 1)].rearrange("a p d -> (a p) d"), ys[:, j % 2, :]).then_inc(stored[j % 2], 16)
                for j in range(2):
                    act.wait_ge(stored[j], 16 * (SLOTS // 2 + 1))

            @block.vector
            def _(dve):
                dve.sem_inc(y_put, 2)

                def put_hidden(n, loads, j):
                    dve.wait_ge(b_loaded[j], loads * 32)
                    dve.wait_ge(h_made, n + 1)
                    nc.vector.tensor_tensor(h[:, j % 2, :], pH[:, j % 2, :], b[:, j, 0:F], ALU.add).then_inc(h_put, 1)

                put_hidden(0, 1, 0)
                with dve.Fori(0, BODIES) as i:
                    for j in range(AHEAD):
                        n = AHEAD * i + j
                        put_hidden(n + 1, i + (1 if j + 1 < AHEAD else 2), (j + 1) % AHEAD)
                        dve.wait_ge(stored[j % 2], (2 * i + j // 2 + 1) * 16)
                        dve.wait_ge(y_made, n + 1)
                        nc.vector.tensor_tensor(ys[:, j % 2, :], pY[:, j % 2, 0:D], b[:, j, F:F + D], ALU.add).then_inc(y_put, 1)

        with ExitStack() as sub:
            sb1, ps1, sem1 = bufs(nc, sub, "f1y")
            Y = [g.w1[:, k * T * D:(k + 1) * T * D].rearrange("p (t d) -> p t d", t=T) for k in range(2)]
            C = T // G
            gathered, done = g.moved[0:C], [g.count(c, 32 * G) for c in range(C)]
            reloaded, loaded = sem1("reloaded"), sem1("loaded")
            gamma, beta = sb1("gamma", [128, D]), sb1("beta", [128, D])
            with stage(nc, g) as block:
                @block.sync
                def _(sp):
                    sp.dma_start(beta[:, :], a["L1_ffn_beta"].partition_broadcast(128)).then_inc(loaded, 16)
                    sp.dma_start(gamma[:, :], a["L1_ffn_gamma"].partition_broadcast(128)).then_inc(loaded, 16)
                    sp.dma_start(g.XN[0:P], g.table256.rearrange("(p t) d -> p t d", p=P)).then_inc(reloaded, 16)

                @block.gpsimd
                def _(pool):
                    for t in range(T):
                        for k in range(2):
                            pool.indirect_dma_start(out=Y[k][0:P, t, :], out_offset=None, in_=g.results[:, :],
                                                    in_offset=bass.IndirectOffsetOnAxis(ap=posi[0:P, 2 * t + k:2 * t + k + 1], axis=0)
                                                    ).then_inc(gathered[t // G], 16)

                @block.vector
                def _(dve):
                    dve.wait_ge(loaded, 32)
                    nc.vector.tensor_tensor(g.X[0:P], g.X[0:P], wide(beta[0:P, :], P, T, D), ALU.add)
                    dve.wait_ge(reloaded, 16)
                    for c in range(C):
                        dve.wait_ge(gathered[c], done[c])
                        for k in range(2):
                            for t in range(c * G, (c + 1) * G):
                                nc.vector.scalar_tensor_tensor(out=g.XN[0:P, t, :], in0=Y[k][0:P, t, :],
                                                               scalar=weight[0:P, t, k:k + 1], in1=g.XN[0:P, t, :],
                                                               op0=ALU.mult, op1=ALU.add)
                            dve.drain()
            layer_norm(nc, g, "f1m", g.XN, Y[0])
            with stage(nc, g) as block:
                @block.vector
                def _(dve):
                    nc.vector.tensor_tensor(Y[0][0:P], Y[0][0:P], wide(gamma[0:P, :], P, T, D), ALU.mult)
                    dve.drain()
                    nc.vector.tensor_tensor(g.X[0:P], g.X[0:P], Y[0][0:P], ALU.add)


def layer2_ffn(nc, g, a):
    NE, _, H1 = a["L2_ffn_eW1"].shape
    H2 = a["L2_ffn_eW2"].shape[2]
    with ExitStack() as ctx:
        sb, ps, sem = bufs(nc, ctx, "f2")
        logits, chosen, weight = sb("logits", [128, T, NE]), sb("chosen", [128, T, 2]), sb("weight", [128, T, 2])
        hot, coef = sb("hot", [128, T, 2, NE]), sb("coef", [128, T, NE])
        s1, s2, s3 = sb("s1", [128, K2, 256]), sb("s2", [128, 2, 128]), sb("s3", [128, D])
        e1, e2, e3 = sb("e1", [128, K2, NE, H1]), sb("e2", [128, NE, H2]), sb("e3", [H2 + 1, NE, D])
        sb1_, sb2_, sb3_ = sb("sb1", [128, 2]), sb("sb2", [128, 1]), sb("sb3", [128, D])
        eb1, eb2 = sb("eb1", [128, NE]), sb("eb2", [H2, NE])
        loaded = sem("loaded")
        with stage(nc, g) as block:
            @block.sync
            def _(sp):
                for out, src in ((s1[:, :, :], a["L2_ffn_sW1"].rearrange("(k p) n -> p k n", p=128)),
                                 (s2[:, :, :], a["L2_ffn_sW2"].rearrange("(k p) n -> p k n", p=128)),
                                 (s3[:, :], a["L2_ffn_sW3"]),
                                 (e1[:, 0], a["L2_ffn_eW1"][:, 0:128, :].rearrange("e p n -> p e n")),
                                 (e1[:, 1], a["L2_ffn_eW1"][:, 128:256, :].rearrange("e p n -> p e n")),
                                 (e2[:, :, :], a["L2_ffn_eW2"].rearrange("e p n -> p e n")),
                                 (e3[0:H2], a["L2_ffn_eW3"].rearrange("e p n -> p e n")),
                                 (e3[H2:H2 + 1, :, :], a["L2_ffn_eb3"].rearrange("(a e) n -> a e n", a=1)),
                                 (sb3_[:, :], a["L2_ffn_sb3"].partition_broadcast(128))):
                    sp.dma_start(out, src).then_inc(loaded, 16)
                with nc.allow_non_contiguous_dma("a few hundred values"):
                    sp.dma_start(sb1_[:, :], a["L2_ffn_sb1"].rearrange("(k p) -> p k", p=128)).then_inc(loaded, 16)
                    sp.dma_start(sb2_[:, :], a["L2_ffn_sb2"].rearrange("(p k) -> p k", k=1)).then_inc(loaded, 16)
                    sp.dma_start(eb1[:, :], a["L2_ffn_eb1"].rearrange("e p -> p e")).then_inc(loaded, 16)
                    sp.dma_start(eb2[:, :], a["L2_ffn_eb2"].rearrange("e p -> p e")).then_inc(loaded, 16)

        gate(nc, g, "f2g", a["L2_ffn_gW"], a["L2_ffn_gb"], NE, logits)
        route(nc, g, "f2r", logits, NE, chosen, softmax_first=True, hot=hot, weight=weight)
        with stage(nc, g) as block:
            @block.vector
            def _(dve):
                nc.vector.tensor_tensor(hot[0:P], hot[0:P], weight[0:P].rearrange("p t (k a) -> p t k a", a=1)
                                        .broadcast_to([P, T, 2, NE]), ALU.mult)
                dve.drain()
                nc.vector.tensor_tensor(coef[0:P], hot[0:P, :, 0, :], hot[0:P, :, 1, :], ALU.add)

        GROUPS_ = ((0, 3), (3, 2))
        WIDE = 3 * P
        xs, xT = sb("xs", [128, G, D]), sb("xT", [128, K2, G * P])
        hs, he = sb("hs", [128, 2, WIDE]), sb("he", [128, NE, WIDE])
        h2s, h2e = sb("h2s", [128, WIDE]), sb("h2e", [H2 + 1, NE, WIDE])
        acc = sb("acc", [128, D])
        pT, pR, pO = ps("pT", [128, 2, 512]), ps("pR", [128, 3, 512]), ps("pO", [128, 3, 512])
        set1, staged, turned, turn_read = (sem(m) for m in ("set1", "staged", "turned", "turn_read"))
        made, put_away, outs, outs_read = (sem(m) for m in ("made", "put_away", "outs", "outs_read"))
        NH = 2 + NE + 1 + NE
        block = ctx.enter_context(stage(nc, g))

        @block.tensor
        def _(pe):
            pe.wait_ge(loaded, 208)
            pe.wait_ge(set1, 1)
            with pe.Fori(0, T // G) as i:
                for j in range(G):
                    pe.wait_ge(staged, i * G + j + 1)
                    pe.wait_ge(turn_read, i * G + j + (1 if j else 2))
                    for k in range(K2):
                        last = nc.tensor.transpose(pT[:, j % 2, k * P:(k + 1) * P], xs[0:P, j, k * 128:(k + 1) * 128], g.ident[0:P, 0:P])
                    last.then_inc(turned, 1)
                pe.wait_ge(turn_read, (i + 1) * G + 2)
                for m, (t0, nt) in enumerate(GROUPS_):
                    cols, w = slice(t0 * P, (t0 + nt) * P), nt * P
                    pieces = [[(s1[:, k, c * 128:(c + 1) * 128], xT[:, k, cols]) for k in range(K2)] for c in range(2)]
                    pieces += [[(e1[:, k, e, :], xT[:, k, cols]) for k in range(K2)] for e in range(NE)]
                    pieces += [[(s2[:, k, :], hs[:, k, 0:w]) for k in range(2)]]
                    pieces += [[(e2[:, e, :], he[:, e, 0:w])] for e in range(NE)]
                    for q, pairs in enumerate(pieces):
                        at = m * NH + q
                        rows = H2 if q > 2 + NE else 128
                        pe.wait_ge(put_away, i * (2 * NH) + at + (1 if at else 2))
                        for k, (lhs, rhs) in enumerate(pairs):
                            last = nc.tensor.matmul(pR[0:rows, at % 3, 0:w], lhs, rhs, start=(k == 0), stop=(k == len(pairs) - 1))
                        last.then_inc(made, 1)
                    pe.wait_ge(put_away, i * (2 * NH) + (m + 1) * NH + 2)
                    for t in range(nt):
                        n = i * G + t0 + t
                        rows = slice(t * P, (t + 1) * P)
                        parts = [(h2s[:, rows], s3[:, :])] + [(h2e[:, e, rows], e3[:, e, :]) for e in range(NE)]
                        for q, (lhs, rhs) in enumerate(parts):
                            if q % 2 == 0:
                                pe.wait_ge(outs_read, n * 3 + q // 2 + 1)
                            last = nc.tensor.matmul(pO[0:P, q // 2, (q % 2) * D:(q % 2 + 1) * D], lhs, rhs, start=True, stop=True)
                            if q % 2 or q == NE:
                                last.then_inc(outs, 1)

        @block.scalar
        def _(act):
            act.wait_ge(loaded, 208)
            act.sem_inc(turned, G)
            act.sem_inc(turn_read, 2)
            act.sem_inc(put_away, 2)
            with act.Fori(0, T // G) as i:
                for j in range(G):
                    act.wait_ge(turned, i * G + j + 1)
                    nc.scalar.copy(xs[0:P, j, :], row(g.XN, i * G + j)).then_inc(staged, 1)
                for j in range(G):
                    act.wait_ge(turned, i * G + j + 1 + G)
                    nc.scalar.copy(xT[:, :, j * P:(j + 1) * P], pT[:, j % 2, 0:K2 * P].rearrange("p (k r) -> p k r", k=K2)).then_inc(turn_read, 1)
                for m, (t0, nt) in enumerate(GROUPS_):
                    w = nt * P
                    places = [(hs[:, c, 0:w], sb1_[:, c:c + 1]) for c in range(2)]
                    places += [(he[:, e, 0:w], eb1[:, e:e + 1]) for e in range(NE)]
                    places += [(h2s[:, 0:w], sb2_[:, :])]
                    places += [(h2e[0:H2, e, 0:w], eb2[:, e:e + 1]) for e in range(NE)]
                    for q, (place, bias) in enumerate(places):
                        at = m * NH + q
                        rows = H2 if q > 2 + NE else 128
                        act.wait_ge(made, i * (2 * NH) + at + 1)
                        nc.scalar.activation(place, pR[0:rows, at % 3, 0:w], ACT.Relu, bias=bias).then_inc(put_away, 1)

        @block.vector
        def _(dve):
            nc.vector.memset(h2e[H2:H2 + 1, :, :], 1.0).then_inc(set1, 1)
            dve.sem_inc(outs_read, 3)
            dve.wait_ge(loaded, 208)
            nc.vector.tensor_tensor(g.X[0:P], g.X[0:P], wide(sb3_[0:P, :], P, T, D), ALU.add)
            with dve.Fori(0, T // G) as i:
                for j in range(G):
                    n = i * G + j
                    for q in range(NE + 1):
                        dve.drain()
                        if q % 2 == 0:
                            dve.wait_ge(outs, n * 3 + q // 2 + 1)
                        part = pO[0:P, q // 2, (q % 2) * D:(q % 2 + 1) * D]
                        if q == 0:
                            last = nc.vector.tensor_tensor(acc[0:P, :], part, row(g.X, n), ALU.add)
                        else:
                            last = nc.vector.scalar_tensor_tensor(
                                out=acc[0:P, :] if q < NE else row(g.X, n), in0=part, scalar=row(coef, n, q - 1, q),
                                in1=acc[0:P, :], op0=ALU.mult, op1=ALU.add)
                        if q % 2 or q == NE:
                            last.then_inc(outs_read, 1)


def layer3_ffn(nc, g, a):
    NE, _, F = a["L3_ffn_w1"].shape
    KF = F // 128
    C = -(-(5 * N) // (4 * NE))
    CS = 4
    with ExitStack() as ctx:
        sb, ps, sem = bufs(nc, ctx, "f3")
        logits = sb("logits", [128, T, NE])
        low = sb("low", [128, T, NE])
        best, total, pos, kept, slot, away = (sb(m, [128, T]) for m in ("best", "total", "pos", "kept", "slot", "away"))
        to, back = sb("to", [128, T], I32), sb("back", [128, T], I32)
        w1, w2 = sb("w1", [128, 2, K2, F]), sb("w2", [128, 2, KF, D])
        b1, b2 = sb("b1", [128, NE, KF]), sb("b2", [128, 2, D])
        b_loaded, loaded = sem("b_loaded"), [sem(f"loaded{j}") for j in range(2)]

        def load_expert(sp, ex, j):
            sp.dma_start(w1[:, j, :, :], a["L3_ffn_w1"][ex].rearrange("a (k p) n -> p (a k) n", p=128)).then_inc(loaded[j], 16)
            sp.dma_start(w2[:, j, :, :], a["L3_ffn_w2"][ex].rearrange("a (k p) n -> p (a k) n", p=128)).then_inc(loaded[j], 16)
            sp.dma_start(b2[:, j, :], a["L3_ffn_b2"][ex, :].rearrange("a n -> (a n)").partition_broadcast(128)).then_inc(loaded[j], 16)

        with stage(nc, g) as block:
            @block.sync
            def _(sp):
                with nc.allow_non_contiguous_dma("the biases, once"):
                    for e in range(NE):
                        sp.dma_start(b1[:, e, :], a["L3_ffn_b1"][e].rearrange("(k p) -> p k", p=128)).then_inc(b_loaded, 16)
                for j in range(2):
                    load_expert(sp, bass.ds(j, 1), j)

        gate(nc, g, "f3g", a["L3_ffn_gate_w"], a["L3_ffn_gate_b"], NE, logits)
        centred, powers = sem("centred"), sem("powers")
        with stage(nc, g) as block:
            L = logits[0:P]

            @block.vector
            def _(dve):
                nc.vector.tensor_reduce(total[0:P], L, AX, ALU.max)
                dve.drain()
                nc.vector.tensor_tensor(L, L, deep(total[0:P], P, T, NE), ALU.subtract).then_inc(centred, 1)
                dve.wait_ge(powers, 1)
                nc.vector.tensor_reduce(total[0:P], L, AX, ALU.add)
                nc.vector.tensor_reduce(best[0:P], L, AX, ALU.max)
                dve.drain()
                nc.vector.reciprocal(total[0:P], total[0:P])
                nc.vector.tensor_tensor(low[0:P], L, deep(best[0:P], P, T, NE), ALU.is_lt)
                dve.drain()
                nc.vector.scalar_tensor_tensor(out=low[0:P], in0=low[0:P], scalar=100.0,
                                               in1=wide(g.iota[0:P, 0:NE], P, T, NE), op0=ALU.mult, op1=ALU.add)
                dve.drain()
                nc.vector.tensor_reduce(best[0:P], low[0:P], AX, ALU.min)

            @block.scalar
            def _(act):
                act.wait_ge(centred, 1)
                nc.scalar.activation(L, L, ACT.Exp).then_inc(powers, 1)

        with ExitStack() as sub:
            sb1, ps1, sem1 = bufs(nc, sub, "f3s")
            hot = sb1("hot", [128, NE, T])
            counting_sort(nc, g, "f3c", best, P, NE, T, pos, hot, base=0)
            placed = sem1("placed")
            scattered, done = g.moved[0], g.count(0, 16 * T)
            block = sub.enter_context(stage(nc, g))

            @block.vector
            def _(dve):
                nc.vector.tensor_scalar(kept[0:P], pos[0:P], float(C), None, ALU.is_lt)
                nc.vector.tensor_scalar(pos[0:P], pos[0:P], float(C - 1), None, ALU.min)
                nc.vector.tensor_scalar(away[0:P], g.iota[0:P, 0:T], float(NE * CS * 128), None, ALU.add)
                nc.vector.tensor_scalar(low[0:P, 0, 0:1], g.iota_p[0:P, :], float(T), None, ALU.mult)
                dve.drain()
                nc.vector.scalar_tensor_tensor(out=slot[0:P], in0=best[0:P], scalar=float(CS * 128), in1=pos[0:P],
                                               op0=ALU.mult, op1=ALU.add)
                nc.vector.tensor_scalar(away[0:P], away[0:P], low[0:P, 0, 0:1], None, ALU.add)
                nc.vector.tensor_tensor(total[0:P], total[0:P], kept[0:P], ALU.mult)
                dve.drain()
                nc.vector.tensor_copy(back[0:P], slot[0:P])
                nc.vector.tensor_tensor(pos[0:P], slot[0:P], away[0:P], ALU.subtract)
                dve.drain()
                nc.vector.tensor_tensor(pos[0:P], pos[0:P], kept[0:P], ALU.mult)
                dve.drain()
                nc.vector.tensor_tensor(to[0:P], pos[0:P], away[0:P], ALU.add).then_inc(placed, 1)

            @block.gpsimd
            def _(pool):
                pool.wait_ge(placed, 1)
                for t in range(T):
                    pool.indirect_dma_start(out=g.bins[:, :],
                                            out_offset=bass.IndirectOffsetOnAxis(ap=to[0:P, t:t + 1], axis=0),
                                            in_=g.XN[0:P, t, :], in_offset=None).then_inc(scattered, 16)
                pool.wait_ge(scattered, done)

        with ExitStack() as sub:
            sb1, ps1, sem1 = bufs(nc, sub, "f3e")
            xs, xT = sb1("xs", [128, 2, CS, D]), sb1("xT", [128, K2, CS * 128])
            hT, ys = sb1("hT", [128, KF, CS * 128]), sb1("ys", [128, 2, CS, D])
            pT, pH, pY = (ps1(m, [128, 2, 512]) for m in ("pT", "pH", "pY"))
            stored = [sem1(f"stored{j}") for j in range(2)]
            x_turned, x_read, h_made, h_read, y_made, y_put, used = (
                sem1(m) for m in ("x_turned", "x_read", "h_made", "h_read", "y_made", "y_put", "used"))
            bins = g.bins[0:NE * CS * 128, :].rearrange("(e s p) d -> e p s d", p=128, s=CS)
            results = g.results[0:NE * CS * 128, :].rearrange("(e s p) d -> e p s d", p=128, s=CS)
            block = sub.enter_context(stage(nc, g))

            @block.sync
            def _(sp):
                def load_rows(ex, j):
                    sp.dma_start(xs[:, j, :, :], bins[ex].rearrange("a p s d -> p (a s) d")).then_inc(loaded[j], 16)

                for j in range(2):
                    load_rows(bass.ds(j, 1), j)
                with sp.Fori(0, NE // 2 - 1) as i:
                    for j in range(2):
                        sp.wait_ge(used, 2 * i + j + 1)
                        load_rows(bass.ds(2 * i + j + 2, 1), j)
                        load_expert(sp, bass.ds(2 * i + j + 2, 1), j)

            @block.tensor
            def _(pe):
                with pe.Fori(0, NE // 2) as i:
                    for j in range(2):
                        n = 2 * i + j
                        pe.wait_ge(loaded[j], (i + 1) * 64)
                        for k in range(K2):
                            for s in range(CS):
                                last = nc.tensor.transpose(pT[:, k, s * 128:(s + 1) * 128], xs[:, j, s, k * 128:(k + 1) * 128], g.ident[:, :])
                            last.then_inc(x_turned, 1)
                        pe.wait_ge(x_read, 2 * n + 2)
                        for f in range(KF):
                            pe.wait_ge(h_read, n * KF + f + 1)
                            for k in range(K2):
                                last = nc.tensor.matmul(pH[:, f % 2, :], w1[:, j, k, f * 128:(f + 1) * 128], xT[:, k, :],
                                                        start=(k == 0), stop=(k == K2 - 1))
                            last.then_inc(h_made, 1)
                        pe.wait_ge(h_read, (n + 1) * KF + 2)
                        for s in range(CS):
                            pe.wait_ge(y_put, n * CS + s + 1)
                            for f in range(KF):
                                last = nc.tensor.matmul(pY[:, s % 2, 0:D], hT[:, f, s * 128:(s + 1) * 128], w2[:, j, f, :],
                                                        start=(f == 0), stop=(f == KF - 1))
                            last.then_inc(y_made, 1)

            @block.scalar
            def _(act):
                act.wait_ge(b_loaded, 16 * NE)
                act.sem_inc(h_read, 2)
                with act.Fori(0, NE // 2) as i:
                    for j in range(2):
                        n = 2 * i + j
                        for k in range(K2):
                            act.wait_ge(x_turned, 2 * n + k + 1)
                            nc.scalar.copy(xT[:, k, :], pT[:, k, :]).then_inc(x_read, 1)
                        for f in range(KF):
                            act.wait_ge(h_made, n * KF + f + 1)
                            nc.scalar.activation(hT[:, f, :], pH[:, f % 2, :], ACT.Relu,
                                                 bias=row(b1, n, f, f + 1, p=128)).then_inc(h_read, 1)
                        act.wait_ge(y_put, (n + 1) * CS + 2)
                        act.dma_start(results[bass.ds(n, 1)].rearrange("a p s d -> p (a s) d"), ys[:, j, :, :]).then_inc(stored[j], 16)
                for j in range(2):
                    act.wait_ge(stored[j], 16 * (NE // 2 + 1))

            @block.vector
            def _(dve):
                dve.sem_inc(y_put, 2)
                for j in range(2):
                    dve.sem_inc(stored[j], 16)
                with dve.Fori(0, NE // 2) as i:
                    for j in range(2):
                        n = 2 * i + j
                        dve.wait_ge(stored[j], (i + 1) * 16)
                        for s in range(CS):
                            dve.wait_ge(y_made, n * CS + s + 1)
                            nc.vector.tensor_tensor(ys[:, j, s, :], pY[:, s % 2, 0:D], b2[:, j, :], ALU.add).then_inc(y_put, 1)
                        dve.drain().then_inc(used, 1)

        with ExitStack() as sub:
            sb1, ps1, sem1 = bufs(nc, sub, "f3y")
            Y, flag, const = sb1("Y", [128, T, D]), sb1("flag", [128, T, D], I32), sb1("const", [128, 3])
            GROUPED = T // G
            gathered, done = g.moved[0:GROUPED], [g.count(c, 16 * G) for c in range(GROUPED)]
            finished, stored = sem1("finished"), sem1("stored")
            result = g.out.rearrange("(p t) d -> p t d", p=P)
            block = sub.enter_context(stage(nc, g))

            @block.sync
            def _(sp):
                for c in range(GROUPED):
                    sp.wait_ge(finished, c + 1)
                    sp.dma_start(result[:, c * G:(c + 1) * G, :], g.X[0:P, c * G:(c + 1) * G, :]).then_inc(stored, 16)
                sp.wait_ge(stored, 16 * GROUPED)

            @block.gpsimd
            def _(pool):
                for t in range(T):
                    pool.indirect_dma_start(out=Y[0:P, t, :], out_offset=None, in_=g.results[:, :],
                                            in_offset=bass.IndirectOffsetOnAxis(ap=back[0:P, t:t + 1], axis=0)
                                            ).then_inc(gathered[t // G], 16)

            @block.vector
            def _(dve):
                for k, value in enumerate((0.0, 1e4, -1e4)):
                    nc.vector.memset(const[:, k:k + 1], value)
                largest = 3.4028234663852886e38
                for c in range(GROUPED):
                    dve.wait_ge(gathered[c], done[c])
                    tiles = slice(c * G, (c + 1) * G)
                    y, f, x = Y[0:P, tiles], flag[0:P, tiles], g.X[0:P, tiles]
                    nc.vector.tensor_tensor(y, y, deep(total[0:P, tiles], P, G, D), ALU.mult)
                    dve.drain()
                    nc.vector.tensor_tensor(f, y, y, ALU.not_equal)
                    dve.drain()
                    for k in range(3):
                        if k:
                            nc.vector.tensor_scalar(f, y, largest if k == 1 else -largest, None,
                                                    ALU.is_gt if k == 1 else ALU.is_lt)
                            dve.drain()
                        nc.vector.copy_predicated(y, f, const[0:P, k:k + 1].rearrange("p (a b) -> p a b", a=1).broadcast_to([P, G, D]))
                        dve.drain()
                    nc.vector.tensor_tensor(x, x, y, ALU.add).then_inc(finished, 1)


def build(nc, a, out):
    with ExitStack() as ctx:
        def sb(name, shape, dt=F32):
            return ctx.enter_context(nc.sbuf_tensor(name, shape, dt))

        def dram(name, shape, dt=F32):
            return nc.dram_tensor(name, shape, dt, kind="Internal").ap()

        g = Shared()
        g.X = sb("X", [128, T, D])
        g.XN = sb("XN", [128, T, D])
        g.ident = sb("ident", [128, 128])
        g.tri = sb("tri", [128, 128])
        g.iota = sb("iota", [128, ST])
        g.iota_p = sb("iota_p", [128, 1])
        g.ones = sb("ones", [128, ST])
        g.zeros = sb("zeros", [128, 264])
        g.slots = sb("slots", [128, ST + R // 2, 4])
        g.kmap = sb("kmap", [1, ST], I32)
        g.dinv1 = sb("dinv1", [128, T])
        g.dinv2 = sb("dinv2", [128, T])
        g.slots_dram = dram("slots_dram", (128 * (ST + ET - EC), 4))
        g.table260 = dram("table260", (N, D + 4))
        g.table4 = dram("table4", (N, 4))
        g.table64 = dram("table64", (N, 64))
        g.table128 = dram("table128", (N, 128))
        g.table256 = dram("table256", (N, D))
        g.relations = dram("relations", (8 * N, D))
        g.bins = dram("bins", (68 * 128, D))
        g.results = dram("results", (64 * 128, D))
        g.moved = [ctx.enter_context(nc.semaphore(f"moved{j}")) for j in range(R)]
        sent = [0] * R

        def count(j, n):
            sent[j] += n
            return sent[j]

        g.count = count
        g.block, g.phase = None, 0
        g.cleared, g.w_loaded, g.tables_stored, g.slots_back = (
            ctx.enter_context(nc.semaphore(m)) for m in ("cleared", "w_loaded", "tables_stored", "slots_back"))
        g.phase_done = ctx.enter_context(nc.semaphore("phase_done"))
        constants(nc, g, a["x"])
        with ExitStack() as early:
            g.rec = early.enter_context(nc.sbuf_tensor("rec", [128, ET, 4], F32))
            g.rec_row = early.enter_context(nc.sbuf_tensor("rec_row", [128, ET], I32))
            prepare_graph(nc, g, a["src"], a["dst"], a["edge_type_8"], a["edge_weight"])
            clear_semaphores(nc)
            with nc.Block() as block:
                g.block = block
                scatter_edges(nc, g, 0, ET // 4)
                layer0_gnn(nc, g, a)
                scatter_edges(nc, g, ET // 4, ET)
                layer0_ffn(nc, g, a)
                load_slots(nc, g)
                layer1_table(nc, g, a)

                @block.sync
                def _(sp):
                    sp.wait_ge(g.slots_back, 16)
            g.block = None
        clear_semaphores(nc)
        with ExitStack() as early:
            NE, _, F = a["L1_ffn_w1"].shape
            g.w1 = early.enter_context(nc.sbuf_tensor("w1", [128, NE * K2 * F], F32))
            g.w2 = early.enter_context(nc.sbuf_tensor("w2", [128, NE * F // 128 * D], F32))
            layer1_gnn(nc, g, a)
            clear_semaphores(nc)
            layer1_ffn(nc, g, a)
            clear_semaphores(nc)
        g.out = out
        for layer in (layer2_gnn, layer2_ffn, layer3_gnn, layer3_ffn):
            layer(nc, g, a)
            clear_semaphores(nc)


TURNED = ("L0_ffn_W_x", "L2_gnn_W6", "L2_gnn_W7", "L2_gnn_Wp", "L3_gnn_weight")


def kernel(**inputs):
    import numpy as np
    import concourse.bacc as bacc
    from concourse.bass_utils import run_bass_kernel_spmd as run

    nc = bacc.Bacc("TRN2", target_bir_lowering=False, num_devices=1)
    arrays, args = {}, {}
    for name, value in inputs.items():
        v = np.ascontiguousarray(value)
        if name in TURNED:
            v = np.ascontiguousarray(np.swapaxes(v, -1, -2))
        arrays[f"in_{name}"] = v
        args[name] = nc.dram_tensor(f"in_{name}", v.shape, mybir.dt.from_np(v.dtype), kind="ExternalInput").ap()
    out = nc.dram_tensor("out_x", (N, D), F32, kind="ExternalOutput").ap()
    build(nc, args, out)
    return run(nc, [arrays], core_ids=[0]).results[0]["out_x"]
```
